# Optimizing a Trainium2 kernel written in Bass

```python
import numpy as np
import jax
import jax.numpy as jnp

def _softmax(x, axis=-1):
    return jax.nn.softmax(x, axis=axis)

def _gelu(x):
    return jax.nn.gelu(x, approximate=True)

def _silu(x):
    return jax.nn.silu(x)

def _sigmoid(x):
    return jax.nn.sigmoid(x)

def _layernorm(x, axis=-1, eps=1e-05):
    m = jnp.mean(x, axis=axis, keepdims=True)
    v = jnp.var(x, axis=axis, keepdims=True)
    return (x - m) / jnp.sqrt(v + eps)

def _scatter_add(tgt, idx, src, axis=0):
    return tgt.at[idx].add(src)

def _segment_sum(src, seg, n):
    return jax.ops.segment_sum(src, seg, n)
kernel_name = 'mk_seq_preln_d4_jaxref_r8_d323d7'

def setup_inputs(seed: int=0):
    np.random.seed(seed)
    _w = jnp.asarray

    def _L0_attn_setup():
        import jax, jax.numpy as jnp
        import numpy as np
        D_MODEL = 128
        N_HEADS = 16
        FEAT_DIM = 16
        V_DIM = 64
        EPS = 1e-12

        def taylor_exp(x):
            d = x.shape[-1]
            rd = jnp.sqrt(jnp.float32(d))
            rrd = jnp.sqrt(rd)
            r2 = jnp.sqrt(jnp.float32(2.0))
            x2 = (x[..., :, None] * x[..., None, :]).reshape(*x.shape[:-1], d * d) / r2
            ones = jnp.ones(x.shape[:-1] + (1,), dtype=x.dtype)
            return jnp.concatenate([ones, x / rrd, x2 / rd], axis=-1)
        key = jax.random.key(seed)
        k0, k1, k2, k3, k4 = jax.random.split(key, 5)
        b, l = (2, 256)
        scale = 1.0 / np.sqrt(D_MODEL)
        return {'hidden_states': jax.random.normal(k0, (b, l, D_MODEL), dtype=jnp.float32), 'Wq': jax.random.normal(k1, (D_MODEL, N_HEADS * FEAT_DIM), dtype=jnp.float32) * scale, 'Wk': jax.random.normal(k2, (D_MODEL, N_HEADS * FEAT_DIM), dtype=jnp.float32) * scale, 'Wv': jax.random.normal(k3, (D_MODEL, N_HEADS * V_DIM), dtype=jnp.float32) * scale, 'Wo': jax.random.normal(k4, (N_HEADS * V_DIM, D_MODEL), dtype=jnp.float32) * scale}
    _L0_attn_in = _L0_attn_setup()

    def _L0_ffn_setup():
        import jax, jax.numpy as jnp
        import numpy as np
        B, S, D, F, E, K = (2, 256, 128, 256, 8, 2)
        key = jax.random.key(seed)
        ks = jax.random.split(key, 5)
        scale = 0.02
        return {'x': jax.random.normal(ks[0], (B, S, D), dtype=jnp.float32), 'Wg': jax.random.normal(ks[1], (E, D), dtype=jnp.float32) * scale, 'W1': jax.random.normal(ks[2], (E, F, D), dtype=jnp.float32) * scale, 'W2': jax.random.normal(ks[3], (E, F, D), dtype=jnp.float32) * scale, 'W3': jax.random.normal(ks[4], (E, D, F), dtype=jnp.float32) * scale}
    _L0_ffn_in = _L0_ffn_setup()

    def _L1_attn_setup():
        import jax, jax.numpy as jnp
        import numpy as np
        B, S, D_IN = (2, 256, 128)
        H, D_HEAD = (16, 64)
        key = jax.random.key(seed)
        k1, k2, k3 = jax.random.split(key, 3)
        x = jax.random.normal(k1, (B, S, D_IN), dtype=jnp.float32)
        kernel = jax.random.normal(k2, (3, H, D_IN, D_HEAD), dtype=jnp.float32) * np.float32(np.sqrt(2.0 / D_IN))
        WO = jax.random.normal(k3, (1, H * D_HEAD, D_IN), dtype=jnp.float32) * np.float32(np.sqrt(2.0 / (H * D_HEAD)))
        return {'x': x, 'kernel': kernel, 'WO': WO}
    _L1_attn_in = _L1_attn_setup()

    def _L1_ffn_setup():
        import jax, jax.numpy as jnp
        import numpy as np
        DIM = 128
        DEPTH = 2
        HEADS = 8
        DIM_HEAD = 64
        WINDOW = 64
        INNER = HEADS * DIM_HEAD
        HID = int(DIM * 4 * 2 / 3)
        B, N = (2, 1024)
        QK_SCALE = 8.0

        def shift_token(t):
            t1, t2 = jnp.split(t, 2, axis=-1)
            t2 = jnp.pad(t2, ((0, 0), (1, 0), (0, 0)))[:, :-1]
            return jnp.concatenate([t1, t2], axis=-1)

        def l2norm(t):
            return t / jnp.clip(jnp.linalg.norm(t, axis=-1, keepdims=True), 1e-12)

        def rotate_half(x):
            x1, x2 = jnp.split(x, 2, axis=-1)
            return jnp.concatenate([-x2, x1], axis=-1)

        def rotary_xpos(q, k):
            n = q.shape[-2]
            half_idx = jnp.arange(0, DIM_HEAD, 2, dtype=jnp.float32)
            inv_freq = 1.0 / 10000.0 ** (half_idx / DIM_HEAD)
            t = jnp.arange(n, dtype=jnp.float32)
            freqs = t[:, None] * inv_freq[None, :]
            freqs = jnp.concatenate([freqs, freqs], axis=-1)
            base = (half_idx + 0.4 * DIM_HEAD) / (1.4 * DIM_HEAD)
            power = (t - n // 2) / float(WINDOW // 2)
            scale = base[None, :] ** power[:, None]
            scale = jnp.concatenate([scale, scale], axis=-1)
            cos, sin = (jnp.cos(freqs), jnp.sin(freqs))
            q = q * cos * scale + rotate_half(q) * sin * scale
            k = k * cos / scale + rotate_half(k) * sin / scale
            return (q, k)

        def local_attention(q, k, v):
            b, h, n, d = q.shape
            w = n // WINDOW
            bq = q.reshape(b, h, w, WINDOW, d) * QK_SCALE
            bk = k.reshape(b, h, w, WINDOW, d)
            bv = v.reshape(b, h, w, WINDOW, d)

            def look_around(t):
                p = jnp.pad(t, ((0, 0), (0, 0), (1, 0), (0, 0), (0, 0)))
                return jnp.concatenate([p[:, :, :w], p[:, :, 1:]], axis=3)
            bk, bv = (look_around(bk), look_around(bv))
            bt = jnp.arange(n).reshape(w, WINDOW)
            btp = jnp.pad(bt, ((1, 0), (0, 0)), constant_values=-1)
            btk = jnp.concatenate([btp[:w], btp[1:]], axis=1)
            sim = jnp.einsum('bhwid,bhwjd->bhwij', bq, bk)
            i = bt[:, :, None]
            j = btk[:, None, :]
            mask = (i < j) | (i > j + WINDOW) | (j == -1)
            sim = jnp.where(mask, -jnp.finfo(sim.dtype).max, sim)
            attn = jax.nn.softmax(sim, axis=-1)
            out = jnp.einsum('bhwij,bhwjd->bhwid', attn, bv)
            return out.reshape(b, h, n, d)

        def _layer(x, wqkv, qs, ksc, wo, lg, lb, w1, b1, w2, b2):
            b, n, _ = x.shape
            h = shift_token(x)
            qkv = h @ wqkv
            q, k, v = jnp.split(qkv, 3, axis=-1)
            to_heads = lambda t: t.reshape(b, n, HEADS, DIM_HEAD).transpose(0, 2, 1, 3)
            q, k, v = (to_heads(q), to_heads(k), to_heads(v))
            q = l2norm(q) * qs
            k = l2norm(k) * ksc
            q, k = rotary_xpos(q, k)
            o = local_attention(q, k, v)
            o = o.transpose(0, 2, 1, 3).reshape(b, n, INNER)
            x = x + o @ wo
            h = shift_token(x)
            mu = h.mean(-1, keepdims=True)
            var = h.var(-1, keepdims=True)
            h = (h - mu) / jnp.sqrt(var + 1e-05) * lg + lb
            h = h @ w1 + b1
            a, g = jnp.split(h, 2, axis=-1)
            h = a * jax.nn.gelu(g, approximate=False)
            x = x + h @ w2 + b2
            return x
        key = jax.random.key(seed)
        ks = jax.random.split(key, 6)
        return {'x': jax.random.normal(ks[0], (B, N, DIM), jnp.float32), 'wqkv': jax.random.normal(ks[1], (DEPTH, DIM, 3 * INNER), jnp.float32) * 0.02, 'q_scale': jnp.ones((DEPTH, DIM_HEAD), jnp.float32), 'k_scale': jnp.ones((DEPTH, DIM_HEAD), jnp.float32), 'wo': jax.random.normal(ks[2], (DEPTH, INNER, DIM), jnp.float32) * 0.02, 'ln_g': jnp.ones((DEPTH, DIM), jnp.float32), 'ln_b': jnp.zeros((DEPTH, DIM), jnp.float32), 'w1': jax.random.normal(ks[3], (DEPTH, DIM, 2 * HID), jnp.float32) * 0.02, 'b1': jnp.zeros((DEPTH, 2 * HID), jnp.float32), 'w2': jax.random.normal(ks[4], (DEPTH, HID, DIM), jnp.float32) * 0.02, 'b2': jnp.zeros((DEPTH, DIM), jnp.float32)}
    _L1_ffn_in = _L1_ffn_setup()

    def _L2_attn_setup():
        import jax, jax.numpy as jnp
        import numpy as np
        from jax import lax
        EPS = 1e-05

        def _rmsnorm(x, w):
            return x * lax.rsqrt(jnp.mean(x * x, axis=-1, keepdims=True) + EPS) * w

        def _mamba_block(u, W_in, conv_w, conv_b, W_x, W_dt, b_dt, A_log, Dp, W_out):
            ED, K = conv_w.shape
            R = W_dt.shape[0]
            N = A_log.shape[1]
            L = u.shape[1]
            xz = u @ W_in
            xs, z = (xz[..., :ED], xz[..., ED:])
            xc = lax.conv_general_dilated(xs.transpose(0, 2, 1), conv_w[:, None, :], window_strides=(1,), padding=[(K - 1, 0)], feature_group_count=ED) + conv_b[None, :, None]
            xc = jax.nn.silu(xc).transpose(0, 2, 1)
            dbc = xc @ W_x
            dt, Bm, Cm = (dbc[..., :R], dbc[..., R:R + N], dbc[..., R + N:])
            delta = jax.nn.softplus(dt @ W_dt + b_dt)
            A = -jnp.exp(A_log)
            dA = jnp.exp(delta[..., None] * A)
            dBx = delta[..., None] * Bm[:, :, None, :] * xc[..., None]

            def comb(c1, c2):
                a1, b1 = c1
                a2, b2 = c2
                return (a1 * a2, a2 * b1 + b2)
            _, h = lax.associative_scan(comb, (dA, dBx), axis=1)
            y = jnp.einsum('blen,bln->ble', h, Cm) + Dp * xc
            y = y * jax.nn.silu(z)
            return y @ W_out
        key = jax.random.key(seed)
        B, L, D = (1, 128, 128)
        ED, N, R, K = (2 * D, 16, 64, 4)
        ks = jax.random.split(key, 8)
        s = 0.02
        return {'x': jax.random.normal(ks[0], (B, L, D), dtype=jnp.float32), 'rms_w': jnp.ones((D,), jnp.float32), 'W_in': jax.random.normal(ks[1], (D, 2 * ED), jnp.float32) * s, 'conv_w': jax.random.normal(ks[2], (ED, K), jnp.float32) * s, 'conv_b': jnp.zeros((ED,), jnp.float32), 'W_x': jax.random.normal(ks[3], (ED, R + 2 * N), jnp.float32) * s, 'W_dt': jax.random.normal(ks[4], (R, ED), jnp.float32) * s, 'b_dt': jax.random.normal(ks[5], (ED,), jnp.float32) * 0.1, 'A_log': jnp.broadcast_to(jnp.log(jnp.arange(1, N + 1, dtype=jnp.float32)), (ED, N)).copy(), 'Dp': jnp.ones((ED,), jnp.float32), 'W_out': jax.random.normal(ks[6], (ED, D), jnp.float32) * s, 'ln_w': jnp.ones((D,), jnp.float32), 'ln_b': jnp.zeros((D,), jnp.float32)}
    _L2_attn_in = _L2_attn_setup()

    def _L2_ffn_setup():
        import jax, jax.numpy as jnp
        import numpy as np
        ALPHA = 1.0
        key = jax.random.key(seed)
        ks = jax.random.split(key, 7)
        B, S, IN, OUT = (8, 1024, 128, 128)
        RANK, DDIM, UDIM = (4, 100, 50)
        return {'hidden_states': jax.random.normal(ks[0], (B, S, IN), dtype=jnp.float32), 'W': jax.random.normal(ks[1], (OUT, IN), dtype=jnp.float32) * 0.02, 'b': jax.random.normal(ks[2], (OUT,), dtype=jnp.float32) * 0.02, 'lora_down': jax.random.normal(ks[3], (RANK, DDIM), dtype=jnp.float32) * 0.1, 'lora_up': jax.random.normal(ks[4], (UDIM, RANK), dtype=jnp.float32) * 0.1, 'down_aux': jax.random.normal(ks[5], (DDIM, IN), dtype=jnp.float32) * 0.03, 'up_aux': jax.random.normal(ks[6], (OUT, UDIM), dtype=jnp.float32) * 0.03}
    _L2_ffn_in = _L2_ffn_setup()

    def _L3_attn_setup():
        import jax, jax.numpy as jnp
        import numpy as np
        B, S, HID, NH = (4, 512, 128, 16)
        D = HID // NH
        EPS = 1e-05

        def _delta_scan(q, k, v, beta):
            vsum = v.sum(-1)
            qs = jnp.moveaxis(q, 1, 0)
            ks_ = jnp.moveaxis(k, 1, 0)
            vs = jnp.moveaxis(vsum, 1, 0)
            bs = jnp.moveaxis(beta, 1, 0)

            def step(h, inp):
                q_t, k_t, vsum_t, beta_t = inp
                h = h * beta_t[..., None, None]
                h = h + (k_t * vsum_t[..., None])[:, :, None, :]
                o_t = jnp.einsum('bhj,bhjk->bhk', q_t, h)
                return (h, o_t)
            h0 = jnp.zeros((q.shape[0], q.shape[2], D, D), dtype=q.dtype)
            _, o = jax.lax.scan(step, h0, (qs, ks_, vs, bs))
            return jnp.moveaxis(o, 0, 1)
        key = jax.random.key(seed)
        ks = jax.random.split(key, 8)
        x = jax.random.normal(ks[0], (B, S, HID), dtype=jnp.float32)
        sc = 0.03
        Wq = jax.random.normal(ks[1], (HID, HID), dtype=jnp.float32) * sc
        Wk = jax.random.normal(ks[2], (HID, HID), dtype=jnp.float32) * sc
        Wv = jax.random.normal(ks[3], (HID, HID), dtype=jnp.float32) * sc
        Wbeta = jax.random.normal(ks[4], (HID, NH), dtype=jnp.float32) * sc
        b_beta = jnp.full((NH,), 0.9, dtype=jnp.float32)
        Wo = jax.random.normal(ks[5], (HID, HID), dtype=jnp.float32) * sc
        b_o = jnp.zeros((HID,), dtype=jnp.float32)
        ln_g = jnp.ones((HID,), dtype=jnp.float32)
        ln_b = jnp.zeros((HID,), dtype=jnp.float32)
        return {'x': x, 'Wq': Wq, 'Wk': Wk, 'Wv': Wv, 'Wbeta': Wbeta, 'b_beta': b_beta, 'Wo': Wo, 'b_o': b_o, 'ln_g': ln_g, 'ln_b': ln_b}
    _L3_attn_in = _L3_attn_setup()

    def _L3_ffn_setup():
        import jax, jax.numpy as jnp
        import numpy as np
        D_MODEL = 128
        NUM_EXPERTS = 8
        TOP_K = 2
        B, S = (1, 256)
        key = jax.random.key(seed)
        ks = jax.random.split(key, 8)
        sd = 1.0 / np.sqrt(D_MODEL)
        x = jax.random.normal(ks[0], (B, S, D_MODEL), dtype=jnp.float32)
        gate_w = jax.random.normal(ks[1], (D_MODEL, NUM_EXPERTS), dtype=jnp.float32) * sd
        gate_b = jnp.zeros((NUM_EXPERTS,), dtype=jnp.float32)
        w1 = jax.random.normal(ks[2], (NUM_EXPERTS, D_MODEL, 8 * D_MODEL), dtype=jnp.float32) * sd
        b1 = jnp.zeros((NUM_EXPERTS, 8 * D_MODEL), dtype=jnp.float32)
        w2 = jax.random.normal(ks[3], (NUM_EXPERTS, 4 * D_MODEL, D_MODEL), dtype=jnp.float32) * (1.0 / np.sqrt(4 * D_MODEL))
        b2 = jnp.zeros((NUM_EXPERTS, D_MODEL), dtype=jnp.float32)
        return {'x': x, 'gate_w': gate_w, 'gate_b': gate_b, 'w1': w1, 'b1': b1, 'w2': w2, 'b2': b2}
    _L3_ffn_in = _L3_ffn_setup()
    _d = {'L0_attn_hidden_states': _L0_attn_in['hidden_states'], 'L0_attn_Wq': _L0_attn_in['Wq'], 'L0_attn_Wk': _L0_attn_in['Wk'], 'L0_attn_Wv': _L0_attn_in['Wv'], 'L0_attn_Wo': _L0_attn_in['Wo'], 'L0_ffn_Wg': _L0_ffn_in['Wg'], 'L0_ffn_W1': _L0_ffn_in['W1'], 'L0_ffn_W2': _L0_ffn_in['W2'], 'L0_ffn_W3': _L0_ffn_in['W3'], 'L1_attn_kernel': _L1_attn_in['kernel'], 'L1_attn_WO': _L1_attn_in['WO'], 'L1_ffn_wqkv': _L1_ffn_in['wqkv'], 'L1_ffn_q_scale': _L1_ffn_in['q_scale'], 'L1_ffn_k_scale': _L1_ffn_in['k_scale'], 'L1_ffn_wo': _L1_ffn_in['wo'], 'L1_ffn_ln_g': _L1_ffn_in['ln_g'], 'L1_ffn_ln_b': _L1_ffn_in['ln_b'], 'L1_ffn_w1': _L1_ffn_in['w1'], 'L1_ffn_b1': _L1_ffn_in['b1'], 'L1_ffn_w2': _L1_ffn_in['w2'], 'L1_ffn_b2': _L1_ffn_in['b2'], 'L2_attn_rms_w': _L2_attn_in['rms_w'], 'L2_attn_W_in': _L2_attn_in['W_in'], 'L2_attn_conv_w': _L2_attn_in['conv_w'], 'L2_attn_conv_b': _L2_attn_in['conv_b'], 'L2_attn_W_x': _L2_attn_in['W_x'], 'L2_attn_W_dt': _L2_attn_in['W_dt'], 'L2_attn_b_dt': _L2_attn_in['b_dt'], 'L2_attn_A_log': _L2_attn_in['A_log'], 'L2_attn_Dp': _L2_attn_in['Dp'], 'L2_attn_W_out': _L2_attn_in['W_out'], 'L2_attn_ln_w': _L2_attn_in['ln_w'], 'L2_attn_ln_b': _L2_attn_in['ln_b'], 'L2_ffn_W': _L2_ffn_in['W'], 'L2_ffn_b': _L2_ffn_in['b'], 'L2_ffn_lora_down': _L2_ffn_in['lora_down'], 'L2_ffn_lora_up': _L2_ffn_in['lora_up'], 'L2_ffn_down_aux': _L2_ffn_in['down_aux'], 'L2_ffn_up_aux': _L2_ffn_in['up_aux'], 'L3_attn_Wq': _L3_attn_in['Wq'], 'L3_attn_Wk': _L3_attn_in['Wk'], 'L3_attn_Wv': _L3_attn_in['Wv'], 'L3_attn_Wbeta': _L3_attn_in['Wbeta'], 'L3_attn_b_beta': _L3_attn_in['b_beta'], 'L3_attn_Wo': _L3_attn_in['Wo'], 'L3_attn_b_o': _L3_attn_in['b_o'], 'L3_attn_ln_g': _L3_attn_in['ln_g'], 'L3_attn_ln_b': _L3_attn_in['ln_b'], 'L3_ffn_gate_w': _L3_ffn_in['gate_w'], 'L3_ffn_gate_b': _L3_ffn_in['gate_b'], 'L3_ffn_w1': _L3_ffn_in['w1'], 'L3_ffn_b1': _L3_ffn_in['b1'], 'L3_ffn_w2': _L3_ffn_in['w2'], 'L3_ffn_b2': _L3_ffn_in['b2']}
    _x0 = _d['L0_attn_hidden_states']
    _d['L0_attn_hidden_states'] = jax.random.normal(jax.random.fold_in(jax.random.key(seed), 1), (4, 512, 128), dtype=_x0.dtype)
    del _x0
    return _d

def reference(L0_attn_hidden_states, L0_attn_Wq, L0_attn_Wk, L0_attn_Wv, L0_attn_Wo, L0_ffn_Wg, L0_ffn_W1, L0_ffn_W2, L0_ffn_W3, L1_attn_kernel, L1_attn_WO, L1_ffn_wqkv, L1_ffn_q_scale, L1_ffn_k_scale, L1_ffn_wo, L1_ffn_ln_g, L1_ffn_ln_b, L1_ffn_w1, L1_ffn_b1, L1_ffn_w2, L1_ffn_b2, L2_attn_rms_w, L2_attn_W_in, L2_attn_conv_w, L2_attn_conv_b, L2_attn_W_x, L2_attn_W_dt, L2_attn_b_dt, L2_attn_A_log, L2_attn_Dp, L2_attn_W_out, L2_attn_ln_w, L2_attn_ln_b, L2_ffn_W, L2_ffn_b, L2_ffn_lora_down, L2_ffn_lora_up, L2_ffn_down_aux, L2_ffn_up_aux, L3_attn_Wq, L3_attn_Wk, L3_attn_Wv, L3_attn_Wbeta, L3_attn_b_beta, L3_attn_Wo, L3_attn_b_o, L3_attn_ln_g, L3_attn_ln_b, L3_ffn_gate_w, L3_ffn_gate_b, L3_ffn_w1, L3_ffn_b1, L3_ffn_w2, L3_ffn_b2):

    def _L0_attn_ref(hidden_states, Wq, Wk, Wv, Wo):
        import jax, jax.numpy as jnp
        import numpy as np
        D_MODEL = 128
        N_HEADS = 16
        FEAT_DIM = 16
        V_DIM = 64
        EPS = 1e-12

        def taylor_exp(x):
            d = x.shape[-1]
            rd = jnp.sqrt(jnp.float32(d))
            rrd = jnp.sqrt(rd)
            r2 = jnp.sqrt(jnp.float32(2.0))
            x2 = (x[..., :, None] * x[..., None, :]).reshape(*x.shape[:-1], d * d) / r2
            ones = jnp.ones(x.shape[:-1] + (1,), dtype=x.dtype)
            return jnp.concatenate([ones, x / rrd, x2 / rd], axis=-1)
        b, l, _ = hidden_states.shape
        q = (hidden_states @ Wq).reshape(b, l, N_HEADS, FEAT_DIM).transpose(0, 2, 1, 3)
        k = (hidden_states @ Wk).reshape(b, l, N_HEADS, FEAT_DIM).transpose(0, 2, 1, 3)
        v = (hidden_states @ Wv).reshape(b, l, N_HEADS, V_DIM).transpose(0, 2, 1, 3)
        qf = taylor_exp(q)
        kf = taylor_exp(k)
        A = jnp.einsum('bhnf,bhmf->bhnm', qf, kf)
        A = jnp.tril(A)
        y = jnp.einsum('bhnm,bhme->bhne', A, v)
        z = 1.0 / (jnp.einsum('bhlf,bhlf->bhl', qf, jnp.cumsum(kf, axis=2)) + EPS)
        y = y * z[..., None]
        out = y.transpose(0, 2, 1, 3).reshape(b, l, N_HEADS * V_DIM) @ Wo
        return out

    def _L0_ffn_ref(x, Wg, W1, W2, W3):
        import jax, jax.numpy as jnp
        import numpy as np
        B, S, D, F, E, K = (2, 256, 128, 256, 8, 2)
        k = K
        scores = jnp.einsum('bsd,ed->bse', x, Wg)
        topk_scores, topk_idx = jax.lax.top_k(scores, k)
        topk_probs = jax.nn.softmax(topk_scores, axis=-1)
        h1 = jnp.einsum('bsd,efd->bsef', x, W1)
        h2 = jnp.einsum('bsd,efd->bsef', x, W2)
        hidden = jax.nn.silu(h1) * h2
        expert_out = jnp.einsum('bsef,edf->bsed', hidden, W3)
        onehot = jax.nn.one_hot(topk_idx, scores.shape[-1], dtype=x.dtype)
        gating = jnp.einsum('bsk,bske->bse', topk_probs, onehot)
        return jnp.einsum('bse,bsed->bsd', gating, expert_out)

    def _L1_attn_ref(x, kernel, WO):
        import jax, jax.numpy as jnp
        import numpy as np
        B, S, D_IN = (2, 256, 128)
        H, D_HEAD = (16, 64)
        b, s, _ = x.shape
        h, d = (kernel.shape[1], kernel.shape[3])
        q = jnp.einsum('bsm,hmd->bhsd', x, kernel[0])
        k = jnp.einsum('bsm,hmd->bhsd', x, kernel[1])
        v = jnp.einsum('bsm,hmd->bhsd', x, kernel[2])
        scale = jnp.float32(1.0 / (d * d * h))
        scores = jnp.einsum('bhsd,bhtd->bhst', q, k) * scale
        attn = jax.nn.softmax(scores, axis=-1)
        out = jnp.einsum('bhst,bhtd->bhsd', attn, v)
        out = jnp.transpose(out, (0, 2, 3, 1)).reshape(b, s, d * h)
        out = jnp.einsum('bsf,fm->bsm', out, WO[0])
        return out

    def _L1_ffn_ref(x, wqkv, q_scale, k_scale, wo, ln_g, ln_b, w1, b1, w2, b2):
        import jax, jax.numpy as jnp
        import numpy as np
        DIM = 128
        DEPTH = 2
        HEADS = 8
        DIM_HEAD = 64
        WINDOW = 64
        INNER = HEADS * DIM_HEAD
        HID = int(DIM * 4 * 2 / 3)
        B, N = (2, 1024)
        QK_SCALE = 8.0

        def shift_token(t):
            t1, t2 = jnp.split(t, 2, axis=-1)
            t2 = jnp.pad(t2, ((0, 0), (1, 0), (0, 0)))[:, :-1]
            return jnp.concatenate([t1, t2], axis=-1)

        def l2norm(t):
            return t / jnp.clip(jnp.linalg.norm(t, axis=-1, keepdims=True), 1e-12)

        def rotate_half(x):
            x1, x2 = jnp.split(x, 2, axis=-1)
            return jnp.concatenate([-x2, x1], axis=-1)

        def rotary_xpos(q, k):
            n = q.shape[-2]
            half_idx = jnp.arange(0, DIM_HEAD, 2, dtype=jnp.float32)
            inv_freq = 1.0 / 10000.0 ** (half_idx / DIM_HEAD)
            t = jnp.arange(n, dtype=jnp.float32)
            freqs = t[:, None] * inv_freq[None, :]
            freqs = jnp.concatenate([freqs, freqs], axis=-1)
            base = (half_idx + 0.4 * DIM_HEAD) / (1.4 * DIM_HEAD)
            power = (t - n // 2) / float(WINDOW // 2)
            scale = base[None, :] ** power[:, None]
            scale = jnp.concatenate([scale, scale], axis=-1)
            cos, sin = (jnp.cos(freqs), jnp.sin(freqs))
            q = q * cos * scale + rotate_half(q) * sin * scale
            k = k * cos / scale + rotate_half(k) * sin / scale
            return (q, k)

        def local_attention(q, k, v):
            b, h, n, d = q.shape
            w = n // WINDOW
            bq = q.reshape(b, h, w, WINDOW, d) * QK_SCALE
            bk = k.reshape(b, h, w, WINDOW, d)
            bv = v.reshape(b, h, w, WINDOW, d)

            def look_around(t):
                p = jnp.pad(t, ((0, 0), (0, 0), (1, 0), (0, 0), (0, 0)))
                return jnp.concatenate([p[:, :, :w], p[:, :, 1:]], axis=3)
            bk, bv = (look_around(bk), look_around(bv))
            bt = jnp.arange(n).reshape(w, WINDOW)
            btp = jnp.pad(bt, ((1, 0), (0, 0)), constant_values=-1)
            btk = jnp.concatenate([btp[:w], btp[1:]], axis=1)
            sim = jnp.einsum('bhwid,bhwjd->bhwij', bq, bk)
            i = bt[:, :, None]
            j = btk[:, None, :]
            mask = (i < j) | (i > j + WINDOW) | (j == -1)
            sim = jnp.where(mask, -jnp.finfo(sim.dtype).max, sim)
            attn = jax.nn.softmax(sim, axis=-1)
            out = jnp.einsum('bhwij,bhwjd->bhwid', attn, bv)
            return out.reshape(b, h, n, d)

        def _layer(x, wqkv, qs, ksc, wo, lg, lb, w1, b1, w2, b2):
            b, n, _ = x.shape
            h = shift_token(x)
            qkv = h @ wqkv
            q, k, v = jnp.split(qkv, 3, axis=-1)
            to_heads = lambda t: t.reshape(b, n, HEADS, DIM_HEAD).transpose(0, 2, 1, 3)
            q, k, v = (to_heads(q), to_heads(k), to_heads(v))
            q = l2norm(q) * qs
            k = l2norm(k) * ksc
            q, k = rotary_xpos(q, k)
            o = local_attention(q, k, v)
            o = o.transpose(0, 2, 1, 3).reshape(b, n, INNER)
            x = x + o @ wo
            h = shift_token(x)
            mu = h.mean(-1, keepdims=True)
            var = h.var(-1, keepdims=True)
            h = (h - mu) / jnp.sqrt(var + 1e-05) * lg + lb
            h = h @ w1 + b1
            a, g = jnp.split(h, 2, axis=-1)
            h = a * jax.nn.gelu(g, approximate=False)
            x = x + h @ w2 + b2
            return x
        for l in range(DEPTH):
            x = _layer(x, wqkv[l], q_scale[l], k_scale[l], wo[l], ln_g[l], ln_b[l], w1[l], b1[l], w2[l], b2[l])
        return x

    def _L2_attn_ref(x, rms_w, W_in, conv_w, conv_b, W_x, W_dt, b_dt, A_log, Dp, W_out, ln_w, ln_b):
        import jax, jax.numpy as jnp
        import numpy as np
        from jax import lax
        EPS = 1e-05

        def _rmsnorm(x, w):
            return x * lax.rsqrt(jnp.mean(x * x, axis=-1, keepdims=True) + EPS) * w

        def _mamba_block(u, W_in, conv_w, conv_b, W_x, W_dt, b_dt, A_log, Dp, W_out):
            ED, K = conv_w.shape
            R = W_dt.shape[0]
            N = A_log.shape[1]
            L = u.shape[1]
            xz = u @ W_in
            xs, z = (xz[..., :ED], xz[..., ED:])
            xc = lax.conv_general_dilated(xs.transpose(0, 2, 1), conv_w[:, None, :], window_strides=(1,), padding=[(K - 1, 0)], feature_group_count=ED) + conv_b[None, :, None]
            xc = jax.nn.silu(xc).transpose(0, 2, 1)
            dbc = xc @ W_x
            dt, Bm, Cm = (dbc[..., :R], dbc[..., R:R + N], dbc[..., R + N:])
            delta = jax.nn.softplus(dt @ W_dt + b_dt)
            A = -jnp.exp(A_log)
            dA = jnp.exp(delta[..., None] * A)
            dBx = delta[..., None] * Bm[:, :, None, :] * xc[..., None]

            def comb(c1, c2):
                a1, b1 = c1
                a2, b2 = c2
                return (a1 * a2, a2 * b1 + b2)
            _, h = lax.associative_scan(comb, (dA, dBx), axis=1)
            y = jnp.einsum('blen,bln->ble', h, Cm) + Dp * xc
            y = y * jax.nn.silu(z)
            return y @ W_out
        depth = 6
        for _ in range(depth):
            inner = _mamba_block(_rmsnorm(x, rms_w), W_in, conv_w, conv_b, W_x, W_dt, b_dt, A_log, Dp, W_out) + x
            x = inner + x
        mu = jnp.mean(x, axis=-1, keepdims=True)
        var = jnp.mean((x - mu) ** 2, axis=-1, keepdims=True)
        return (x - mu) * lax.rsqrt(var + EPS) * ln_w + ln_b

    def _L2_ffn_ref(hidden_states, W, b, lora_down, lora_up, down_aux, up_aux):
        import jax, jax.numpy as jnp
        import numpy as np
        ALPHA = 1.0
        lilora_weight = up_aux @ (lora_up @ (lora_down @ down_aux))
        base = jnp.einsum('bsi,oi->bso', hidden_states, W) + b
        delta = jnp.einsum('bsi,oi->bso', hidden_states, lilora_weight)
        return base + ALPHA * delta

    def _L3_attn_ref(x, Wq, Wk, Wv, Wbeta, b_beta, Wo, b_o, ln_g, ln_b):
        import jax, jax.numpy as jnp
        import numpy as np
        B, S, HID, NH = (4, 512, 128, 16)
        D = HID // NH
        EPS = 1e-05

        def _delta_scan(q, k, v, beta):
            vsum = v.sum(-1)
            qs = jnp.moveaxis(q, 1, 0)
            ks_ = jnp.moveaxis(k, 1, 0)
            vs = jnp.moveaxis(vsum, 1, 0)
            bs = jnp.moveaxis(beta, 1, 0)

            def step(h, inp):
                q_t, k_t, vsum_t, beta_t = inp
                h = h * beta_t[..., None, None]
                h = h + (k_t * vsum_t[..., None])[:, :, None, :]
                o_t = jnp.einsum('bhj,bhjk->bhk', q_t, h)
                return (h, o_t)
            h0 = jnp.zeros((q.shape[0], q.shape[2], D, D), dtype=q.dtype)
            _, o = jax.lax.scan(step, h0, (qs, ks_, vs, bs))
            return jnp.moveaxis(o, 0, 1)
        b, s, hid = x.shape
        residual = x
        q = (x @ Wq).reshape(b, s, NH, D)
        k = (x @ Wk).reshape(b, s, NH, D)
        v = (x @ Wv).reshape(b, s, NH, D)
        beta = jax.nn.sigmoid(x @ Wbeta + b_beta)
        o = _delta_scan(q, k, v, beta).reshape(b, s, hid)
        out = o @ Wo + b_o
        y = residual + out
        mu = y.mean(-1, keepdims=True)
        var = ((y - mu) ** 2).mean(-1, keepdims=True)
        return ln_g * (y - mu) * jax.lax.rsqrt(var + EPS) + ln_b

    def _L3_ffn_ref(x, gate_w, gate_b, w1, b1, w2, b2):
        import jax, jax.numpy as jnp
        import numpy as np
        D_MODEL = 128
        NUM_EXPERTS = 8
        TOP_K = 2
        B, S = (1, 256)
        gate_logits = jnp.einsum('bsd,de->bse', x, gate_w) + gate_b
        weights, indices = jax.lax.top_k(gate_logits, TOP_K)
        weights = jax.nn.softmax(weights, axis=-1)
        h = jnp.einsum('bsd,edh->ebsh', x, w1) + b1[:, None, None, :]
        xh, gh = jnp.split(h, 2, axis=-1)
        act = jax.nn.silu(gh) * xh
        out_e = jnp.einsum('ebsf,efd->ebsd', act, w2) + b2[:, None, None, :]
        out_e = jnp.transpose(out_e, (1, 2, 0, 3))
        sel = jnp.take_along_axis(out_e, indices[..., None], axis=2)
        return jnp.sum(sel * weights[..., None], axis=2)
    x = L0_attn_hidden_states
    x = x + _L0_attn_ref(_layernorm(x, axis=-1), L0_attn_Wq, L0_attn_Wk, L0_attn_Wv, L0_attn_Wo)
    x = x + _L0_ffn_ref(_layernorm(x, axis=-1), L0_ffn_Wg, L0_ffn_W1, L0_ffn_W2, L0_ffn_W3)
    x = x + _L1_attn_ref(_layernorm(x, axis=-1), L1_attn_kernel, L1_attn_WO)
    x = x + _L1_ffn_ref(_layernorm(x, axis=-1), L1_ffn_wqkv, L1_ffn_q_scale, L1_ffn_k_scale, L1_ffn_wo, L1_ffn_ln_g, L1_ffn_ln_b, L1_ffn_w1, L1_ffn_b1, L1_ffn_w2, L1_ffn_b2)
    x = x + _L2_attn_ref(_layernorm(x, axis=-1), L2_attn_rms_w, L2_attn_W_in, L2_attn_conv_w, L2_attn_conv_b, L2_attn_W_x, L2_attn_W_dt, L2_attn_b_dt, L2_attn_A_log, L2_attn_Dp, L2_attn_W_out, L2_attn_ln_w, L2_attn_ln_b)
    x = x + _L2_ffn_ref(_layernorm(x, axis=-1), L2_ffn_W, L2_ffn_b, L2_ffn_lora_down, L2_ffn_lora_up, L2_ffn_down_aux, L2_ffn_up_aux)
    x = x + _L3_attn_ref(_layernorm(x, axis=-1), L3_attn_Wq, L3_attn_Wk, L3_attn_Wv, L3_attn_Wbeta, L3_attn_b_beta, L3_attn_Wo, L3_attn_b_o, L3_attn_ln_g, L3_attn_ln_b)
    x = x + _L3_ffn_ref(_layernorm(x, axis=-1), L3_ffn_gate_w, L3_ffn_gate_b, L3_ffn_w1, L3_ffn_b1, L3_ffn_w2, L3_ffn_b2)
    return x

_drawn_inputs = setup_inputs


def setup_inputs(seed=0):
    import zlib

    import numpy as np

    out = dict(_drawn_inputs(seed))
    spreads = {'L1_ffn_q_scale': (1.0, 0.6),
     'L1_ffn_k_scale': (1.0, 0.6),
     'L1_ffn_ln_g': (1.0, 0.6),
     'L1_ffn_ln_b': (0.0, 0.8),
     'L1_ffn_b1': (0.0, 0.8),
     'L1_ffn_b2': (0.0, 0.435),
     'L2_attn_rms_w': (1.0, 0.6),
     'L2_attn_conv_b': (0.0, 0.8),
     'L2_attn_Dp': (1.0, 0.6),
     'L2_attn_ln_w': (1.0, 0.6),
     'L2_attn_ln_b': (0.0, 0.8),
     'L3_attn_b_beta': (0.8999999761581421, 0.6),
     'L3_attn_b_o': (0.0, 2.0),
     'L3_attn_ln_g': (1.0, 0.6),
     'L3_attn_ln_b': (0.0, 0.8),
     'L3_ffn_gate_b': (0.0, 2.0),
     'L3_ffn_b1': (0.0, 2.0),
     'L3_ffn_b2': (0.0, 2.0)}
    factors = {'L0_ffn_Wg': 8.0,
     'L0_ffn_W1': 8.0,
     'L0_ffn_W2': 7.861,
     'L0_ffn_W3': 8.0,
     'L1_ffn_w1': 5.747,
     'L1_ffn_w2': 5.741,
     'L2_attn_W_in': 8.0,
     'L2_attn_conv_w': 8.0,
     'L2_attn_W_x': 8.0,
     'L2_attn_W_dt': 8.0,
     'L2_attn_b_dt': 8.0,
     'L2_attn_A_log': 8.0,
     'L2_attn_W_out': 8.0,
     'L2_ffn_b': 59.984,
     'L2_ffn_lora_down': 8.0,
     'L2_ffn_lora_up': 8.0,
     'L2_ffn_down_aux': 8.0,
     'L2_ffn_up_aux': 8.0,
     'L3_attn_Wbeta': 64.0,
     'L2_ffn_W': 8.0,
     'L3_attn_Wq': 8.0,
     'L3_attn_Wk': 8.0,
     'L3_attn_Wv': 8.0,
     'L3_attn_Wo': 8.0,
     'L3_ffn_gate_w': 5.555,
     'L3_ffn_w1': 6.135,
     'L3_ffn_w2': 5.937}
    for name, (base, spread) in spreads.items():
        noise = np.random.default_rng([zlib.crc32(name.encode()), seed]).standard_normal(out[name].shape)
        drawn = base * np.exp(spread * noise) if base else spread * noise
        out[name] = jnp.asarray(drawn.astype(out[name].dtype))
    for name, factor in factors.items():
        out[name] = (out[name] * factor).astype(out[name].dtype)
    return out
```

```python
from contextlib import ExitStack, contextmanager

import numpy as np
import concourse.bass as bass
from concourse import mybir

F32 = mybir.dt.float32
ALU = mybir.AluOpType
ACT = mybir.ActivationFunctionType
AX = mybir.AxisListType

P = 128
BATCH, S = 4, 512
GROUP = 2
NT = S // P
EPS = 1e-5
EXPLN = "natural_log_exp_and_others"

L0H, L0F, HD = 16, 16, 64
EXPERTS = 8
LH, LD, WIN = 8, 64, 64
HID = 341
HT = [(0, 128), (128, 128), (256, HID - 256)]
DEPTH, ED, NS, RANK, TAPS = 6, 256, 16, 64, 4
ET = ED // P
NGR = 4
MOE_F = 512
ROUTE_COLS = NT * EXPERTS


class Bag:
    pass


def flat(ap):
    return ap.rearrange("p a b -> p (a b)")


@contextmanager
def Stage(nc, names):
    with ExitStack() as ctx:
        sems = {n: ctx.enter_context(nc.semaphore(n)) for n in names.split()}
        yield sems
        for q in sems.values():
            nc.sync.sem_clear(q)
        nc.all_engine_barrier()


LN_SEMS = " ln_mean ln_xc ln_sq ln_var ln_log ln_rstd xn_ready "


def ln_tensor(pe, k, s, src, src_ready=None):
    for c in range(GROUP):
        if src_ready is not None:
            pe.wait_ge(src_ready, c + 1)
        pe.matmul(k.ps[:, 6 + c, :], k.mean_mat[:, :], src[:, c, :], start=True, stop=True).then_inc(s["ln_mean"], 1)
    for c in range(GROUP):
        pe.wait_ge(s["ln_sq"], c + 1)
        pe.matmul(k.ps[:, 6 + c, :], k.mean_mat[:, :], k.sq[:, c, :], start=True, stop=True).then_inc(s["ln_var"], 1)


def ln_scalar(act, k, s):
    for c in range(GROUP):
        act.wait_ge(s["ln_xc"], c + 1)
        act.activation(k.sq[:, c, :], k.xc[:, c, :], ACT.Square).then_inc(s["ln_sq"], 1)
    for c in range(GROUP):
        act.wait_ge(s["ln_var"], c + 1)
        act.activation(k.sq[:, c, :], k.ps[:, 6 + c, :], ACT.Ln, bias=k.eps[:, 0:1]).then_inc(s["ln_log"], 1)
        act.wait_ge(s["ln_log"], c + 1)
        act.activation(k.sq[:, c, :], k.sq[:, c, :], ACT.Exp, scale=-0.5).then_inc(s["ln_rstd"], 1)


def ln_vector(dve, k, s, src, dst):
    for c in range(GROUP):
        dve.wait_ge(s["ln_mean"], c + 1)
        dve.tensor_tensor(k.xc[:, c, :], src[:, c, :], k.ps[:, 6 + c, :], ALU.subtract).then_inc(s["ln_xc"], 1)
    for c in range(GROUP):
        dve.wait_ge(s["ln_rstd"], c + 1)
        dve.tensor_tensor(dst[:, c, :], k.xc[:, c, :], k.sq[:, c, :], ALU.mult).then_inc(s["xn_ready"], 1)


ROUTE_SEMS = " logits_ps route_chain route_diff route_exp gate_tm gate_ps gate_sb "


def route_tensor_logits(pe, k, s, c, w_gate):
    for t in range(NT):
        mm = pe.matmul(k.ps[:, c, EXPERTS * t:EXPERTS * (t + 1)], k.xn[:, c, P * t:P * (t + 1)], w_gate[:, :],
                       start=True, stop=True)
    mm.then_inc(s["logits_ps"], 1)


def route_tensor_turn(pe, k, s, c):
    pe.wait_ge(s["gate_tm"], c + 1)
    for t in range(NT):
        mm = pe.transpose(k.ps[0:EXPERTS, 2 + c, P * t:P * (t + 1)], k.gates[:, c, t, :], k.ident[:, :])
    mm.then_inc(s["gate_ps"], 1)


def route_scalar(act, k, s, c):
    act.wait_ge(s["route_diff"], c + 1)
    act.activation(k.r_exp[:, c, :, :], k.r_diff[:, c, :, :], ACT.Exp).then_inc(s["route_exp"], 1)


def route_vector(dve, k, s, c, done, gate_b=None):

    def link(ins):
        done[0] += 1
        ins.then_inc(s["route_chain"], 1)
        dve.wait_ge(s["route_chain"], done[0])

    lg = k.r_logit[:, c, :, :]
    dve.wait_ge(s["logits_ps"], c + 1)
    link(dve.tensor_copy(flat(lg), k.ps[:, c, 0:ROUTE_COLS]))
    if gate_b is not None:
        link(dve.tensor_tensor(lg, lg, gate_b[:, None, :].to_broadcast([P, NT, EXPERTS]), ALU.add))
    shape = [P, NT, EXPERTS, EXPERTS]
    other, own = lg[:, :, None, :].to_broadcast(shape), lg[:, :, :, None].to_broadcast(shape)
    dve.tensor_tensor(k.r_gt[:, :, :, :], other, own, ALU.is_gt)
    link(dve.tensor_tensor(k.r_eq[:, :, :, :], other, own, ALU.is_equal))
    link(dve.tensor_tensor(k.r_eq[:, :, :, :], k.r_eq[:, :, :, :],
                           k.lower[:, None, :, :].to_broadcast(shape), ALU.mult))
    link(dve.tensor_tensor(k.r_gt[:, :, :, :], k.r_gt[:, :, :, :], k.r_eq[:, :, :, :], ALU.add))
    link(dve.tensor_reduce(k.r_rank[:, :, :], k.r_gt[:, :, :, :], AX.X, ALU.add))
    dve.tensor_scalar(k.r_sel[:, :, :], k.r_rank[:, :, :], 2.0, None, ALU.is_lt)
    link(dve.tensor_reduce(k.r_max[:, :], lg, AX.X, ALU.max))
    dve.tensor_tensor(k.r_diff[:, c, :, :], lg, k.r_max[:, :, None].to_broadcast([P, NT, EXPERTS]),
                      ALU.subtract).then_inc(s["route_diff"], 1)
    dve.wait_ge(s["route_exp"], c + 1)
    link(dve.tensor_tensor(k.r_sel[:, :, :], k.r_sel[:, :, :], k.r_exp[:, c, :, :], ALU.mult))
    link(dve.tensor_reduce(k.r_sum[:, :], k.r_sel[:, :, :], AX.X, ALU.add))
    link(dve.reciprocal(k.r_sum[:, :], k.r_sum[:, :]))
    dve.tensor_tensor(k.gates[:, c, :, :], k.r_sel[:, :, :], k.r_sum[:, :, None].to_broadcast([P, NT, EXPERTS]),
                      ALU.mult).then_inc(s["gate_tm"], 1)
    dve.wait_ge(s["gate_ps"], c + 1)
    dve.tensor_copy(k.gate_t[:, c, :], k.ps[0:EXPERTS, 2 + c, :]).then_inc(s["gate_sb"], 1)


def stage_load(nc, k, g, x_dram):
    with Stage(nc, "x_in x_turned x_sb") as s:
        with nc.Block() as block:
            @block.sync
            def _(sp):
                sp.dma_start(k.tok[:, :, :, :], x_dram[bass.ds(g * GROUP, GROUP), :, :]
                             .rearrange("b (t p) d -> p b t d", p=P)).then_inc(s["x_in"], 16)

            @block.tensor
            def _(pe):
                pe.wait_ge(s["x_in"], 16)
                for c in range(GROUP):
                    for t in range(NT):
                        mm = pe.transpose(k.ps[:, c, P * t:P * (t + 1)], k.tok[:, c, t, :], k.ident[:, :])
                    mm.then_inc(s["x_turned"], 1)

            @block.vector
            def _(dve):
                for c in range(GROUP):
                    dve.wait_ge(s["x_turned"], c + 1)
                    dve.tensor_copy(k.x[:, c, :], k.ps[:, c, :]).then_inc(s["x_sb"], 1)


def stage_taylor(nc, k, w):
    WIDE = [S - P * t for t in range(NT)]
    OFF = [sum(WIDE[:t]) for t in range(NT)]
    COLS = sum(WIDE)
    BANKCOLS = [(OFF[0], WIDE[0]), (OFF[1], WIDE[1]), (OFF[2], WIDE[2] + WIDE[3])]
    NPROJ = 4 + 4 + 2 * NT
    with ExitStack() as mem, Stage(nc, LN_SEMS + "zeroed wts mask_v ones_v mask_rdy proj_ps proj_act proj_dve scored squared "
                                   "masked y_ps z_log z_rec normed out_ps x_new") as s:
        sb = lambda n, sh: mem.enter_context(nc.sbuf_tensor(n, sh, F32))
        wq, wk = sb("t_wq", [P, L0H, 32]), sb("t_wk", [P, L0H, 32])
        wv, wo = sb("t_wv", [P, L0H * HD]), sb("t_wo", [P, L0H * HD // P, P])
        qt, kt = sb("t_q", [P, 4, S]), sb("t_k", [P, 4, S])
        v = sb("t_v", [P, NT, L0H // 2, 3, HD])
        a = sb("t_a", [P, 2, COLS])
        mask = sb("t_mask", [P, COLS])
        rz = sb("t_rz", [P, 2, S])
        o = sb("t_o", [P, L0H // 2, S])
        ps = k.ps
        with nc.Block() as block:
            @block.sync
            def _(sp):
                sp.dma_start(wv[:, :], w["L0_attn_Wv"]).then_inc(s["wts"], 16)
                sp.dma_start(wo[:, :, :], w["L0_attn_Wo"].rearrange("(t p) d -> p t d", p=P)).then_inc(s["wts"], 16)
                sp.wait_ge(s["zeroed"], 2)
                sp.dma_start(wq[:, :, 0:L0F], w["L0_attn_Wq"].rearrange("p (h f) -> p h f", f=L0F)).then_inc(s["wts"], 16)
                sp.dma_start(wk[:, :, 0:L0F], w["L0_attn_Wk"].rearrange("p (h f) -> p h f", f=L0F)).then_inc(s["wts"], 16)

            @block.gpsimd
            def _(pool):
                pool.memset(wq[:, :, :], 0.0).then_inc(s["zeroed"], 1)
                pool.memset(wk[:, :, :], 0.0).then_inc(s["zeroed"], 1)
                pool.memset(v[:, :, :, 1, :], 1.0).then_inc(s["ones_v"], 1)
                pool.memset(mask[:, :], 1.0).then_inc(s["mask_v"], 1)
                pool.wait_ge(s["mask_v"], 1)
                for t in range(NT):
                    m = mask[:, OFF[t]:OFF[t] + P]
                    pool.affine_select(out=m, in_=m, compare_op=ALU.is_ge, fill=0.0, base=0,
                                       pattern=[[1, P]], channel_multiplier=-1).then_inc(s["mask_rdy"], 1)

            @block.tensor
            def _(pe):
                ln_tensor(pe, k, s, k.x)
                pe.wait_ge(s["wts"], 64)

                def scores(i):
                    h = i % L0H
                    if i >= 2:
                        pe.wait_ge(s["squared"], 3 * (i - 1))
                    m, r = h // 4, 32 * (h % 4)
                    for t in range(NT):
                        bank, col = 3 * (i % 2) + min(t, 2), (WIDE[2] if t == 3 else 0)
                        mm = pe.matmul(ps[:, bank, col:col + WIDE[t]], kt[r:r + 32, m, P * t:P * (t + 1)],
                                       qt[r:r + 32, m, P * t:S], start=True, stop=True)
                        if t != 2:
                            mm.then_inc(s["scored"], 1)

                def values(i):
                    h = i % L0H
                    pe.wait_ge(s["masked"], i + 1)
                    if i >= 2:
                        pe.wait_ge(s["normed"], i - 1)
                    for t in range(NT):
                        mm = pe.matmul(ps[:, 6 + i % 2, P * t:S], v[:, t, h // 2, h % 2:h % 2 + 2, :],
                                       a[:, i % 2, OFF[t]:OFF[t] + WIDE[t]], start=(t == 0), stop=(t == NT - 1))
                    mm.then_inc(s["y_ps"], 1)

                for c in range(GROUP):
                    pe.wait_ge(s["xn_ready"], c + 1)
                    for n in range(NPROJ):
                        if n >= 6:
                            pe.wait_ge(s["proj_dve"] if n % 2 else s["proj_act"], c * NPROJ // 2 + (n - 6) // 2 + 1)
                        if n == 5 and c > 0:
                            pe.wait_ge(s["x_new"], c)
                        if n < 8:
                            pe.matmul(ps[:, n % 6, :], flat((wk if n % 2 else wq)[:, 4 * (n // 2):4 * (n // 2) + 4, :]),
                                      k.xn[:, c, :], start=True, stop=True).then_inc(s["proj_ps"], 1)
                        else:
                            t, half = (n - 8) // 2, n % 2
                            pe.matmul(ps[:, n % 6, :], k.xn[:, c, P * t:P * (t + 1)], wv[:, 512 * half:512 * half + 512],
                                      start=True, stop=True).then_inc(s["proj_ps"], 1)
                    pe.wait_ge(s["proj_act"], (c + 1) * NPROJ // 2)
                    pe.wait_ge(s["proj_dve"], (c + 1) * NPROJ // 2)
                    if c == 0:
                        pe.wait_ge(s["ones_v"], 1)
                    scores(c * L0H)
                    for h in range(L0H):
                        i = c * L0H + h
                        if h + 1 < L0H:
                            scores(i + 1)
                        values(i)
                    pe.wait_ge(s["normed"], (c + 1) * L0H)
                    for t in range(L0H // 2):
                        mm = pe.matmul(ps[:, 5, :], wo[:, t, :], o[:, t, :], start=(t == 0), stop=(t == L0H // 2 - 1))
                    mm.then_inc(s["out_ps"], 1)

            @block.scalar
            def _(act):
                act.preload_act_table_set(EXPLN)
                ln_scalar(act, k, s)

                def square(i):
                    if i >= 2:
                        act.wait_ge(s["y_ps"], i - 1)
                    for n, (off, wide) in enumerate(BANKCOLS):
                        act.wait_ge(s["scored"], 3 * i + n + 1)
                        act.activation(a[:, i % 2, off:off + wide], ps[:, 3 * (i % 2) + n, 0:wide], ACT.Square,
                                       bias=1.0, scale=0.25).then_inc(s["squared"], 1)

                def invert(i):
                    r = 0 if i % 2 else HD
                    act.wait_ge(s["y_ps"], i + 1)
                    if i >= 2:
                        act.wait_ge(s["normed"], i - 1)
                    act.activation(rz[r:r + HD, i % 2, :], ps[r:r + HD, 6 + i % 2, :], ACT.Ln,
                                   bias=k.eps_z[r:r + HD, 0:1]).then_inc(s["z_log"], 1)
                    act.wait_ge(s["z_log"], i + 1)
                    act.activation(rz[r:r + HD, i % 2, :], rz[r:r + HD, i % 2, :], ACT.Exp, scale=-1.0).then_inc(s["z_rec"], 1)

                for c in range(GROUP):
                    for n in range(0, NPROJ, 2):
                        act.wait_ge(s["proj_ps"], c * NPROJ + n + 1)
                        if n < 8:
                            act.activation(qt[:, n // 2, :], ps[:, n % 6, :], ACT.Copy).then_inc(s["proj_act"], 1)
                        else:
                            act.activation(v[:, (n - 8) // 2, 0:4, 0:3:2, :], ps[:, n % 6, :]
                                           .rearrange("p (a b e) -> p a b e", b=2, e=HD), ACT.Copy).then_inc(s["proj_act"], 1)
                    square(c * L0H)
                    for h in range(L0H):
                        i = c * L0H + h
                        if h + 1 < L0H:
                            square(i + 1)
                        invert(i)

            @block.vector
            def _(dve):
                ln_vector(dve, k, s, k.x, k.xn)
                for c in range(GROUP):
                    for n in range(1, NPROJ, 2):
                        dve.wait_ge(s["proj_ps"], c * NPROJ + n + 1)
                        if n < 8:
                            dve.tensor_copy(kt[:, n // 2, :], ps[:, n % 6, :]).then_inc(s["proj_dve"], 1)
                        else:
                            dve.tensor_copy(v[:, (n - 8) // 2, 4:8, 0:3:2, :], ps[:, n % 6, :]
                                            .rearrange("p (a b e) -> p a b e", b=2, e=HD)).then_inc(s["proj_dve"], 1)
                    if c == 0:
                        dve.wait_ge(s["mask_rdy"], NT)

                    def weights(i):
                        dve.wait_ge(s["squared"], 3 * (i + 1))
                        dve.scalar_tensor_tensor(a[:, i % 2, :], a[:, i % 2, :], 1.0, mask[:, :],
                                                 ALU.add, ALU.mult).then_inc(s["masked"], 1)

                    def normalise(i):
                        r = HD * (i % 2)
                        dve.wait_ge(s["z_rec"], i + 1)
                        dve.tensor_tensor(o[r:r + HD, (i % L0H) // 2, :], ps[r:r + HD, 6 + i % 2, :],
                                          rz[HD - r:P - r, i % 2, :], ALU.mult).then_inc(s["normed"], 1)

                    weights(c * L0H)
                    for h in range(L0H):
                        i = c * L0H + h
                        if h + 1 < L0H:
                            weights(i + 1)
                        normalise(i)
                    dve.wait_ge(s["out_ps"], c + 1)
                    dve.tensor_tensor(k.x[:, c, :], k.x[:, c, :], ps[:, 5, :], ALU.add).then_inc(s["x_new"], 1)


def stage_moe(nc, k, name, w_gate_d, gate_b_d, wa_d, wb_d, wc_d, FT, ba_d=None, bb_d=None, bc_d=None):
    STEPS = EXPERTS * FT
    biased = ba_d is not None
    with ExitStack() as mem, Stage(nc, LN_SEMS + ROUTE_SEMS + "wg_in wab_in wc_in hid_ps silu_sb half_sb hid_sb down_ps x_new") as s:
        sb = lambda n, sh: mem.enter_context(nc.sbuf_tensor(name + n, sh, F32))
        wg = sb("wg", [P, EXPERTS])
        wa, wb = sb("wa", [P, EXPERTS, FT * P]), sb("wb", [P, EXPERTS, FT * P])
        wc = sb("wc", [P, EXPERTS, FT, P])
        sg, hid = sb("sg", [P, 2, S]), sb("hid", [P, 2, S])
        if biased:
            gb, ba, bb, bc = sb("gb", [P, EXPERTS]), sb("ba", [P, EXPERTS, FT]), sb("bb", [P, EXPERTS, FT]), sb("bc", [EXPERTS, P])
        k.r_logit, k.r_diff, k.r_exp = [sb(n, [P, GROUP, NT, EXPERTS]) for n in ("rl", "rd", "re")]
        k.gates = sb("gates", [P, GROUP, NT, EXPERTS])
        k.r_gt, k.r_eq = [sb(n, [P, NT, EXPERTS, EXPERTS]) for n in ("rg", "rq")]
        k.r_rank, k.r_sel = [sb(n, [P, NT, EXPERTS]) for n in ("rr", "rs")]
        k.r_max, k.r_sum = [sb(n, [P, NT]) for n in ("rm", "ru")]
        k.gate_t = sb("gt", [EXPERTS, GROUP, S])
        ps = k.ps
        WG_DMAS = 5 if biased else 1
        with nc.Block() as block:
            @block.sync
            def _(sp):
                sp.dma_start(wg[:, :], w_gate_d).then_inc(s["wg_in"], 16)
                if biased:
                    sp.dma_start(gb[:, :], gate_b_d[None, :].to_broadcast([P, EXPERTS])).then_inc(s["wg_in"], 16)
                    sp.dma_start(ba[:, :, :], ba_d).then_inc(s["wg_in"], 16)
                    sp.dma_start(bb[:, :, :], bb_d).then_inc(s["wg_in"], 16)
                    sp.dma_start(bc[:, :], bc_d).then_inc(s["wg_in"], 16)
                for e in range(EXPERTS):
                    sp.dma_start(wa[:, e, :], wa_d[e]).then_inc(s["wab_in"], 16)
                    sp.dma_start(wb[:, e, :], wb_d[e]).then_inc(s["wab_in"], 16)
                    sp.dma_start(wc[:, e, :, :], wc_d[e].rearrange("(f p) d -> p f d", p=P)).then_inc(s["wc_in"], 16)

            @block.tensor
            def _(pe):
                ln_tensor(pe, k, s, k.x)
                pe.wait_ge(s["wg_in"], 16 * WG_DMAS)
                for c in range(GROUP):
                    pe.wait_ge(s["xn_ready"], c + 1)
                    route_tensor_logits(pe, k, s, c, wg)
                for c in range(GROUP):
                    route_tensor_turn(pe, k, s, c)
                pe.wait_ge(s["wab_in"], 32 * EXPERTS)
                pe.wait_ge(s["wc_in"], 16 * EXPERTS)

                def up(i):
                    c, e, f = i // STEPS, i % STEPS // FT, i % FT
                    if i % STEPS == 0:
                        pe.wait_ge(s["gate_sb"], GROUP)
                    if f == 0:
                        if i >= 2 * FT:
                            pe.wait_ge(s["hid_sb"], i - FT)
                        pe.matmul(ps[:, 4 + (i // FT) % 2, :], k.ident[0:EXPERTS, e, None].to_broadcast([EXPERTS, P]),
                                  k.gate_t[:, c, :], start=True, stop=True)
                    if i >= 2:
                        pe.wait_ge(s["half_sb"], i - 1)
                    b = 2 * (i % 2)
                    pe.matmul(ps[:, b, :], wa[:, e, P * f:P * (f + 1)], k.xn[:, c, :], start=True, stop=True)
                    pe.matmul(ps[:, b + 1, :], wb[:, e, P * f:P * (f + 1)], k.xn[:, c, :], start=True,
                              stop=True).then_inc(s["hid_ps"], 1)

                def down(i):
                    c, e, f = i // STEPS, i % STEPS // FT, i % FT
                    if biased and i % STEPS == 0:
                        pe.matmul(ps[:, 6 + c, :], bc[:, :], k.gate_t[:, c, :], start=True, stop=False)
                    pe.wait_ge(s["hid_sb"], i + 1)
                    pe.matmul(ps[:, 6 + c, :], wc[:, e, f, :], hid[:, i % 2, :],
                              start=(not biased and i % STEPS == 0), stop=(i % STEPS == STEPS - 1)).then_inc(s["down_ps"], 1)

                up(0)
                for i in range(GROUP * STEPS):
                    if i + 1 < GROUP * STEPS:
                        up(i + 1)
                    down(i)

            @block.scalar
            def _(act):
                act.preload_act_table_set(EXPLN)
                ln_scalar(act, k, s)
                for c in range(GROUP):
                    route_scalar(act, k, s, c)
                for i in range(GROUP * STEPS):
                    e, f = i % STEPS // FT, i % FT
                    act.wait_ge(s["hid_ps"], i + 1)
                    if i >= 2:
                        act.wait_ge(s["hid_sb"], i - 1)
                    act.activation(sg[:, i % 2, :], ps[:, 2 * (i % 2), :], ACT.Silu,
                                   bias=(ba[:, e, f:f + 1] if biased else 0.0)).then_inc(s["silu_sb"], 1)

            @block.vector
            def _(dve):
                ln_vector(dve, k, s, k.x, k.xn)
                if biased:
                    dve.wait_ge(s["wg_in"], 16 * WG_DMAS)
                links = [0]
                for c in range(GROUP):
                    route_vector(dve, k, s, c, links, gb if biased else None)
                for i in range(GROUP * STEPS):
                    c, e, f = i // STEPS, i % STEPS // FT, i % FT
                    dve.wait_ge(s["silu_sb"], i + 1)
                    if biased:
                        dve.scalar_tensor_tensor(sg[:, i % 2, :], ps[:, 2 * (i % 2) + 1, :], bb[:, e, f:f + 1],
                                                 sg[:, i % 2, :], ALU.add, ALU.mult).then_inc(s["half_sb"], 1)
                    else:
                        dve.tensor_tensor(sg[:, i % 2, :], sg[:, i % 2, :], ps[:, 2 * (i % 2) + 1, :],
                                          ALU.mult).then_inc(s["half_sb"], 1)
                    dve.wait_ge(s["half_sb"], i + 1)
                    if i >= 2:
                        dve.wait_ge(s["down_ps"], i - 1)
                    dve.tensor_tensor(hid[:, i % 2, :], sg[:, i % 2, :], ps[:, 4 + (i // FT) % 2, :],
                                      ALU.mult).then_inc(s["hid_sb"], 1)
                    if i % STEPS == 0 and c > 0:
                        dve.wait_ge(s["down_ps"], c * STEPS)
                        dve.tensor_tensor(k.x[:, c - 1, :], k.x[:, c - 1, :], ps[:, 6 + c - 1, :], ALU.add).then_inc(s["x_new"], 1)
                dve.wait_ge(s["down_ps"], GROUP * STEPS)
                dve.tensor_tensor(k.x[:, GROUP - 1, :], k.x[:, GROUP - 1, :], ps[:, 6 + GROUP - 1, :], ALU.add).then_inc(s["x_new"], 1)


def stage_softmax(nc, k, w):
    H, PAIRS = 16, 8
    SCALE = 1.0 / (HD * HD * H)
    UNITS = GROUP * H * 2
    UPC = H * 2
    with ExitStack() as mem, Stage(nc, LN_SEMS + "wts ones_v q_ps k_ps q_sb k_sb v_ps v_act v_dve s_ps rowmax negmax exp_sb rowinv "
                                   "p_sb pt_ps pt_act pt_dve y_ps y_sb out_ps x_new") as s:
        sb = lambda n, sh: mem.enter_context(nc.sbuf_tensor(n, sh, F32))
        wq, wk, wv = [sb(n, [P, H * HD]) for n in ("s_wq", "s_wk", "s_wv")]
        wo = sb("s_wo", [P, PAIRS, P])
        q, kk = sb("s_q", [P, 2, S]), sb("s_k", [P, 2, S])
        v = sb("s_v", [P, NT, PAIRS, 3, HD])
        pr, pt = sb("s_p", [P, 2, 2, S]), sb("s_pt", [P, 2, NT, 2 * P])
        mx, nm, rs, ri = [sb(n, [P, 2, 2]) for n in ("s_mx", "s_nm", "s_rs", "s_ri")]
        o = sb("s_o", [P, PAIRS, S])
        ps = k.ps
        with nc.Block() as block:
            @block.sync
            def _(sp):
                for n, t in enumerate((wq, wk, wv)):
                    sp.dma_start(t[:, :].rearrange("p (h d) -> p h d", h=H),
                                 w["L1_attn_kernel"][n].rearrange("h m d -> m h d")).then_inc(s["wts"], 16)
                wo_v = w["L1_attn_WO"][0].rearrange("(d q j) m -> j d q m", q=PAIRS, j=2)
                for j in range(2):
                    sp.dma_start(wo[HD * j:HD * (j + 1), :, :], wo_v[j]).then_inc(s["wts"], 16)

            @block.gpsimd
            def _(pool):
                pool.memset(v[:, :, :, 1, :], 1.0).then_inc(s["ones_v"], 1)
                for n in range(UNITS):
                    pool.wait_ge(s["rowinv"], n + 1)
                    for r in range(2):
                        ins = pool.tensor_scalar(pr[:, n % 2, r, :], pr[:, n % 2, r, :], ri[:, n % 2, r:r + 1], None, ALU.mult)
                    ins.then_inc(s["p_sb"], 1)

            @block.tensor
            def _(pe):
                ln_tensor(pe, k, s, k.x)
                pe.wait_ge(s["wts"], 80)
                pe.wait_ge(s["ones_v"], 1)
                for c in range(GROUP):
                    pe.wait_ge(s["xn_ready"], c + 1)

                def project(g, what):
                    c, p = g // PAIRS, g % PAIRS
                    if what == "q":
                        if g > 0:
                            pe.wait_ge(s["k_sb"], g)
                        pe.matmul(ps[:, 7, :], wq[:, P * p:P * (p + 1)], k.xn[:, c, :], start=True, stop=True).then_inc(s["q_ps"], 1)
                    else:
                        pe.wait_ge(s["q_sb"], g + 1)
                        pe.matmul(ps[:, 7, :], wk[:, P * p:P * (p + 1)], k.xn[:, c, :], start=True, stop=True).then_inc(s["k_ps"], 1)

                def values_in(c):
                    for n in range(2 * NT):
                        if n < 2:
                            if c > 0:
                                pe.wait_ge(s["y_sb"], c * UPC)
                                pe.wait_ge(s["k_sb"], min(c * PAIRS + 1, GROUP * PAIRS))
                            else:
                                pe.wait_ge(s["k_sb"], 1)
                        else:
                            pe.wait_ge(s["v_dve"] if n % 2 else s["v_act"], c * NT + (n - 2) // 2 + 1)
                        t, half = n // 2, n % 2
                        pe.matmul(ps[:, 6 + half, :], k.xn[:, c, P * t:P * (t + 1)], wv[:, 512 * half:512 * half + 512],
                                  start=True, stop=True).then_inc(s["v_ps"], 1)

                def scores(n):
                    g, j, u = n // 4, n // 2 % 2, n % 2
                    if n % 4 == 0:
                        pe.wait_ge(s["q_sb"], g + 1)
                        pe.wait_ge(s["k_sb"], g + 1)
                    if n >= 2:
                        pe.wait_ge(s["exp_sb"], 2 * (n - 1))
                    for r in range(2):
                        tile = 2 * u + r
                        mm = pe.matmul(ps[:, 2 * (n % 2) + r, :], q[HD * j:HD * (j + 1), g % 2, P * tile:P * (tile + 1)],
                                       kk[HD * j:HD * (j + 1), g % 2, :], start=True, stop=True)
                    mm.then_inc(s["s_ps"], 1)

                def turn(n):
                    pe.wait_ge(s["p_sb"], n + 1)
                    if n >= 1:
                        pe.wait_ge(s["pt_act"], n)
                        pe.wait_ge(s["pt_dve"], n)
                    for t in range(NT):
                        for r in range(2):
                            mm = pe.transpose(ps[:, 4 + t // 2, 2 * P * (t % 2) + P * r:2 * P * (t % 2) + P * (r + 1)],
                                              pr[:, n % 2, r, P * t:P * (t + 1)], k.ident[:, :])
                    mm.then_inc(s["pt_ps"], 1)

                def outputs(n):
                    c, h = n // UPC, n // 2 % H
                    if n % UPC == 0:
                        values_in(c)
                        pe.wait_ge(s["v_act"], (c + 1) * NT)
                        pe.wait_ge(s["v_dve"], (c + 1) * NT)
                    pe.wait_ge(s["pt_act"], n + 1)
                    pe.wait_ge(s["pt_dve"], n + 1)
                    if n >= 2:
                        pe.wait_ge(s["y_sb"], n - 1)
                    for t in range(NT):
                        mm = pe.matmul(ps[:, 6, 2 * P * (n % 2):2 * P * (n % 2 + 1)], v[:, t, h // 2, h % 2:h % 2 + 2, :],
                                       pt[:, n % 2, t, :], start=(t == 0), stop=(t == NT - 1))
                    mm.then_inc(s["y_ps"], 1)

                def project_out(c):
                    pe.wait_ge(s["y_sb"], (c + 1) * UPC)
                    for p in range(PAIRS):
                        mm = pe.matmul(ps[:, 6, :], wo[:, p, :], o[:, p, :], start=(p == 0), stop=(p == PAIRS - 1))
                    mm.then_inc(s["out_ps"], 1)
                    pe.wait_ge(s["x_new"], c + 1)

                project(0, "q")
                project(0, "k")
                scores(0)
                scores(1)
                for n in range(UNITS):
                    if n % 4 == 0 and n // 4 + 1 < GROUP * PAIRS and n % UPC:
                        project(n // 4 + 1, "q")
                    if n % 4 == 1 and n // 4 + 1 < GROUP * PAIRS:
                        if n % UPC == 1:
                            project(n // 4 + 1, "q")
                        project(n // 4 + 1, "k")
                    turn(n)
                    if n + 2 < UNITS:
                        scores(n + 2)
                    outputs(n)
                    if n % UPC == UPC - 1:
                        project_out(n // UPC)

            @block.scalar
            def _(act):
                act.preload_act_table_set(EXPLN)
                ln_scalar(act, k, s)

                def q_out(g):
                    act.wait_ge(s["q_ps"], g + 1)
                    act.activation(q[:, g % 2, :], ps[:, 7, :], ACT.Copy).then_inc(s["q_sb"], 1)

                def exps(n):
                    act.wait_ge(s["negmax"], n + 1)
                    if n >= 2:
                        act.wait_ge(s["pt_ps"], n - 1)
                    for r in range(2):
                        act.activation(pr[:, n % 2, r, :], ps[:, 2 * (n % 2) + r, :], ACT.Exp, bias=nm[:, n % 2, r:r + 1],
                                       scale=SCALE, accum_out=rs[:, n % 2, r:r + 1]).then_inc(s["exp_sb"], 1)

                q_out(0)
                exps(0)
                for n in range(UNITS):
                    if n + 1 < UNITS:
                        exps(n + 1)
                    if n % 4 == 0 and n // 4 + 1 < GROUP * PAIRS and n % UPC:
                        q_out(n // 4 + 1)
                    if n % UPC == 1 and n // 4 + 1 < GROUP * PAIRS:
                        q_out(n // 4 + 1)
                    act.wait_ge(s["pt_ps"], n + 1)
                    if n >= 2:
                        act.wait_ge(s["y_ps"], n - 1)
                    act.activation(flat(pt[:, n % 2, 0:2, :]), ps[:, 4, :], ACT.Copy).then_inc(s["pt_act"], 1)
                    if n % UPC == 0:
                        for t in range(NT):
                            act.wait_ge(s["v_ps"], n // UPC * 2 * NT + 2 * t + 1)
                            act.activation(v[:, t, 0:4, 0:3:2, :], ps[:, 6, :].rearrange("p (a b e) -> p a b e", b=2, e=HD),
                                           ACT.Copy).then_inc(s["v_act"], 1)

            @block.vector
            def _(dve):
                ln_vector(dve, k, s, k.x, k.xn)

                def k_out(g):
                    dve.wait_ge(s["k_ps"], g + 1)
                    dve.tensor_copy(kk[:, g % 2, :], ps[:, 7, :]).then_inc(s["k_sb"], 1)

                def row_max(n):
                    dve.wait_ge(s["s_ps"], n + 1)
                    if n >= 2:
                        dve.wait_ge(s["exp_sb"], 2 * (n - 1))
                    dve.tensor_reduce(mx[:, n % 2, :], ps[:, 2 * (n % 2):2 * (n % 2) + 2, :], AX.X, ALU.max).then_inc(s["rowmax"], 1)
                    dve.wait_ge(s["rowmax"], n + 1)
                    dve.tensor_scalar(nm[:, n % 2, :], mx[:, n % 2, :], -SCALE, None, ALU.mult).then_inc(s["negmax"], 1)

                def row_inv(n):
                    dve.wait_ge(s["exp_sb"], 2 * (n + 1))
                    if n >= 2:
                        dve.wait_ge(s["p_sb"], n - 1)
                    dve.reciprocal(ri[:, n % 2, :], rs[:, n % 2, :]).then_inc(s["rowinv"], 1)

                k_out(0)
                row_max(0)
                row_inv(0)
                row_max(1)
                for n in range(UNITS):
                    if n + 1 < UNITS:
                        row_inv(n + 1)
                    if n % 4 == 1 and n // 4 + 1 < GROUP * PAIRS:
                        k_out(n // 4 + 1)
                    dve.wait_ge(s["pt_ps"], n + 1)
                    if n >= 2:
                        dve.wait_ge(s["y_ps"], n - 1)
                    dve.tensor_copy(flat(pt[:, n % 2, 2:4, :]), ps[:, 5, :]).then_inc(s["pt_dve"], 1)
                    if n + 2 < UNITS:
                        row_max(n + 2)
                    if n % UPC == 0:
                        for t in range(NT):
                            dve.wait_ge(s["v_ps"], n // UPC * 2 * NT + 2 * t + 2)
                            dve.tensor_copy(v[:, t, 4:8, 0:3:2, :], ps[:, 7, :].rearrange("p (a b e) -> p a b e", b=2, e=HD))\
                               .then_inc(s["v_dve"], 1)
                    h, u = n // 2 % H, n % 2
                    r = HD * (h % 2)
                    dve.wait_ge(s["y_ps"], n + 1)
                    dve.tensor_copy(o[r:r + HD, h // 2, 2 * P * u:2 * P * (u + 1)], ps[r:r + HD, 6, 2 * P * u:2 * P * (u + 1)])\
                       .then_inc(s["y_sb"], 1)
                    if n % UPC == UPC - 1:
                        c = n // UPC
                        dve.wait_ge(s["out_ps"], c + 1)
                        dve.tensor_tensor(k.x[:, c, :], k.x[:, c, :], ps[:, 6, :], ALU.add).then_inc(s["x_new"], 1)


def stage_local(nc, k, w, wl, layer):
    HPAIRS = LH // 2
    BACK = WIN
    KW = P + BACK
    QK_SCALE = 8.0
    TILES = 2 * HPAIRS
    last = layer == 1
    with ExitStack() as mem, Stage(nc, (LN_SEMS if layer == 0 else "ln_mean ln_xc ln_sq ln_var ln_log ln_rstd xn_ready ") +
                                   "padded masked_rdy folded shifted v_ps v_act v_dve qk_ps sq_sb cos_sb sin_sb raw_sb norm_ps ss_sb "
                                   "root_sb rn_sb bc_ps qk_sb s_ps s_sb rowmax centred exp_sb rowsum rowinv p_sb pt_ps pta_sb ptb_sb "
                                   "o_ps o_sb out_ps y_new shifted2 hn_pre hn_sb up_ps gelu_sb hid_sb down_ps y_end x_new") as s:
        sb = lambda n, sh: mem.enter_context(nc.sbuf_tensor(n + str(layer), sh, F32))
        hs = sb("c_hs", [P, GROUP, BACK + S])
        v = sb("c_v", [P, NT + 1, HPAIRS, 3, LD])
        qq, kp = sb("c_q", [P, HPAIRS, S]), sb("c_k", [P, HPAIRS, BACK + S])
        raw = sb("c_raw", [P, TILES, S])
        sq, sinp = sb("c_sq", [P, 2, S]), sb("c_sin", [P, 2, S])
        rn = sb("c_rn", [2 * TILES, 2, S])
        tab = sb("c_tab", [P, 4, S])
        mask = sb("c_mask", [P, NT, KW])
        sc = sb("c_s", [P, 2, NT, KW])
        mx, su = sb("c_mx", [P, 2, NT]), sb("c_su", [P, 2, NT])
        pta, ptb = sb("c_pta", [P, 2, S]), sb("c_ptb", [BACK, 2, S])
        o = sb("c_o", [P, HPAIRS, S])
        hn, ge, hid = sb("c_hn", [P, GROUP, S]), sb("c_ge", [P, 2, S]), sb("c_hid", [P, 3, S])
        ps, y = k.ps, k.y
        with nc.Block() as block:
            @block.gpsimd
            def _(pool):
                pool.memset(hs[:, :, :], 0.0).then_inc(s["padded"], 1)
                pool.memset(kp[:, :, :], 0.0).then_inc(s["padded"], 1)
                pool.memset(v[:, NT, :, :, :], 0.0).then_inc(s["padded"], 1)
                pool.memset(v[:, 0:NT, :, 1, :], 1.0).then_inc(s["padded"], 1)
                pool.memset(mask[:, :, :], 0.0).then_inc(s["padded"], 1)
                pool.wait_ge(s["padded"], 5)
                pool.affine_select(out=mask[:, :, :], in_=mask[:, :, :], compare_op=ALU.is_ge, fill=-1e30, base=0,
                                   pattern=[[0, NT], [1, KW]], channel_multiplier=-1).then_inc(s["masked_rdy"], 1)
                pool.wait_ge(s["masked_rdy"], 1)
                pool.affine_select(out=mask[:, :, :], in_=mask[:, :, :], compare_op=ALU.is_ge, fill=-1e30, base=WIN,
                                   pattern=[[0, NT], [-1, KW]], channel_multiplier=1).then_inc(s["masked_rdy"], 1)
                pool.wait_ge(s["masked_rdy"], 2)
                pool.affine_select(out=mask[:, 0, :], in_=mask[:, 0, :], compare_op=ALU.is_ge, fill=-1e30, base=-BACK,
                                   pattern=[[1, KW]], channel_multiplier=0).then_inc(s["masked_rdy"], 1)
                for n in range(4):
                    pool.tensor_scalar(tab[:, n, :], k.rot[:, n, :], wl.scales[:, n:n + 1], None, ALU.mult).then_inc(s["folded"], 1)

                pool.wait_ge(s["folded"], 4)
                for c in range(GROUP):
                    if layer == 0:
                        pool.wait_ge(s["xn_ready"], c + 1)
                    pool.tensor_copy(hs[0:64, c, BACK:BACK + S], y[0:64, c, :]).then_inc(s["shifted"], 1)
                    pool.wait_ge(s["shifted"], 2 * c + 1)
                    pool.tensor_copy(hs[64:P, c, BACK + 1:BACK + S], y[64:P, c, 0:S - 1]).then_inc(s["shifted"], 1)
                    pool.wait_ge(s["shifted"], 2 * c + 2)
                for c in range(GROUP):
                    for m in range(TILES):
                        i = c * TILES + m
                        pool.wait_ge(s["sin_sb"], i + 1)
                        if m == 0 and c > 0:
                            pool.wait_ge(s["qk_sb"], c * TILES)
                        pool.tensor_tensor(raw[:, m, :], raw[:, m, :], sinp[:, i % 2, :], ALU.add).then_inc(s["raw_sb"], 1)
                    for h in range(LH):
                        i = c * LH + h
                        pool.wait_ge(s["rowmax"], i + 1)
                        pool.tensor_tensor(sc[:, i % 2, :, :], sc[:, i % 2, :, :],
                                           mx[:, i % 2, :, None].to_broadcast([P, NT, KW]), ALU.subtract).then_inc(s["centred"], 1)
                        pool.wait_ge(s["rowinv"], i + 1)
                        pool.tensor_tensor(sc[:, i % 2, :, :], sc[:, i % 2, :, :],
                                           su[:, i % 2, :, None].to_broadcast([P, NT, KW]), ALU.mult).then_inc(s["p_sb"], 1)
                    pool.wait_ge(s["y_new"], c + 1)
                    pool.wait_ge(s["p_sb"], (c + 1) * LH)
                    pool.tensor_copy(hs[0:64, c, BACK:BACK + S], y[0:64, c, :]).then_inc(s["shifted2"], 1)
                    pool.wait_ge(s["shifted2"], 2 * c + 1)
                    pool.tensor_copy(hs[64:P, c, BACK + 1:BACK + S], y[64:P, c, 0:S - 1]).then_inc(s["shifted2"], 1)
                    pool.wait_ge(s["shifted2"], 2 * c + 2)

            @block.tensor
            def _(pe):
                if layer == 0:
                    ln_tensor(pe, k, s, k.x)
                pe.wait_ge(s["padded"], 5)
                pe.wait_ge(k.w_local, wl.dmas)
                for c in range(GROUP):
                    pe.wait_ge(s["shifted"], 2 * (c + 1))
                    if c > 0:
                        pe.wait_ge(s["y_new"], c)
                    for t in range(NT + 1):
                        rows = P if t < NT else BACK
                        pe.matmul(ps[0:rows, t, :], hs[:, c, P * t:P * t + rows], wl.v[:, :], start=True, stop=True).then_inc(s["v_ps"], 1)
                    for m in range(TILES):
                        i = c * TILES + m
                        if m == 0:
                            pe.wait_ge(s["v_act"], (c + 1) * 3)
                            pe.wait_ge(s["v_dve"], (c + 1) * 2)
                        if m >= 2:
                            pe.wait_ge(s["sin_sb"], i - 1)
                            pe.wait_ge(s["sq_sb"], i - 1)
                        b = 2 * (m % 2)
                        pe.matmul(ps[:, b, :], wl.qk[:, P * m:P * (m + 1)], hs[:, c, BACK:BACK + S], start=True, stop=True)
                        pe.matmul(ps[:, b + 1, :], wl.qkr[:, P * m:P * (m + 1)], hs[:, c, BACK:BACK + S], start=True,
                                  stop=True).then_inc(s["qk_ps"], 1)
                        if m >= 1:
                            pe.wait_ge(s["sq_sb"], i)
                            pe.matmul(ps[0:2 * TILES, 5, :], k.head_sel[:, m - 1, :], sq[:, (i - 1) % 2, :], start=(m == 1),
                                      stop=False).then_inc(s["norm_ps"], 1)
                    i = (c + 1) * TILES - 1
                    pe.wait_ge(s["sq_sb"], i + 1)
                    pe.matmul(ps[0:2 * TILES, 5, :], k.head_sel[:, TILES - 1, :], sq[:, i % 2, :], start=False,
                              stop=True).then_inc(s["norm_ps"], 1)
                    pe.wait_ge(s["rn_sb"], c + 1)
                    for m in range(TILES):
                        i = c * TILES + m
                        if m >= 2:
                            pe.wait_ge(s["qk_sb"], i - 1)
                        pe.matmul(ps[:, 6 + m % 2, :], k.head_sel_t[:, m, :], rn[:, 1, :], start=True, stop=True).then_inc(s["bc_ps"], 1)
                    pe.wait_ge(s["qk_sb"], (c + 1) * TILES)

                    def scores(h):
                        i = c * LH + h
                        m, r = h // 2, LD * (h % 2)
                        if h >= 2:
                            pe.wait_ge(s["s_sb"], i - 1)
                        for t in range(NT):
                            mm = pe.matmul(ps[:, 2 * (i % 2) + t // 2, KW * (t % 2):KW * (t % 2 + 1)],
                                           qq[r:r + LD, m, P * t:P * (t + 1)], kp[r:r + LD, m, P * t:P * t + KW],
                                           start=True, stop=True)
                        mm.then_inc(s["s_ps"], 1)

                    scores(0)
                    for h in range(LH):
                        i = c * LH + h
                        if h + 1 < LH:
                            scores(h + 1)
                        pe.wait_ge(s["p_sb"], i + 1)
                        if h >= 1:
                            pe.wait_ge(s["pta_sb"], i)
                            pe.wait_ge(s["ptb_sb"], i)
                        for t in range(NT):
                            pe.transpose(ps[:, 4, P * t:P * (t + 1)], sc[:, i % 2, t, 0:P], k.ident[:, :])
                            mm = pe.transpose(ps[0:BACK, 5, P * t:P * (t + 1)], sc[:, i % 2, t, P:KW], k.ident[:, :])
                        mm.then_inc(s["pt_ps"], 1)
                        pe.wait_ge(s["pta_sb"], i + 1)
                        pe.wait_ge(s["ptb_sb"], i + 1)
                        if h >= 2:
                            pe.wait_ge(s["o_sb"], i - 1)
                        for t in range(NT):
                            vv = v[:, t, h // 2, h % 2:h % 2 + 2, :]
                            pe.matmul(ps[:, 6 + i % 2, P * t:P * (t + 1)], vv, pta[:, i % 2, P * t:P * (t + 1)], start=True, stop=False)
                            mm = pe.matmul(ps[:, 6 + i % 2, P * t:P * (t + 1)], v[0:BACK, t + 1, h // 2, h % 2:h % 2 + 2, :],
                                           ptb[:, i % 2, P * t:P * (t + 1)], start=False, stop=True)
                        mm.then_inc(s["o_ps"], 1)
                    pe.wait_ge(s["o_sb"], (c + 1) * LH)
                    for p in range(HPAIRS):
                        mm = pe.matmul(ps[:, 0, :], wl.o[:, p, :], o[:, p, :], start=(p == 0), stop=(p == HPAIRS - 1))
                    mm.then_inc(s["out_ps"], 1)
                base = GROUP if layer == 0 else 0
                for c in range(GROUP):
                    pe.wait_ge(s["shifted2"], 2 * (c + 1))
                    pe.matmul(ps[:, 6 + c, :], k.mean_mat[:, :], hs[:, c, BACK:BACK + S], start=True, stop=True).then_inc(s["ln_mean"], 1)
                for c in range(GROUP):
                    pe.wait_ge(s["ln_sq"], base + c + 1)
                    pe.matmul(ps[:, 6 + c, :], k.mean_mat[:, :], k.sq[:, c, :], start=True, stop=True).then_inc(s["ln_var"], 1)
                for c in range(GROUP):
                    pe.wait_ge(s["hn_sb"], c + 1)
                    for f, (off, n) in enumerate(HT):
                        i = c * 3 + f
                        if c == 0 and f == 0:
                            pe.wait_ge(s["y_new"], GROUP)
                        if i >= 2:
                            pe.wait_ge(s["hid_sb"], i - 1)
                        b = 2 * (i % 2)
                        pe.matmul(ps[0:n, b, :], wl.up[:, off:off + n], hn[:, c, :], start=True, stop=True)
                        pe.matmul(ps[0:n, b + 1, :], wl.up[:, HID + off:HID + off + n], hn[:, c, :], start=True,
                                  stop=True).then_inc(s["up_ps"], 1)
                    for f, (off, n) in enumerate(HT):
                        pe.wait_ge(s["hid_sb"], c * 3 + f + 1)
                        mm = pe.matmul(ps[:, 4 + c, :], wl.down[0:n, f, :], hid[0:n, f, :], start=(f == 0), stop=(f == 2))
                    mm.then_inc(s["down_ps"], 1)

            @block.scalar
            def _(act):
                act.preload_act_table_set(EXPLN)
                if layer == 0:
                    ln_scalar(act, k, s)
                for c in range(GROUP):
                    for n in range(0, NT + 1, 2):
                        rows = P if n < NT else BACK
                        act.wait_ge(s["v_ps"], c * (NT + 1) + n + 1)
                        act.activation(v[0:rows, n, :, 0:3:2, :], ps[0:rows, n, :].rearrange("p (a b e) -> p a b e", b=2, e=LD),
                                       ACT.Copy).then_inc(s["v_act"], 1)
                    for m in range(TILES):
                        i = c * TILES + m
                        act.wait_ge(s["cos_sb"], i + 1)
                        if i >= 2:
                            act.wait_ge(s["norm_ps"], i - 1)
                        act.activation(sq[:, i % 2, :], ps[:, 2 * (m % 2), :], ACT.Square).then_inc(s["sq_sb"], 1)
                    act.wait_ge(s["ss_sb"], c + 1)
                    act.activation(rn[:, 0, :], rn[:, 0, :], ACT.Sqrt).then_inc(s["root_sb"], 1)
                    for h in range(LH):
                        i = c * LH + h
                        act.wait_ge(s["centred"], i + 1)
                        act.activation(sc[:, i % 2, :, :], sc[:, i % 2, :, :], ACT.Exp, scale=QK_SCALE).then_inc(s["exp_sb"], 1)
                        act.wait_ge(s["pt_ps"], i + 1)
                        act.activation(pta[:, i % 2, :], ps[:, 4, :], ACT.Copy).then_inc(s["pta_sb"], 1)
                base = GROUP if layer == 0 else 0
                for c in range(GROUP):
                    act.wait_ge(s["ln_xc"], base + c + 1)
                    act.activation(k.sq[:, c, :], k.xc[:, c, :], ACT.Square).then_inc(s["ln_sq"], 1)
                for c in range(GROUP):
                    act.wait_ge(s["ln_var"], base + c + 1)
                    act.activation(k.sq[:, c, :], ps[:, 6 + c, :], ACT.Ln, bias=k.eps[:, 0:1]).then_inc(s["ln_log"], 1)
                    act.wait_ge(s["ln_log"], base + c + 1)
                    act.activation(k.sq[:, c, :], k.sq[:, c, :], ACT.Exp, scale=-0.5).then_inc(s["ln_rstd"], 1)
                for i in range(3 * GROUP):
                    f = i % 3
                    n = HT[f][1]
                    act.wait_ge(s["up_ps"], i + 1)
                    if i >= 2:
                        act.wait_ge(s["hid_sb"], i - 1)
                    act.activation(ge[0:n, i % 2, :], ps[0:n, 2 * (i % 2) + 1, :], ACT.Gelu,
                                   bias=wl.b1[0:n, 3 + f:4 + f]).then_inc(s["gelu_sb"], 1)

            @block.vector
            def _(dve):
                if layer == 0:
                    ln_vector(dve, k, s, k.x, y)
                dve.wait_ge(s["padded"], 5)
                for c in range(GROUP):
                    for n in range(1, NT + 1, 2):
                        dve.wait_ge(s["v_ps"], c * (NT + 1) + n + 1)
                        dve.tensor_copy(v[:, n, :, 0:3:2, :], ps[:, n, :].rearrange("p (a b e) -> p a b e", b=2, e=LD))\
                           .then_inc(s["v_dve"], 1)
                    for m in range(TILES):
                        i = c * TILES + m
                        dve.wait_ge(s["qk_ps"], i + 1)
                        if m == 0:
                            dve.wait_ge(s["folded"], 4)
                        if i >= 2:
                            dve.wait_ge(s["raw_sb"], i - 1)
                        kind = 2 * (m >= HPAIRS)
                        dve.tensor_tensor(raw[:, m, :], ps[:, 2 * (m % 2), :], tab[:, kind, :], ALU.mult).then_inc(s["cos_sb"], 1)
                        dve.tensor_tensor(sinp[:, i % 2, :], ps[:, 2 * (m % 2) + 1, :], tab[:, kind + 1, :], ALU.mult)\
                           .then_inc(s["sin_sb"], 1)
                    dve.wait_ge(s["norm_ps"], (c + 1) * TILES)
                    dve.tensor_scalar(rn[:, 0, :], ps[0:2 * TILES, 5, :], 1e-24, None, ALU.max).then_inc(s["ss_sb"], 1)
                    dve.wait_ge(s["root_sb"], c + 1)
                    dve.reciprocal(rn[:, 1, :], rn[:, 0, :]).then_inc(s["rn_sb"], 1)
                    for m in range(TILES):
                        i = c * TILES + m
                        dve.wait_ge(s["bc_ps"], i + 1)
                        dve.wait_ge(s["raw_sb"], i + 1)
                        dst = qq[:, m, :] if m < HPAIRS else kp[:, m - HPAIRS, BACK:BACK + S]
                        dve.tensor_tensor(dst, raw[:, m, :], ps[:, 6 + m % 2, :], ALU.mult).then_inc(s["qk_sb"], 1)
                    if c == 0:
                        dve.wait_ge(s["masked_rdy"], 3)

                    def mask_max(h):
                        i = c * LH + h
                        dve.wait_ge(s["s_ps"], i + 1)
                        if i >= 2:
                            dve.wait_ge(s["pt_ps"], i - 1)
                        dve.tensor_tensor(sc[:, i % 2, :, :].rearrange("p (a b) k -> p a b k", b=2),
                                          ps[:, 2 * (i % 2):2 * (i % 2) + 2, 0:2 * KW].rearrange("p a (b k) -> p a b k", b=2),
                                          mask[:, :, :].rearrange("p (a b) k -> p a b k", b=2), ALU.add).then_inc(s["s_sb"], 1)
                        dve.wait_ge(s["s_sb"], i + 1)
                        dve.tensor_reduce(mx[:, i % 2, :], sc[:, i % 2, :, :], AX.X, ALU.max).then_inc(s["rowmax"], 1)

                    mask_max(0)
                    for h in range(LH):
                        i = c * LH + h
                        if h + 1 < LH:
                            mask_max(h + 1)
                        dve.wait_ge(s["exp_sb"], i + 1)
                        dve.tensor_reduce(su[:, i % 2, :], sc[:, i % 2, :, :], AX.X, ALU.add).then_inc(s["rowsum"], 1)
                        dve.wait_ge(s["rowsum"], i + 1)
                        dve.reciprocal(su[:, i % 2, :], su[:, i % 2, :]).then_inc(s["rowinv"], 1)
                        dve.wait_ge(s["pt_ps"], i + 1)
                        dve.tensor_copy(ptb[:, i % 2, :], ps[0:BACK, 5, :]).then_inc(s["ptb_sb"], 1)
                        dve.wait_ge(s["o_ps"], i + 1)
                        r = LD * (h % 2)
                        dve.tensor_copy(o[r:r + LD, h // 2, :], ps[r:r + LD, 6 + i % 2, :]).then_inc(s["o_sb"], 1)
                    dve.wait_ge(s["out_ps"], c + 1)
                    dve.tensor_tensor(y[:, c, :], y[:, c, :], ps[:, 0, :], ALU.add).then_inc(s["y_new"], 1)
                base = GROUP if layer == 0 else 0
                for c in range(GROUP):
                    dve.wait_ge(s["ln_mean"], base + c + 1)
                    dve.tensor_tensor(k.xc[:, c, :], hs[:, c, BACK:BACK + S], ps[:, 6 + c, :], ALU.subtract).then_inc(s["ln_xc"], 1)
                for c in range(GROUP):
                    dve.wait_ge(s["ln_rstd"], base + c + 1)
                    dve.tensor_tensor(k.xc[:, c, :], k.xc[:, c, :], k.sq[:, c, :], ALU.mult).then_inc(s["hn_pre"], 1)
                    dve.wait_ge(s["hn_pre"], c + 1)
                    dve.tensor_scalar(hn[:, c, :], k.xc[:, c, :], wl.ln[:, 0:1], wl.ln[:, 1:2], ALU.mult, ALU.add).then_inc(s["hn_sb"], 1)
                for c in range(GROUP):
                    for f, (off, n) in enumerate(HT):
                        i = c * 3 + f
                        dve.wait_ge(s["gelu_sb"], i + 1)
                        if f == 0 and c > 0:
                            dve.wait_ge(s["down_ps"], c)
                        dve.scalar_tensor_tensor(hid[0:n, f, :], ps[0:n, 2 * (i % 2), :], wl.b1[0:n, f:f + 1], ge[0:n, i % 2, :],
                                                 ALU.add, ALU.mult).then_inc(s["hid_sb"], 1)
                    dve.wait_ge(s["down_ps"], c + 1)
                    dve.scalar_tensor_tensor(y[:, c, :], ps[:, 4 + c, :], wl.ln[:, 2:3], y[:, c, :], ALU.add, ALU.add)\
                       .then_inc(s["y_end"], 1)
                    if last:
                        dve.wait_ge(s["y_end"], c + 1)
                        dve.tensor_tensor(k.x[:, c, :], k.x[:, c, :], y[:, c, :], ALU.add).then_inc(s["x_new"], 1)


def stage_ln_y(nc, k):
    with Stage(nc, LN_SEMS) as s:
        with nc.Block() as block:
            @block.tensor
            def _(pe):
                ln_tensor(pe, k, s, k.x)

            @block.scalar
            def _(act):
                act.preload_act_table_set(EXPLN)
                ln_scalar(act, k, s)

            @block.vector
            def _(dve):
                ln_vector(dve, k, s, k.x, k.y)


def stage_mamba(nc, k, w, mw):
    UNITS = (NS // NGR) * ET
    with ExitStack() as mem, Stage(nc, "rms_sq rms_ps rms_log rms_rstd u_sb xz_ps xs_sb tap0 tap_sb z_sb xc_sb dbc_ps dbc_sb dt_ps dt_abs "
                                   "dt_exp dt_log dt_relu delta_sb dx_sb bcast_ps b_sb c_sb da_sb zero_col bx_sb h_sb hc_sb y_ps "
                                   "y_skip yg_sb out_ps y_new") as s:
        sb = lambda n, sh: mem.enter_context(nc.sbuf_tensor(n, sh, F32))
        PADT = TAPS - 1
        xs = sb("m_xs", [P, GROUP, ET, PADT + S])
        cv, xc = sb("m_cv", [P, GROUP, ET, S]), sb("m_xc", [P, GROUP, ET, S])
        zg = sb("m_zg", [P, GROUP, ET, S])
        dbc = sb("m_dbc", [RANK + 2 * NS, GROUP, S])
        dl, dx = sb("m_dl", [P, GROUP, ET, S]), sb("m_dx", [P, GROUP, ET, S])
        rl = sb("m_rl", [P, ET, S])
        bb, cc = sb("m_bb", [P, 2, NGR, S]), sb("m_cc", [P, 2, NGR, S])
        da, bx, hh = [sb(n, [P, 2, NGR, S]) for n in ("m_da", "m_bx", "m_h")]
        yg = sb("m_yg", [P, ET, S])
        ps, y = k.ps, k.y
        NG4 = NS // NGR
        with nc.Block() as block:
            @block.gpsimd
            def _(pool):
                pool.memset(xs[:, :, :, 0:PADT], 0.0).then_inc(s["zero_col"], 1)
                pool.memset(da[:, :, :, 0:1], 0.0).then_inc(s["zero_col"], 1)
                for u in range(GROUP * UNITS):
                    c, ng, e = u // UNITS, u % UNITS // ET, u % ET
                    if u % UNITS == 0:
                        pool.wait_ge(s["dx_sb"], (c + 1) * ET)
                    pool.wait_ge(s["b_sb"], (c * NG4 + ng + 1) * NGR)
                    if u >= 2:
                        pool.wait_ge(s["h_sb"], u - 1)
                    pool.tensor_tensor(bx[:, u % 2, :, :], bb[:, (c * NG4 + ng) % 2, :, :],
                                       dx[:, c, e, None, :].to_broadcast([P, NGR, S]), ALU.mult).then_inc(s["bx_sb"], 1)

            @block.tensor
            def _(pe):
                for c in range(GROUP):
                    pe.wait_ge(s["rms_sq"], c + 1)
                    pe.matmul(ps[:, 6 + c, :], k.mean_mat[:, :], k.sq[:, c, :], start=True, stop=True).then_inc(s["rms_ps"], 1)
                for c in range(GROUP):
                    pe.wait_ge(s["u_sb"], c + 1)
                    if c == 1:
                        pe.wait_ge(s["rms_log"], GROUP)
                    for m in range(2 * ET):
                        pe.matmul(ps[:, 2 * c + m % 2 + 4 * (m // 2), :], mw.win[:, P * m:P * (m + 1)], k.xn[:, c, :],
                                  start=True, stop=True).then_inc(s["xz_ps"], 1)
                for c in range(GROUP):
                    pe.wait_ge(s["xc_sb"], (c + 1) * ET)
                    pe.wait_ge(s["xs_sb"], (c + 1) * ET)
                    for e in range(ET):
                        mm = pe.matmul(ps[0:RANK + 2 * NS, 2 * c, :], mw.wx[:, e, :], xc[:, c, e, :], start=(e == 0), stop=(e == ET - 1))
                    mm.then_inc(s["dbc_ps"], 1)
                pe.wait_ge(s["z_sb"], GROUP * ET)
                for c in range(GROUP):
                    pe.wait_ge(s["dbc_sb"], c + 1)
                    for e in range(ET):
                        pe.matmul(ps[:, 4 + 2 * c + e, :], mw.wdt[:, P * e:P * (e + 1)], dbc[0:RANK, c, :],
                                  start=True, stop=True).then_inc(s["dt_ps"], 1)

                def broadcast(c, ng):
                    for r in range(2 * NGR):
                        i = (c * NG4 + ng) * 2 * NGR + r
                        if i >= 4:
                            pe.wait_ge(s["c_sb"] if r % 2 else s["b_sb"], (i - 4) // 2 + 1)
                        row = RANK + NS * (r % 2) + NGR * ng + r // 2
                        pe.matmul(ps[:, i % 4, :], k.ident[RANK:RANK + 2 * NS, row, None].to_broadcast([2 * NS, P]),
                                  dbc[RANK:RANK + 2 * NS, c, :], start=True, stop=True).then_inc(s["bcast_ps"], 1)

                def reduce(u):
                    c, ng, e = u // UNITS, u % UNITS // ET, u % ET
                    pe.wait_ge(s["hc_sb"], u + 1)
                    for n in range(NGR):
                        mm = pe.matmul(ps[:, 4 + e, :], k.ident[:, :], hh[:, u % 2, n, :], start=(ng == 0 and n == 0),
                                       stop=(ng == NG4 - 1 and n == NGR - 1))
                    mm.then_inc(s["y_ps"], 1)

                pe.wait_ge(s["dbc_sb"], GROUP)
                broadcast(0, 0)
                for c in range(GROUP):
                    for ng in range(NG4):
                        nxt = c * NG4 + ng + 1
                        if nxt < GROUP * NG4:
                            broadcast(nxt // NG4, nxt % NG4)
                        if c == 0 and ng == 0:
                            pe.wait_ge(s["delta_sb"], GROUP * ET)
                        if c > 0 and ng == 0:
                            pe.wait_ge(s["yg_sb"], c * ET)
                        for e in range(ET):
                            reduce((c * NG4 + ng) * ET + e)
                    pe.wait_ge(s["yg_sb"], (c + 1) * ET)
                    for e in range(ET):
                        mm = pe.matmul(ps[:, 6 + c, :], mw.wout[:, e, :], yg[:, e, :], start=(e == 0), stop=(e == ET - 1))
                    mm.then_inc(s["out_ps"], 1)

            @block.scalar
            def _(act):
                act.preload_act_table_set(EXPLN)
                for c in range(GROUP):
                    act.activation(k.sq[:, c, :], y[:, c, :], ACT.Square).then_inc(s["rms_sq"], 1)
                for c in range(GROUP):
                    act.wait_ge(s["rms_ps"], c + 1)
                    act.activation(k.sq[:, c, :], ps[:, 6 + c, :], ACT.Ln, bias=k.eps[:, 0:1]).then_inc(s["rms_log"], 1)
                    act.wait_ge(s["rms_log"], c + 1)
                    act.activation(k.sq[:, c, :], k.sq[:, c, :], ACT.Exp, scale=-0.5).then_inc(s["rms_rstd"], 1)
                for c in range(GROUP):
                    for m in range(ET):
                        act.wait_ge(s["xz_ps"], 2 * ET * c + m + 1)
                        act.activation(xs[:, c, m, PADT:PADT + S], ps[:, 2 * c + m, :], ACT.Copy).then_inc(s["xs_sb"], 1)
                for c in range(GROUP):
                    for m in range(ET):
                        act.wait_ge(s["xz_ps"], 2 * ET * c + ET + m + 1)
                        act.activation(zg[:, c, m, :], ps[:, 4 + 2 * c + m, :], ACT.Silu).then_inc(s["z_sb"], 1)
                for i in range(GROUP * ET):
                    act.wait_ge(s["tap_sb"], i * (TAPS - 1) + TAPS - 1)
                    act.activation(xc[:, i // ET, i % ET, :], cv[:, i // ET, i % ET, :], ACT.Silu).then_inc(s["xc_sb"], 1)
                for c in range(GROUP):
                    act.wait_ge(s["dbc_ps"], c + 1)
                    act.activation(dbc[:, c, :], ps[0:RANK + 2 * NS, 2 * c, :], ACT.Copy).then_inc(s["dbc_sb"], 1)
                for i in range(GROUP * ET):
                    c, e = i // ET, i % ET
                    act.wait_ge(s["dt_ps"], i + 1)
                    act.activation(dl[:, c, e, :], ps[:, 4 + i, :], ACT.Abs, bias=mw.cols[:, 2, e:e + 1]).then_inc(s["dt_abs"], 1)
                for i in range(GROUP * ET):
                    c, e = i // ET, i % ET
                    act.wait_ge(s["dt_abs"], i + 1)
                    act.activation(dl[:, c, e, :], dl[:, c, e, :], ACT.Exp, scale=-1.0).then_inc(s["dt_exp"], 1)
                for i in range(GROUP * ET):
                    c, e = i // ET, i % ET
                    act.wait_ge(s["dt_exp"], i + 1)
                    act.activation(dl[:, c, e, :], dl[:, c, e, :], ACT.Ln, bias=1.0).then_inc(s["dt_log"], 1)

                def copy_bc(c, ng):
                    g = c * NG4 + ng
                    for r in range(2 * NGR):
                        act.wait_ge(s["bcast_ps"], g * 2 * NGR + r + 1)
                        if r % 2 == 0:
                            if r == 0 and g >= 2:
                                act.wait_ge(s["bx_sb"], (g - 1) * ET)
                            act.activation(bb[:, g % 2, r // 2, :], ps[:, (g * 2 * NGR + r) % 4, :], ACT.Copy).then_inc(s["b_sb"], 1)
                        else:
                            if r == 1 and g >= 2:
                                act.wait_ge(s["hc_sb"], (g - 1) * ET)
                            act.activation(cc[:, g % 2, r // 2, :], ps[:, (g * 2 * NGR + r) % 4, :], ACT.Copy).then_inc(s["c_sb"], 1)

                def decay(u):
                    c, ng, e = u // UNITS, u % UNITS // ET, u % ET
                    if u == 0:
                        act.wait_ge(s["zero_col"], 2)
                        act.wait_ge(s["delta_sb"], GROUP * ET)
                    if u >= 2:
                        act.wait_ge(s["h_sb"], u - 1)
                    for n in range(NGR):
                        ins = act.activation(da[:, u % 2, n, 1:S], dl[:, c, e, 1:S], ACT.Exp,
                                             scale=mw.a[:, e, NGR * ng + n:NGR * ng + n + 1])
                    ins.then_inc(s["da_sb"], 1)

                copy_bc(0, 0)
                for g in range(GROUP * NG4):
                    for e in range(ET):
                        decay(g * ET + e)
                    if g + 1 < GROUP * NG4:
                        copy_bc((g + 1) // NG4, (g + 1) % NG4)

            @block.vector
            def _(dve):
                for c in range(GROUP):
                    dve.wait_ge(s["rms_rstd"], c + 1)
                    dve.scalar_tensor_tensor(k.xn[:, c, :], y[:, c, :], mw.vec[:, 0:1], k.sq[:, c, :], ALU.mult, ALU.mult)\
                       .then_inc(s["u_sb"], 1)
                dve.wait_ge(s["zero_col"], 2)
                for i in range(GROUP * ET):
                    c, e = i // ET, i % ET
                    dve.wait_ge(s["xs_sb"], i + 1)
                    dve.tensor_scalar(cv[:, c, e, :], xs[:, c, e, PADT:PADT + S], mw.taps[:, e, PADT:PADT + 1], mw.cols[:, 0, e:e + 1],
                                      ALU.mult, ALU.add).then_inc(s["tap0"], 1)
                    dve.wait_ge(s["tap0"], i + 1)
                    for j in range(TAPS - 1):
                        if j:
                            dve.wait_ge(s["tap_sb"], i * (TAPS - 1) + j)
                        dve.scalar_tensor_tensor(cv[:, c, e, :], xs[:, c, e, j:j + S], mw.taps[:, e, j:j + 1], cv[:, c, e, :],
                                                 ALU.mult, ALU.add).then_inc(s["tap_sb"], 1)
                for i in range(GROUP * ET):
                    c, e = i // ET, i % ET
                    dve.wait_ge(s["dt_log"], i + 1)
                    dve.tensor_scalar(rl[:, e, :], ps[:, 4 + i, :], mw.cols[:, 2, e:e + 1], 0.0, ALU.add, ALU.max).then_inc(s["dt_relu"], 1)
                    dve.wait_ge(s["dt_relu"], i + 1)
                    dve.tensor_tensor(dl[:, c, e, :], dl[:, c, e, :], rl[:, e, :], ALU.add).then_inc(s["delta_sb"], 1)
                    dve.wait_ge(s["delta_sb"], i + 1)
                    dve.tensor_tensor(dx[:, c, e, :], dl[:, c, e, :], xc[:, c, e, :], ALU.mult).then_inc(s["dx_sb"], 1)
                for u in range(GROUP * UNITS):
                    c, ng, e = u // UNITS, u % UNITS // ET, u % ET
                    dve.wait_ge(s["da_sb"], u + 1)
                    dve.wait_ge(s["bx_sb"], u + 1)
                    if u >= 2:
                        dve.wait_ge(s["y_ps"], u - 1)
                    dve.tensor_tensor_scan(flat(hh[:, u % 2, :, :]), flat(da[:, u % 2, :, :]), flat(bx[:, u % 2, :, :]), 0.0,
                                           ALU.mult, ALU.add).then_inc(s["h_sb"], 1)
                    dve.wait_ge(s["h_sb"], u + 1)
                    dve.wait_ge(s["c_sb"], (c * NG4 + ng + 1) * NGR)
                    dve.tensor_tensor(hh[:, u % 2, :, :], hh[:, u % 2, :, :], cc[:, (c * NG4 + ng) % 2, :, :], ALU.mult).then_inc(s["hc_sb"], 1)
                    if u % UNITS == UNITS - 1:
                        for e in range(ET):
                            i = c * ET + e
                            dve.wait_ge(s["y_ps"], u + 1)
                            if e == 0 and c > 0:
                                dve.wait_ge(s["out_ps"], c)
                            dve.scalar_tensor_tensor(yg[:, e, :], xc[:, c, e, :], mw.cols[:, 1, e:e + 1], ps[:, 4 + e, :],
                                                     ALU.mult, ALU.add).then_inc(s["y_skip"], 1)
                            dve.wait_ge(s["y_skip"], i + 1)
                            dve.tensor_tensor(yg[:, e, :], yg[:, e, :], zg[:, c, e, :], ALU.mult).then_inc(s["yg_sb"], 1)
                        dve.wait_ge(s["out_ps"], c + 1)
                        dve.scalar_tensor_tensor(y[:, c, :], y[:, c, :], 2.0, ps[:, 6 + c, :], ALU.mult, ALU.add).then_inc(s["y_new"], 1)


def stage_lowrank(nc, k, w, mw):
    with ExitStack() as mem, Stage(nc, LN_SEMS + "wts affine x_mid m1_ps m1_sb m2_ps m2_sb lo_ps lo_sb out_ps x_new") as s:
        sb = lambda n, sh: mem.enter_context(nc.sbuf_tensor(n, sh, F32))
        wt, b = sb("r_w", [P, P]), sb("r_b", [P, 1])
        ld, lu = sb("r_ld", [100, 4]), sb("r_lu", [4, 50])
        da, ua = sb("r_da", [100, P]), sb("r_ua", [50, P])
        m1, m2, lo = sb("r_m1", [4, P]), sb("r_m2", [50, P]), sb("r_lo", [P, P])
        ps = k.ps
        with nc.Block() as block:
            @block.sync
            def _(sp):
                for dst, src in ((wt, w["L2_ffn_W"]), (b, w["L2_ffn_b"]), (ld, w["L2_ffn_lora_down"]), (lu, w["L2_ffn_lora_up"]),
                                 (da, w["L2_ffn_down_aux"]), (ua, w["L2_ffn_up_aux"])):
                    sp.dma_start(dst[:, :], src).then_inc(s["wts"], 16)

            @block.tensor
            def _(pe):
                ln_tensor(pe, k, s, k.y)
                pe.wait_ge(s["wts"], 96)
                pe.matmul(ps[0:4, 0, 0:P], ld[:, :], da[:, :], start=True, stop=True).then_inc(s["m1_ps"], 1)
                pe.wait_ge(s["m1_sb"], 1)
                pe.matmul(ps[0:50, 1, 0:P], lu[:, :], m1[:, :], start=True, stop=True).then_inc(s["m2_ps"], 1)
                pe.wait_ge(s["m2_sb"], 1)
                pe.matmul(ps[:, 2, 0:P], m2[:, :], ua[:, :], start=True, stop=True).then_inc(s["lo_ps"], 1)
                for c in range(GROUP):
                    pe.wait_ge(s["x_mid"], c + 1)
                    pe.matmul(ps[:, 6 + c, :], k.mean_mat[:, :], k.x[:, c, :], start=True, stop=True).then_inc(s["ln_mean"], 1)
                for c in range(GROUP):
                    pe.wait_ge(s["ln_sq"], GROUP + c + 1)
                    pe.matmul(ps[:, 6 + c, :], k.mean_mat[:, :], k.sq[:, c, :], start=True, stop=True).then_inc(s["ln_var"], 1)
                pe.wait_ge(s["lo_sb"], 1)
                for c in range(GROUP):
                    pe.wait_ge(s["xn_ready"], GROUP + c + 1)
                    pe.matmul(ps[:, 3 + c, :], wt[:, :], k.xn[:, c, :], start=True, stop=False)
                    pe.matmul(ps[:, 3 + c, :], lo[:, :], k.xn[:, c, :], start=False, stop=True).then_inc(s["out_ps"], 1)

            @block.scalar
            def _(act):
                act.preload_act_table_set(EXPLN)
                ln_scalar(act, k, s)
                act.wait_ge(s["m1_ps"], 1)
                act.activation(m1[:, :], ps[0:4, 0, 0:P], ACT.Copy).then_inc(s["m1_sb"], 1)
                act.wait_ge(s["m2_ps"], 1)
                act.activation(m2[:, :], ps[0:50, 1, 0:P], ACT.Copy).then_inc(s["m2_sb"], 1)
                act.wait_ge(s["lo_ps"], 1)
                act.activation(lo[:, :], ps[:, 2, 0:P], ACT.Copy).then_inc(s["lo_sb"], 1)
                for c in range(GROUP):
                    act.wait_ge(s["ln_xc"], GROUP + c + 1)
                    act.activation(k.sq[:, c, :], k.xc[:, c, :], ACT.Square).then_inc(s["ln_sq"], 1)
                for c in range(GROUP):
                    act.wait_ge(s["ln_var"], GROUP + c + 1)
                    act.activation(k.sq[:, c, :], ps[:, 6 + c, :], ACT.Ln, bias=k.eps[:, 0:1]).then_inc(s["ln_log"], 1)
                    act.wait_ge(s["ln_log"], GROUP + c + 1)
                    act.activation(k.sq[:, c, :], k.sq[:, c, :], ACT.Exp, scale=-0.5).then_inc(s["ln_rstd"], 1)

            @block.vector
            def _(dve):
                ln_vector(dve, k, s, k.y, k.y)
                for c in range(GROUP):
                    dve.wait_ge(s["xn_ready"], c + 1)
                    dve.tensor_scalar(k.y[:, c, :], k.y[:, c, :], mw.vec[:, 1:2], mw.vec[:, 2:3], ALU.mult, ALU.add).then_inc(s["affine"], 1)
                    dve.wait_ge(s["affine"], c + 1)
                    dve.tensor_tensor(k.x[:, c, :], k.x[:, c, :], k.y[:, c, :], ALU.add).then_inc(s["x_mid"], 1)
                for c in range(GROUP):
                    dve.wait_ge(s["ln_mean"], GROUP + c + 1)
                    dve.tensor_tensor(k.xc[:, c, :], k.x[:, c, :], ps[:, 6 + c, :], ALU.subtract).then_inc(s["ln_xc"], 1)
                for c in range(GROUP):
                    dve.wait_ge(s["ln_rstd"], GROUP + c + 1)
                    dve.tensor_tensor(k.xn[:, c, :], k.xc[:, c, :], k.sq[:, c, :], ALU.mult).then_inc(s["xn_ready"], 1)
                dve.wait_ge(s["wts"], 96)
                for c in range(GROUP):
                    dve.wait_ge(s["out_ps"], c + 1)
                    dve.scalar_tensor_tensor(k.x[:, c, :], ps[:, 3 + c, :], b[:, 0:1], k.x[:, c, :], ALU.add, ALU.add).then_inc(s["x_new"], 1)


def stage_delta(nc, k, w):
    H, D = 16, 8
    with ExitStack() as mem, Stage(nc, LN_SEMS + "wts block0 block_rdy fold_ps fold_sb proj_ps beta_sb vs_sb qs_sb kv_sb g_sb o_sb out_ps r_sb "
                                   "affine x_new") as s:
        sb = lambda n, sh: mem.enter_context(nc.sbuf_tensor(n, sh, F32))
        wk, wo, wqt, wvt = [sb(n, [P, P]) for n in ("d_wk", "d_wo", "d_wqt", "d_wvt")]
        wb, cols = sb("d_wb", [P, H]), sb("d_cols", [P, 4])
        blk = sb("d_blk", [P, H, D])
        wqs, wvs = sb("d_wqs", [P, P]), sb("d_wvs", [P, P])
        wbr = sb("d_wbr", [P, H, D])
        beta, vs, qs, kv, g, o, r = [sb(n, [P, GROUP, S]) for n in ("d_beta", "d_vs", "d_qs", "d_kv", "d_g", "d_o", "d_r")]
        ps = k.ps
        with nc.Block() as block:
            @block.sync
            def _(sp):
                for dst, src in ((wk, w["L3_attn_Wk"]), (wo, w["L3_attn_Wo"]), (wqt, w["L3_attn_Wq"]), (wvt, w["L3_attn_Wv"]),
                                 (wb, w["L3_attn_Wbeta"]), (cols, w["L3_cols"])):
                    sp.dma_start(dst[:, :], src).then_inc(s["wts"], 16)

            @block.gpsimd
            def _(pool):
                pool.memset(blk[:, :, :], 1.0).then_inc(s["block0"], 1)
                pool.wait_ge(s["block0"], 1)
                pool.affine_select(out=blk[:, :, :], in_=blk[:, :, :], compare_op=ALU.is_ge, fill=0.0, base=0,
                                   pattern=[[-D, H], [0, D]], channel_multiplier=1).then_inc(s["block0"], 1)
                pool.wait_ge(s["block0"], 2)
                pool.affine_select(out=blk[:, :, :], in_=blk[:, :, :], compare_op=ALU.is_ge, fill=0.0, base=D - 1,
                                   pattern=[[D, H], [0, D]], channel_multiplier=-1).then_inc(s["block0"], 1)
                pool.wait_ge(s["wts"], 96)
                pool.tensor_copy(wbr[:, :, :], wb[:, :, None].to_broadcast([P, H, D])).then_inc(s["block_rdy"], 1)

            @block.tensor
            def _(pe):
                ln_tensor(pe, k, s, k.x)
                pe.wait_ge(s["wts"], 96)
                pe.wait_ge(s["block0"], 3)
                pe.wait_ge(s["block_rdy"], 1)
                pe.matmul(ps[:, 4, 0:P], wvt[:, :], flat(blk[:, :, :]), start=True, stop=True).then_inc(s["fold_ps"], 1)
                pe.matmul(ps[:, 5, 0:P], wqt[:, :], flat(blk[:, :, :]), start=True, stop=True).then_inc(s["fold_ps"], 1)
                pe.wait_ge(s["fold_sb"], 2)
                for c in range(GROUP):
                    pe.wait_ge(s["xn_ready"], c + 1)
                    if c > 0:
                        pe.wait_ge(s["kv_sb"], c)
                        pe.wait_ge(s["beta_sb"], c)
                        pe.wait_ge(s["qs_sb"], c)
                    for n, wt in enumerate((flat(wbr[:, :, :]), wvs[:, :], wqs[:, :], wk[:, :])):
                        pe.matmul(ps[:, n, :], wt, k.xn[:, c, :], start=True, stop=True).then_inc(s["proj_ps"], 1)
                for c in range(GROUP):
                    pe.wait_ge(s["o_sb"], c + 1)
                    pe.matmul(ps[:, 4 + c, :], wo[:, :], o[:, c, :], start=True, stop=True).then_inc(s["out_ps"], 1)
                for c in range(GROUP):
                    pe.wait_ge(s["r_sb"], c + 1)
                    pe.matmul(ps[:, 6 + c, :], k.mean_mat[:, :], r[:, c, :], start=True, stop=True).then_inc(s["ln_mean"], 1)
                for c in range(GROUP):
                    pe.wait_ge(s["ln_sq"], GROUP + c + 1)
                    pe.matmul(ps[:, 6 + c, :], k.mean_mat[:, :], k.sq[:, c, :], start=True, stop=True).then_inc(s["ln_var"], 1)

            @block.scalar
            def _(act):
                act.preload_act_table_set(EXPLN)
                ln_scalar(act, k, s)
                for n, dst in enumerate((wvs, wqs)):
                    act.wait_ge(s["fold_ps"], n + 1)
                    act.activation(dst[:, :], ps[:, 4 + n, 0:P], ACT.Copy).then_inc(s["fold_sb"], 1)
                act.wait_ge(s["wts"], 96)
                for c in range(GROUP):
                    act.wait_ge(s["proj_ps"], 4 * c + 1)
                    act.activation(beta[:, c, :], ps[:, 0, :], ACT.Sigmoid, bias=cols[:, 0:1]).then_inc(s["beta_sb"], 1)
                    act.wait_ge(s["proj_ps"], 4 * c + 2)
                    act.activation(vs[:, c, :], ps[:, 1, :], ACT.Copy).then_inc(s["vs_sb"], 1)
                    act.wait_ge(s["proj_ps"], 4 * c + 3)
                    act.activation(qs[:, c, :], ps[:, 2, :], ACT.Copy).then_inc(s["qs_sb"], 1)
                for c in range(GROUP):
                    act.wait_ge(s["ln_xc"], GROUP + c + 1)
                    act.activation(k.sq[:, c, :], k.xc[:, c, :], ACT.Square).then_inc(s["ln_sq"], 1)
                for c in range(GROUP):
                    act.wait_ge(s["ln_var"], GROUP + c + 1)
                    act.activation(k.sq[:, c, :], ps[:, 6 + c, :], ACT.Ln, bias=k.eps[:, 0:1]).then_inc(s["ln_log"], 1)
                    act.wait_ge(s["ln_log"], GROUP + c + 1)
                    act.activation(k.sq[:, c, :], k.sq[:, c, :], ACT.Exp, scale=-0.5).then_inc(s["ln_rstd"], 1)

            @block.vector
            def _(dve):
                ln_vector(dve, k, s, k.x, k.xn)
                for c in range(GROUP):
                    dve.wait_ge(s["vs_sb"], c + 1)
                    dve.wait_ge(s["proj_ps"], 4 * c + 4)
                    dve.tensor_tensor(kv[:, c, :], vs[:, c, :], ps[:, 3, :], ALU.mult).then_inc(s["kv_sb"], 1)
                    dve.wait_ge(s["kv_sb"], c + 1)
                    dve.wait_ge(s["beta_sb"], c + 1)
                    dve.tensor_tensor_scan(g[:, c, :], beta[:, c, :], kv[:, c, :], 0.0, ALU.mult, ALU.add).then_inc(s["g_sb"], 1)
                    dve.wait_ge(s["g_sb"], c + 1)
                    dve.wait_ge(s["qs_sb"], c + 1)
                    dve.tensor_tensor(o[:, c, :], g[:, c, :], qs[:, c, :], ALU.mult).then_inc(s["o_sb"], 1)
                for c in range(GROUP):
                    dve.wait_ge(s["out_ps"], c + 1)
                    dve.scalar_tensor_tensor(r[:, c, :], ps[:, 4 + c, :], cols[:, 1:2], k.xn[:, c, :], ALU.add, ALU.add).then_inc(s["r_sb"], 1)
                for c in range(GROUP):
                    dve.wait_ge(s["ln_mean"], GROUP + c + 1)
                    dve.tensor_tensor(k.xc[:, c, :], r[:, c, :], ps[:, 6 + c, :], ALU.subtract).then_inc(s["ln_xc"], 1)
                for c in range(GROUP):
                    dve.wait_ge(s["ln_rstd"], GROUP + c + 1)
                    dve.tensor_tensor(r[:, c, :], k.xc[:, c, :], k.sq[:, c, :], ALU.mult).then_inc(s["affine"], 1)
                    dve.wait_ge(s["affine"], 2 * c + 1)
                    dve.tensor_scalar(r[:, c, :], r[:, c, :], cols[:, 2:3], cols[:, 3:4], ALU.mult, ALU.add).then_inc(s["affine"], 1)
                    dve.wait_ge(s["affine"], 2 * c + 2)
                    dve.tensor_tensor(k.x[:, c, :], k.x[:, c, :], r[:, c, :], ALU.add).then_inc(s["x_new"], 1)


def stage_store(nc, k, g, out_dram):
    with Stage(nc, "turned tok_sb stored") as s:
        with nc.Block() as block:
            @block.tensor
            def _(pe):
                for c in range(GROUP):
                    for t in range(NT):
                        mm = pe.transpose(k.ps[:, c, P * t:P * (t + 1)], k.x[:, c, P * t:P * (t + 1)], k.ident[:, :])
                    mm.then_inc(s["turned"], 1)

            @block.vector
            def _(dve):
                for c in range(GROUP):
                    dve.wait_ge(s["turned"], c + 1)
                    dve.tensor_copy(flat(k.tok[:, c, :, :]), k.ps[:, c, :]).then_inc(s["tok_sb"], 1)

            @block.sync
            def _(sp):
                sp.wait_ge(s["tok_sb"], GROUP)
                sp.dma_start(out_dram[bass.ds(g * GROUP, GROUP), :, :].rearrange("b (t p) d -> p b t d", p=P),
                             k.tok[:, :, :, :]).then_inc(s["stored"], 16)
                sp.wait_ge(s["stored"], 16)


def build(nc, d):
    w = d
    with ExitStack() as ctx:
        sb = lambda n, sh: ctx.enter_context(nc.sbuf_tensor(n, sh, F32))
        k = Bag()
        k.ps = ctx.enter_context(nc.psum_tensor("ps", [P, 8, S], F32))
        k.ident, k.mean_mat = sb("ident", [P, P]), sb("mean_mat", [P, P])
        k.eps, k.eps_z = sb("eps", [P, 1]), sb("eps_z", [P, 1])
        k.lower = sb("lower", [P, EXPERTS, EXPERTS])
        k.head_sel, k.head_sel_t = sb("head_sel", [P, 8, 16]), sb("head_sel_t", [16, 8, P])
        k.x, k.y, k.xn, k.xc, k.sq = [sb(n, [P, GROUP, S]) for n in ("x", "y", "xn", "xc", "sq")]
        k.tok = k.sq[:, :, :].rearrange("p b (t d) -> p b t d", d=P)
        mw = Bag()
        mw.win = sb("mw_in", [P, 2 * ED])
        mw.taps = sb("mw_taps", [P, ET, TAPS])
        mw.cols = sb("mw_cols", [P, 3, ET])
        mw.wx = sb("mw_x", [P, ET, RANK + 2 * NS])
        mw.wdt = sb("mw_dt", [RANK, ED])
        mw.a = sb("mw_a", [P, ET, NS])
        mw.wout = sb("mw_out", [P, ET, P])
        mw.vec = sb("mw_vec", [P, 3])

        with Stage(nc, "fills sel wts a_exp") as s:
            with nc.Block() as block:
                @block.sync
                def _(sp):
                    for dst, src in ((mw.win[:, :], w["L2_attn_W_in"]), (mw.taps[:, :, :], w["L2_attn_conv_w"].rearrange("(e p) t -> p e t", p=P)),
                                     (mw.cols[:, :, :], w["L2_cols"]), (mw.wx[:, :, :], w["L2_attn_W_x"].rearrange("(e p) n -> p e n", p=P)),
                                     (mw.wdt[:, :], w["L2_attn_W_dt"]), (mw.a[:, :, :], w["L2_attn_A_log"].rearrange("(e p) n -> p e n", p=P)),
                                     (mw.wout[:, :, :], w["L2_attn_W_out"].rearrange("(e p) n -> p e n", p=P)), (mw.vec[:, :], w["L2_vec"]),
                                     (k.head_sel[:, :, :], w["head_sel"]), (k.head_sel_t[:, :, :], w["head_sel_t"])):
                        sp.dma_start(dst, src).then_inc(s["wts"], 16)
                    sp.wait_ge(s["wts"], 160)

                @block.gpsimd
                def _(pool):
                    pool.memset(k.ident[:, :], 0.0).then_inc(s["fills"], 1)
                    pool.memset(k.mean_mat[:, :], 1.0 / P).then_inc(s["fills"], 1)
                    pool.memset(k.eps[:, :], EPS).then_inc(s["fills"], 1)
                    pool.memset(k.eps_z[:, :], 2e-12).then_inc(s["fills"], 1)
                    pool.memset(k.lower[:, :, :], 1.0).then_inc(s["fills"], 1)
                    pool.wait_ge(s["fills"], 5)
                    pool.affine_select(out=k.ident[:, :], in_=k.ident[:, :], compare_op=ALU.not_equal, fill=1.0, base=0,
                                       pattern=[[-1, P]], channel_multiplier=1).then_inc(s["sel"], 1)
                    pool.affine_select(out=k.lower[:, :, :], in_=k.lower[:, :, :], compare_op=ALU.is_gt, fill=0.0, base=0,
                                       pattern=[[1, EXPERTS], [-1, EXPERTS]], channel_multiplier=0).then_inc(s["sel"], 1)
                    pool.wait_ge(s["sel"], 2)

                @block.scalar
                def _(act):
                    act.wait_ge(s["wts"], 160)
                    act.activation(mw.a[:, :, :], mw.a[:, :, :], ACT.Exp).then_inc(s["a_exp"], 1)

                @block.vector
                def _(dve):
                    dve.wait_ge(s["a_exp"], 1)
                    dve.tensor_scalar(mw.a[:, :, :], mw.a[:, :, :], -1.0, None, ALU.mult).then_inc(s["a_exp"], 1)
                    dve.wait_ge(s["a_exp"], 2)

        with nc.Fori(0, BATCH // GROUP) as g:
            stage_load(nc, k, g, w["x"])
            stage_taylor(nc, k, w)
            stage_moe(nc, k, "e", w["L0_ffn_Wg"], None, w["L0_ffn_W1"], w["L0_ffn_W2"], w["L0_ffn_W3"], 2)
            stage_softmax(nc, k, w)
            with ExitStack() as lmem:
                lsb = lambda n, sh: lmem.enter_context(nc.sbuf_tensor(n, sh, F32))
                k.rot = lsb("rot", [P, 4, S])
                for layer in range(2):
                    with ExitStack() as wmem, Stage(nc, "w_local") as ws:
                        wsb = lambda n, sh: wmem.enter_context(nc.sbuf_tensor(n + str(layer), sh, F32))
                        k.w_local = ws["w_local"]
                        wl = Bag()
                        wl.v = wsb("lw_v", [P, 512])
                        wl.qk = wsb("lw_qk", [P, 1024])
                        wl.qkr = wsb("lw_qkr", [P, 1024])
                        wl.o = wsb("lw_o", [P, 4, P])
                        wl.up = wsb("lw_up", [P, 2 * HID])
                        wl.down = wsb("lw_down", [P, 3, P])
                        wl.scales = wsb("lw_sc", [P, 4])
                        wl.b1 = wsb("lw_b1", [P, 6])
                        wl.ln = wsb("lw_ln", [P, 3])
                        wl.dmas = 0
                        with nc.Block() as block:
                            @block.sync
                            def _(sp):
                                moves = [(wl.v[:, :], w["L1_ffn_wqkv"][layer, :, 1024:1536]), (wl.qk[:, :], w["L1_ffn_wqkv"][layer, :, 0:1024]),
                                         (wl.qkr[:, :], w["L1_qk_rot"][layer]), (wl.o[:, :, :], w["L1_ffn_wo"][layer].rearrange("(t p) d -> p t d", p=P)),
                                         (wl.up[:, :], w["L1_ffn_w1"][layer]), (wl.scales[:, :], w["L1_scales"][layer]), (wl.ln[:, :], w["L1_ln"][layer])]
                                for f, (off, n) in enumerate(HT):
                                    moves += [(wl.down[0:n, f, :], w["L1_ffn_w2"][layer, off:off + n, :])]
                                    for half in range(2):
                                        moves += [(wl.b1[0:n, 3 * half + f:3 * half + f + 1],
                                                   w["L1_ffn_b1"][layer, HID * half + off:HID * half + off + n][:, None])]
                                if layer == 0:
                                    moves += [(k.rot[:, :, :], w["rot_tables"])]
                                for dst, src in moves:
                                    sp.dma_start(dst, src).then_inc(ws["w_local"], 16)
                                wl.dmas = 16 * len(moves)
                                sp.wait_ge(ws["w_local"], wl.dmas)
                        stage_local(nc, k, w, wl, layer)
            stage_ln_y(nc, k)
            with nc.Fori(0, DEPTH):
                stage_mamba(nc, k, w, mw)
            stage_lowrank(nc, k, w, mw)
            stage_delta(nc, k, w)
            stage_moe(nc, k, "f", w["L3_ffn_gate_w"], w["L3_ffn_gate_b"], w["L3_wa"], w["L3_wb"], w["L3_ffn_w2"], 4, w["L3_ba"], w["L3_bb"], w["L3_ffn_b2"])
            stage_store(nc, k, g, w["out"])


def rotary_tables():
    f = np.float32
    half = np.arange(0, LD, 2, dtype=f)
    inv = (f(1.0) / np.power(f(10000.0), half / f(LD))).astype(f)
    t = np.arange(S, dtype=f)
    freqs = (t[:, None] * inv[None, :]).astype(f)
    freqs = np.concatenate([freqs, freqs], -1)
    base = ((half + f(0.4 * LD)) / f(1.4 * LD)).astype(f)
    power = ((t - f(S // 2)) / f(WIN // 2)).astype(f)
    scale = np.power(base[None, :], power[:, None]).astype(f)
    scale = np.concatenate([scale, scale], -1)
    cos, sin = np.cos(freqs), np.sin(freqs)
    sign = np.where(np.arange(LD) < LD // 2, f(-1), f(1))[None, :]
    tabs = [cos * scale, sin * scale * sign, cos / scale, sin / scale * sign]
    return np.ascontiguousarray(np.stack([np.tile(a.T, (2, 1)) for a in tabs], 1).astype(f))


def head_selectors():
    sel = np.zeros((P, 8, 16), np.float32)
    for m in range(8):
        for j in range(2):
            sel[LD * j:LD * (j + 1), m, 2 * m + j] = 1
    return sel, np.ascontiguousarray(sel.transpose(2, 1, 0))


def lay_out(i):
    a = {n: np.ascontiguousarray(v) for n, v in i.items()}
    T = lambda v, *ax: np.ascontiguousarray(v.transpose(*ax))
    o = {"x": a["L0_attn_hidden_states"]}
    for n in ("L0_attn_Wq", "L0_attn_Wk", "L0_attn_Wv", "L0_attn_Wo", "L1_attn_kernel", "L1_attn_WO", "L1_ffn_wqkv", "L1_ffn_wo",
              "L1_ffn_w1", "L1_ffn_b1", "L1_ffn_w2", "L2_attn_W_in", "L2_attn_conv_w", "L2_attn_W_x", "L2_attn_W_dt",
              "L2_attn_A_log", "L2_attn_W_out", "L2_ffn_down_aux", "L3_attn_Wk", "L3_attn_Wo", "L3_attn_Wbeta", "L3_ffn_gate_w",
              "L3_ffn_gate_b", "L3_ffn_w2", "L3_ffn_b2"):
        o[n] = a[n]
    for n in ("L0_ffn_Wg", "L2_ffn_W", "L2_ffn_lora_down", "L2_ffn_lora_up", "L2_ffn_up_aux", "L3_attn_Wq", "L3_attn_Wv"):
        o[n] = T(a[n], 1, 0)
    for n in ("L0_ffn_W1", "L0_ffn_W2", "L0_ffn_W3"):
        o[n] = T(a[n], 0, 2, 1)
    qk = a["L1_ffn_wqkv"][:, :, 0:1024].reshape(2, P, 16, 2, 32)
    o["L1_qk_rot"] = np.ascontiguousarray(qk[:, :, :, ::-1, :]).reshape(2, P, 1024)
    two = lambda v: np.tile(v, (1, 2))
    swap = lambda v: np.concatenate([v[:, 32:], v[:, :32]], 1)
    qs, ks = a["L1_ffn_q_scale"], a["L1_ffn_k_scale"]
    o["L1_scales"] = np.ascontiguousarray(np.stack([two(qs), two(swap(qs)), two(ks), two(swap(ks))], -1))
    o["L1_ln"] = np.ascontiguousarray(np.stack([a["L1_ffn_ln_g"], a["L1_ffn_ln_b"], a["L1_ffn_b2"]], -1))
    o["rot_tables"] = rotary_tables()
    o["head_sel"], o["head_sel_t"] = head_selectors()
    ecol = lambda n: a[n].reshape(ET, P).T
    o["L2_cols"] = np.ascontiguousarray(np.stack([ecol("L2_attn_conv_b"), ecol("L2_attn_Dp"), ecol("L2_attn_b_dt")], 1))
    o["L2_vec"] = np.ascontiguousarray(np.stack([a["L2_attn_rms_w"], a["L2_attn_ln_w"], a["L2_attn_ln_b"]], -1))
    o["L2_ffn_b"] = a["L2_ffn_b"][:, None]
    o["L3_cols"] = np.ascontiguousarray(np.stack([np.repeat(a["L3_attn_b_beta"], 8), a["L3_attn_b_o"], a["L3_attn_ln_g"],
                                                  a["L3_attn_ln_b"]], -1))
    w1, b1 = a["L3_ffn_w1"], a["L3_ffn_b1"].reshape(EXPERTS, 2, MOE_F // P, P)
    o["L3_wa"], o["L3_wb"] = np.ascontiguousarray(w1[:, :, MOE_F:]), np.ascontiguousarray(w1[:, :, :MOE_F])
    o["L3_ba"], o["L3_bb"] = T(b1[:, 1], 2, 0, 1), T(b1[:, 0], 2, 0, 1)
    return o


def kernel(**inputs):
    import numpy as _np
    import concourse.bacc as _bacc
    from concourse import mybir as _mybir
    from concourse.bass_utils import run_bass_kernel_spmd as _run

    nc = _bacc.Bacc("TRN2", target_bir_lowering=False, num_devices=1)
    arrays, d = {}, {}
    for name, a in lay_out({n: _np.asarray(v) for n, v in inputs.items()}).items():
        a = _np.ascontiguousarray(a)
        arrays[f"in_{name}"] = a
        d[name] = nc.dram_tensor(f"in_{name}", a.shape, _mybir.dt.from_np(a.dtype), kind="ExternalInput").ap()
    d["out"] = nc.dram_tensor("out_0", (BATCH, S, P), F32, kind="ExternalOutput").ap()
    build(nc, d)
    r = _run(nc, [arrays], core_ids=[0])
    return r.results[0]["out_0"]
```

```python
from contextlib import ExitStack, contextmanager

import numpy as np
import concourse.bass as bass
from concourse import mybir

F32 = mybir.dt.float32
BF16 = mybir.dt.bfloat16
ALU = mybir.AluOpType
ACT = mybir.ActivationFunctionType
AX = mybir.AxisListType

P = 128
BATCH, S = 4, 512
GROUP = 2
NT = S // P
EPS = 1e-5
EXPLN = "natural_log_exp_and_others"

L0H, L0F, HD = 16, 16, 64
EXPERTS = 8
LH, LD, WIN = 8, 64, 64
HID = 341
HT = [(0, 128), (128, 128), (256, HID - 256)]
DEPTH, ED, NS, RANK, TAPS = 6, 256, 16, 64, 4
ET = ED // P
NGR = 4
MOE_F = 512
ROUTE_COLS = NT * EXPERTS


class Bag:
    pass


def flat(ap):
    return ap.rearrange("p a b -> p (a b)")


@contextmanager
def Stage(nc, names):
    with ExitStack() as ctx:
        sems = {n: ctx.enter_context(nc.semaphore(n)) for n in names.split()}
        yield sems
        for q in sems.values():
            nc.sync.sem_clear(q)
        nc.all_engine_barrier()


LN_SEMS = " ln_mean ln_xc ln_sq ln_var ln_log ln_rstd xn_ready "


def ln_tensor(pe, k, s, src, src_ready=None):
    for c in range(GROUP):
        if src_ready is not None:
            pe.wait_ge(src_ready, c + 1)
        pe.matmul(k.ps[:, 6 + c, :], k.mean_mat[:, :], src[:, c, :], start=True, stop=True).then_inc(s["ln_mean"], 1)
    for c in range(GROUP):
        pe.wait_ge(s["ln_sq"], c + 1)
        pe.matmul(k.ps[:, 6 + c, :], k.mean_mat[:, :], k.sq[:, c, :], start=True, stop=True).then_inc(s["ln_var"], 1)


def ln_scalar(act, k, s):
    for c in range(GROUP):
        act.wait_ge(s["ln_xc"], c + 1)
        act.activation(k.sq[:, c, :], k.xc[:, c, :], ACT.Square).then_inc(s["ln_sq"], 1)
    for c in range(GROUP):
        act.wait_ge(s["ln_var"], c + 1)
        act.activation(k.sq[:, c, :], k.ps[:, 6 + c, :], ACT.Ln, bias=k.eps[:, 0:1]).then_inc(s["ln_log"], 1)
        act.wait_ge(s["ln_log"], c + 1)
        act.activation(k.sq[:, c, :], k.sq[:, c, :], ACT.Exp, scale=-0.5).then_inc(s["ln_rstd"], 1)


def ln_vector(dve, k, s, src, dst):
    for c in range(GROUP):
        dve.wait_ge(s["ln_mean"], c + 1)
        dve.tensor_tensor(k.xc[:, c, :], src[:, c, :], k.ps[:, 6 + c, :], ALU.subtract).then_inc(s["ln_xc"], 1)
    for c in range(GROUP):
        dve.wait_ge(s["ln_rstd"], c + 1)
        dve.tensor_tensor(dst[:, c, :], k.xc[:, c, :], k.sq[:, c, :], ALU.mult).then_inc(s["xn_ready"], 1)


ROUTE_SEMS = " logits_ps route_chain route_diff route_exp gate_tm gate_ps gate_sb "


def route_tensor_logits(pe, k, s, c, w_gate):
    for t in range(NT):
        mm = pe.matmul(k.ps[:, c, EXPERTS * t:EXPERTS * (t + 1)], k.xn[:, c, P * t:P * (t + 1)], w_gate[:, :],
                       start=True, stop=True)
    mm.then_inc(s["logits_ps"], 1)


def route_tensor_turn(pe, k, s, c):
    pe.wait_ge(s["gate_tm"], c + 1)
    for t in range(NT):
        mm = pe.transpose(k.ps[0:EXPERTS, 2 + c, P * t:P * (t + 1)], k.gates[:, c, t, :], k.ident[:, :])
    mm.then_inc(s["gate_ps"], 1)


def route_scalar(act, k, s, c):
    act.wait_ge(s["route_diff"], c + 1)
    act.activation(k.r_exp[:, c, :, :], k.r_diff[:, c, :, :], ACT.Exp).then_inc(s["route_exp"], 1)


def route_vector(dve, k, s, c, done, gate_b=None):

    def link(ins):
        done[0] += 1
        ins.then_inc(s["route_chain"], 1)
        dve.wait_ge(s["route_chain"], done[0])

    lg = k.r_logit[:, c, :, :]
    dve.wait_ge(s["logits_ps"], c + 1)
    link(dve.tensor_copy(flat(lg), k.ps[:, c, 0:ROUTE_COLS]))
    if gate_b is not None:
        link(dve.tensor_tensor(lg, lg, gate_b[:, None, :].to_broadcast([P, NT, EXPERTS]), ALU.add))
    shape = [P, NT, EXPERTS, EXPERTS]
    other, own = lg[:, :, None, :].to_broadcast(shape), lg[:, :, :, None].to_broadcast(shape)
    dve.tensor_tensor(k.r_gt[:, :, :, :], other, own, ALU.is_gt)
    link(dve.tensor_tensor(k.r_eq[:, :, :, :], other, own, ALU.is_equal))
    link(dve.tensor_tensor(k.r_eq[:, :, :, :], k.r_eq[:, :, :, :],
                           k.lower[:, None, :, :].to_broadcast(shape), ALU.mult))
    link(dve.tensor_tensor(k.r_gt[:, :, :, :], k.r_gt[:, :, :, :], k.r_eq[:, :, :, :], ALU.add))
    link(dve.tensor_reduce(k.r_rank[:, :, :], k.r_gt[:, :, :, :], AX.X, ALU.add))
    dve.tensor_scalar(k.r_sel[:, :, :], k.r_rank[:, :, :], 2.0, None, ALU.is_lt)
    link(dve.tensor_reduce(k.r_max[:, :], lg, AX.X, ALU.max))
    dve.tensor_tensor(k.r_diff[:, c, :, :], lg, k.r_max[:, :, None].to_broadcast([P, NT, EXPERTS]),
                      ALU.subtract).then_inc(s["route_diff"], 1)
    dve.wait_ge(s["route_exp"], c + 1)
    link(dve.tensor_tensor(k.r_sel[:, :, :], k.r_sel[:, :, :], k.r_exp[:, c, :, :], ALU.mult))
    link(dve.tensor_reduce(k.r_sum[:, :], k.r_sel[:, :, :], AX.X, ALU.add))
    link(dve.reciprocal(k.r_sum[:, :], k.r_sum[:, :]))
    dve.tensor_tensor(k.gates[:, c, :, :], k.r_sel[:, :, :], k.r_sum[:, :, None].to_broadcast([P, NT, EXPERTS]),
                      ALU.mult).then_inc(s["gate_tm"], 1)
    dve.wait_ge(s["gate_ps"], c + 1)
    dve.tensor_copy(k.gate_t[:, c, :], k.ps[0:EXPERTS, 2 + c, :]).then_inc(s["gate_sb"], 1)


def stage_load(nc, k, g, x_dram):
    with Stage(nc, "x_in x_turned x_sb") as s:
        with nc.Block() as block:
            @block.sync
            def _(sp):
                sp.dma_start(k.tok[:, :, :, :], x_dram[bass.ds(g * GROUP, GROUP), :, :]
                             .rearrange("b (t p) d -> p b t d", p=P)).then_inc(s["x_in"], 16)

            @block.tensor
            def _(pe):
                pe.wait_ge(s["x_in"], 16)
                for c in range(GROUP):
                    for t in range(NT):
                        mm = pe.transpose(k.ps[:, c, P * t:P * (t + 1)], k.tok[:, c, t, :], k.ident[:, :])
                    mm.then_inc(s["x_turned"], 1)

            @block.vector
            def _(dve):
                for c in range(GROUP):
                    dve.wait_ge(s["x_turned"], c + 1)
                    dve.tensor_copy(k.x[:, c, :], k.ps[:, c, :]).then_inc(s["x_sb"], 1)


def stage_taylor(nc, k, w, later):
    WIDE = [S - P * t for t in range(NT)]
    OFF = [sum(WIDE[:t]) for t in range(NT)]
    COLS = sum(WIDE)
    BANKCOLS = [(OFF[0], WIDE[0]), (OFF[1], WIDE[1]), (OFF[2], WIDE[2] + WIDE[3])]
    NPROJ = 4 + 4 + 2 * NT
    with ExitStack() as mem, Stage(nc, LN_SEMS + "zeroed wts mask_v ones_v mask_rdy proj_ps proj_act proj_dve scored squared "
                                   "masked y_ps z_log z_rec normed out_ps x_new") as s:
        sb = lambda n, sh: mem.enter_context(nc.sbuf_tensor(n, sh, F32))
        wq, wk = sb("t_wq", [P, L0H, 32]), sb("t_wk", [P, L0H, 32])
        wv, wo = sb("t_wv", [P, L0H * HD]), sb("t_wo", [P, L0H * HD // P, P])
        qt, kt = sb("t_q", [P, 4, S]), sb("t_k", [P, 4, S])
        v = sb("t_v", [P, NT, L0H // 2, 3, HD])
        a = sb("t_a", [P, 2, COLS])
        mask = sb("t_mask", [P, COLS])
        rz = sb("t_rz", [P, 2, S])
        o = sb("t_o", [P, L0H // 2, S])
        ps = k.ps
        with nc.Block() as block:
            @block.sync
            def _(sp):
                sp.dma_start(wv[:, :], w["L0_attn_Wv"]).then_inc(s["wts"], 16)
                sp.dma_start(wo[:, :, :], w["L0_attn_Wo"].rearrange("(t p) d -> p t d", p=P)).then_inc(s["wts"], 16)
                sp.wait_ge(s["zeroed"], 2)
                sp.dma_start(wq[:, :, 0:L0F], w["L0_attn_Wq"].rearrange("p (h f) -> p h f", f=L0F)).then_inc(s["wts"], 16)
                sp.dma_start(wk[:, :, 0:L0F], w["L0_attn_Wk"].rearrange("p (h f) -> p h f", f=L0F)).then_inc(s["wts"], 16)
                load_ahead(sp, later)

            @block.gpsimd
            def _(pool):
                pool.memset(wq[:, :, :], 0.0).then_inc(s["zeroed"], 1)
                pool.memset(wk[:, :, :], 0.0).then_inc(s["zeroed"], 1)
                pool.memset(v[:, :, :, 1, :], 1.0).then_inc(s["ones_v"], 1)
                pool.memset(mask[:, :], 1.0).then_inc(s["mask_v"], 1)
                pool.wait_ge(s["mask_v"], 1)
                for t in range(NT):
                    m = mask[:, OFF[t]:OFF[t] + P]
                    pool.affine_select(out=m, in_=m, compare_op=ALU.is_ge, fill=0.0, base=0,
                                       pattern=[[1, P]], channel_multiplier=-1).then_inc(s["mask_rdy"], 1)

            @block.tensor
            def _(pe):
                ln_tensor(pe, k, s, k.x)
                pe.wait_ge(s["wts"], 64)

                def scores(i):
                    h = i % L0H
                    if i >= 2:
                        pe.wait_ge(s["squared"], 3 * (i - 1))
                    m, r = h // 4, 32 * (h % 4)
                    for t in range(NT):
                        bank, col = 3 * (i % 2) + min(t, 2), (WIDE[2] if t == 3 else 0)
                        mm = pe.matmul(ps[:, bank, col:col + WIDE[t]], kt[r:r + 32, m, P * t:P * (t + 1)],
                                       qt[r:r + 32, m, P * t:S], start=True, stop=True)
                        if t != 2:
                            mm.then_inc(s["scored"], 1)

                def values(i):
                    h = i % L0H
                    pe.wait_ge(s["masked"], i + 1)
                    if i >= 2:
                        pe.wait_ge(s["normed"], i - 1)
                    for t in range(NT):
                        mm = pe.matmul(ps[:, 6 + i % 2, P * t:S], v[:, t, h // 2, h % 2:h % 2 + 2, :],
                                       a[:, i % 2, OFF[t]:OFF[t] + WIDE[t]], start=(t == 0), stop=(t == NT - 1))
                    mm.then_inc(s["y_ps"], 1)

                for c in range(GROUP):
                    pe.wait_ge(s["xn_ready"], c + 1)
                    for n in range(NPROJ):
                        if n >= 6:
                            pe.wait_ge(s["proj_dve"] if n % 2 else s["proj_act"], c * NPROJ // 2 + (n - 6) // 2 + 1)
                        if n == 5 and c > 0:
                            pe.wait_ge(s["x_new"], c)
                        if n < 8:
                            pe.matmul(ps[:, n % 6, :], flat((wk if n % 2 else wq)[:, 4 * (n // 2):4 * (n // 2) + 4, :]),
                                      k.xn[:, c, :], start=True, stop=True).then_inc(s["proj_ps"], 1)
                        else:
                            t, half = (n - 8) // 2, n % 2
                            pe.matmul(ps[:, n % 6, :], k.xn[:, c, P * t:P * (t + 1)], wv[:, 512 * half:512 * half + 512],
                                      start=True, stop=True).then_inc(s["proj_ps"], 1)
                    pe.wait_ge(s["proj_act"], (c + 1) * NPROJ // 2)
                    pe.wait_ge(s["proj_dve"], (c + 1) * NPROJ // 2)
                    if c == 0:
                        pe.wait_ge(s["ones_v"], 1)
                    scores(c * L0H)
                    for h in range(L0H):
                        i = c * L0H + h
                        if h + 1 < L0H:
                            scores(i + 1)
                        values(i)
                    pe.wait_ge(s["normed"], (c + 1) * L0H)
                    for t in range(L0H // 2):
                        mm = pe.matmul(ps[:, 5, :], wo[:, t, :], o[:, t, :], start=(t == 0), stop=(t == L0H // 2 - 1))
                    mm.then_inc(s["out_ps"], 1)

            @block.scalar
            def _(act):
                act.preload_act_table_set(EXPLN)
                ln_scalar(act, k, s)

                def square(i):
                    if i >= 2:
                        act.wait_ge(s["y_ps"], i - 1)
                    for n, (off, wide) in enumerate(BANKCOLS):
                        act.wait_ge(s["scored"], 3 * i + n + 1)
                        act.activation(a[:, i % 2, off:off + wide], ps[:, 3 * (i % 2) + n, 0:wide], ACT.Square,
                                       bias=1.0, scale=0.25).then_inc(s["squared"], 1)

                def invert(i):
                    r = 0 if i % 2 else HD
                    act.wait_ge(s["y_ps"], i + 1)
                    if i >= 2:
                        act.wait_ge(s["normed"], i - 1)
                    act.activation(rz[r:r + HD, i % 2, :], ps[r:r + HD, 6 + i % 2, :], ACT.Ln,
                                   bias=k.eps_z[r:r + HD, 0:1]).then_inc(s["z_log"], 1)
                    act.wait_ge(s["z_log"], i + 1)
                    act.activation(rz[r:r + HD, i % 2, :], rz[r:r + HD, i % 2, :], ACT.Exp, scale=-1.0).then_inc(s["z_rec"], 1)

                for c in range(GROUP):
                    for n in range(0, NPROJ, 2):
                        act.wait_ge(s["proj_ps"], c * NPROJ + n + 1)
                        if n < 8:
                            act.activation(qt[:, n // 2, :], ps[:, n % 6, :], ACT.Copy).then_inc(s["proj_act"], 1)
                        else:
                            act.activation(v[:, (n - 8) // 2, 0:4, 0:3:2, :], ps[:, n % 6, :]
                                           .rearrange("p (a b e) -> p a b e", b=2, e=HD), ACT.Copy).then_inc(s["proj_act"], 1)
                    square(c * L0H)
                    for h in range(L0H):
                        i = c * L0H + h
                        if h + 1 < L0H:
                            square(i + 1)
                        invert(i)

            @block.vector
            def _(dve):
                ln_vector(dve, k, s, k.x, k.xn)
                for c in range(GROUP):
                    for n in range(1, NPROJ, 2):
                        dve.wait_ge(s["proj_ps"], c * NPROJ + n + 1)
                        if n < 8:
                            dve.tensor_copy(kt[:, n // 2, :], ps[:, n % 6, :]).then_inc(s["proj_dve"], 1)
                        else:
                            dve.tensor_copy(v[:, (n - 8) // 2, 4:8, 0:3:2, :], ps[:, n % 6, :]
                                            .rearrange("p (a b e) -> p a b e", b=2, e=HD)).then_inc(s["proj_dve"], 1)
                    if c == 0:
                        dve.wait_ge(s["mask_rdy"], NT)

                    def weights(i):
                        dve.wait_ge(s["squared"], 3 * (i + 1))
                        dve.scalar_tensor_tensor(a[:, i % 2, :], a[:, i % 2, :], 1.0, mask[:, :],
                                                 ALU.add, ALU.mult).then_inc(s["masked"], 1)

                    def normalise(i):
                        r = HD * (i % 2)
                        dve.wait_ge(s["z_rec"], i + 1)
                        dve.tensor_tensor(o[r:r + HD, (i % L0H) // 2, :], ps[r:r + HD, 6 + i % 2, :],
                                          rz[HD - r:P - r, i % 2, :], ALU.mult).then_inc(s["normed"], 1)

                    weights(c * L0H)
                    for h in range(L0H):
                        i = c * L0H + h
                        if h + 1 < L0H:
                            weights(i + 1)
                        normalise(i)
                    dve.wait_ge(s["out_ps"], c + 1)
                    dve.tensor_tensor(k.x[:, c, :], k.x[:, c, :], ps[:, 5, :], ALU.add).then_inc(s["x_new"], 1)


def load_ahead(sp, later):
    for weights in later:
        for dst, src in weights.moves:
            sp.dma_start(dst, src).then_inc(weights.loaded, 16)


def moe_weights(nc, ctx, name, sem, w_gate_d, gate_b_d, wa_d, wb_d, wc_d, FT, ba_d=None, bb_d=None, bc_d=None):
    sb = lambda n, sh: ctx.enter_context(nc.sbuf_tensor(name + n, sh, F32))
    mo = Bag()
    mo.loaded, mo.biased = sem, ba_d is not None
    mo.wg = sb("wg", [P, EXPERTS])
    mo.wa, mo.wb = sb("wa", [P, EXPERTS, FT * P]), sb("wb", [P, EXPERTS, FT * P])
    mo.wc = sb("wc", [P, EXPERTS, FT, P])
    moves = [(mo.wg[:, :], w_gate_d)]
    if mo.biased:
        mo.gb, mo.ba, mo.bb, mo.bc = sb("gb", [P, EXPERTS]), sb("ba", [P, EXPERTS, FT]), sb("bb", [P, EXPERTS, FT]), sb("bc", [EXPERTS, P])
        moves += [(mo.gb[:, :], gate_b_d[None, :].to_broadcast([P, EXPERTS])), (mo.ba[:, :, :], ba_d), (mo.bb[:, :, :], bb_d),
                  (mo.bc[:, :], bc_d)]
    for e in range(EXPERTS):
        moves += [(mo.wa[:, e, :], wa_d[e]), (mo.wb[:, e, :], wb_d[e]), (mo.wc[:, e, :, :], wc_d[e].rearrange("(f p) d -> p f d", p=P))]
    mo.moves, mo.dmas = moves, 16 * len(moves)
    return mo


def stage_moe(nc, k, name, mo, FT):
    STEPS = EXPERTS * FT
    biased, wg, wa, wb, wc = mo.biased, mo.wg, mo.wa, mo.wb, mo.wc
    if biased:
        gb, ba, bb, bc = mo.gb, mo.ba, mo.bb, mo.bc
    with ExitStack() as mem, Stage(nc, LN_SEMS + ROUTE_SEMS + "hid_ps silu_sb half_sb hid_sb down_ps x_new") as s:
        sb = lambda n, sh: mem.enter_context(nc.sbuf_tensor(name + n, sh, F32))
        sg, hid = sb("sg", [P, 2, S]), sb("hid", [P, 2, S])
        k.r_logit, k.r_diff, k.r_exp = [sb(n, [P, GROUP, NT, EXPERTS]) for n in ("rl", "rd", "re")]
        k.gates = sb("gates", [P, GROUP, NT, EXPERTS])
        k.r_gt, k.r_eq = [sb(n, [P, NT, EXPERTS, EXPERTS]) for n in ("rg", "rq")]
        k.r_rank, k.r_sel = [sb(n, [P, NT, EXPERTS]) for n in ("rr", "rs")]
        k.r_max, k.r_sum = [sb(n, [P, NT]) for n in ("rm", "ru")]
        k.gate_t = sb("gt", [EXPERTS, GROUP, S])
        ps = k.ps
        with nc.Block() as block:
            @block.tensor
            def _(pe):
                ln_tensor(pe, k, s, k.x)
                pe.wait_ge(mo.loaded, mo.dmas)
                for c in range(GROUP):
                    pe.wait_ge(s["xn_ready"], c + 1)
                    route_tensor_logits(pe, k, s, c, wg)
                for c in range(GROUP):
                    route_tensor_turn(pe, k, s, c)

                def up(i):
                    c, e, f = i // STEPS, i % STEPS // FT, i % FT
                    if i % STEPS == 0:
                        pe.wait_ge(s["gate_sb"], GROUP)
                    if f == 0:
                        if i >= 2 * FT:
                            pe.wait_ge(s["hid_sb"], i - FT)
                        pe.matmul(ps[:, 4 + (i // FT) % 2, :], k.ident[0:EXPERTS, e, None].to_broadcast([EXPERTS, P]),
                                  k.gate_t[:, c, :], start=True, stop=True)
                    if i >= 2:
                        pe.wait_ge(s["half_sb"], i - 1)
                    b = 2 * (i % 2)
                    pe.matmul(ps[:, b, :], wa[:, e, P * f:P * (f + 1)], k.xn[:, c, :], start=True, stop=True)
                    pe.matmul(ps[:, b + 1, :], wb[:, e, P * f:P * (f + 1)], k.xn[:, c, :], start=True,
                              stop=True).then_inc(s["hid_ps"], 1)

                def down(i):
                    c, e, f = i // STEPS, i % STEPS // FT, i % FT
                    if biased and i % STEPS == 0:
                        pe.matmul(ps[:, 6 + c, :], bc[:, :], k.gate_t[:, c, :], start=True, stop=False)
                    pe.wait_ge(s["hid_sb"], i + 1)
                    pe.matmul(ps[:, 6 + c, :], wc[:, e, f, :], hid[:, i % 2, :],
                              start=(not biased and i % STEPS == 0), stop=(i % STEPS == STEPS - 1)).then_inc(s["down_ps"], 1)

                up(0)
                for i in range(GROUP * STEPS):
                    if i + 1 < GROUP * STEPS:
                        up(i + 1)
                    down(i)

            @block.scalar
            def _(act):
                act.preload_act_table_set(EXPLN)
                ln_scalar(act, k, s)
                act.wait_ge(mo.loaded, mo.dmas)
                for c in range(GROUP):
                    route_scalar(act, k, s, c)
                for i in range(GROUP * STEPS):
                    e, f = i % STEPS // FT, i % FT
                    act.wait_ge(s["hid_ps"], i + 1)
                    if i >= 2:
                        act.wait_ge(s["hid_sb"], i - 1)
                    act.activation(sg[:, i % 2, :], ps[:, 2 * (i % 2), :], ACT.Silu,
                                   bias=(ba[:, e, f:f + 1] if biased else 0.0)).then_inc(s["silu_sb"], 1)

            @block.vector
            def _(dve):
                ln_vector(dve, k, s, k.x, k.xn)
                if biased:
                    dve.wait_ge(mo.loaded, mo.dmas)
                links = [0]
                for c in range(GROUP):
                    route_vector(dve, k, s, c, links, gb if biased else None)
                for i in range(GROUP * STEPS):
                    c, e, f = i // STEPS, i % STEPS // FT, i % FT
                    dve.wait_ge(s["silu_sb"], i + 1)
                    if biased:
                        dve.scalar_tensor_tensor(sg[:, i % 2, :], ps[:, 2 * (i % 2) + 1, :], bb[:, e, f:f + 1],
                                                 sg[:, i % 2, :], ALU.add, ALU.mult).then_inc(s["half_sb"], 1)
                    else:
                        dve.tensor_tensor(sg[:, i % 2, :], sg[:, i % 2, :], ps[:, 2 * (i % 2) + 1, :],
                                          ALU.mult).then_inc(s["half_sb"], 1)
                    dve.wait_ge(s["half_sb"], i + 1)
                    if i >= 2:
                        dve.wait_ge(s["down_ps"], i - 1)
                    dve.tensor_tensor(hid[:, i % 2, :], sg[:, i % 2, :], ps[:, 4 + (i // FT) % 2, :],
                                      ALU.mult).then_inc(s["hid_sb"], 1)
                    if i % STEPS == 0 and c > 0:
                        dve.wait_ge(s["down_ps"], c * STEPS)
                        dve.tensor_tensor(k.x[:, c - 1, :], k.x[:, c - 1, :], ps[:, 6 + c - 1, :], ALU.add).then_inc(s["x_new"], 1)
                dve.wait_ge(s["down_ps"], GROUP * STEPS)
                dve.tensor_tensor(k.x[:, GROUP - 1, :], k.x[:, GROUP - 1, :], ps[:, 6 + GROUP - 1, :], ALU.add).then_inc(s["x_new"], 1)


def stage_softmax(nc, k, w, later):
    H, PAIRS = 16, 8
    SCALE = 1.0 / (HD * HD * H)
    UNITS = GROUP * H * 2
    UPC = H * 2
    with ExitStack() as mem, Stage(nc, LN_SEMS + "wts ones_v q_ps k_ps q_sb k_sb v_ps v_act v_dve s_ps rowmax negmax exp_sb rowinv "
                                   "p_sb pt_ps pt_act pt_dve y_ps y_sb out_ps x_new") as s:
        sb = lambda n, sh: mem.enter_context(nc.sbuf_tensor(n, sh, F32))
        wq, wk, wv = [sb(n, [P, H * HD]) for n in ("s_wq", "s_wk", "s_wv")]
        wo = sb("s_wo", [P, PAIRS, P])
        q, kk = sb("s_q", [P, 2, S]), sb("s_k", [P, 2, S])
        v = sb("s_v", [P, NT, PAIRS, 3, HD])
        pr, pt = sb("s_p", [P, 2, 2, S]), sb("s_pt", [P, 2, NT, 2 * P])
        mx, nm, rs, ri = [sb(n, [P, 2, 2]) for n in ("s_mx", "s_nm", "s_rs", "s_ri")]
        o = sb("s_o", [P, PAIRS, S])
        ps = k.ps
        with nc.Block() as block:
            @block.sync
            def _(sp):
                for n, t in enumerate((wq, wk, wv)):
                    sp.dma_start(t[:, :].rearrange("p (h d) -> p h d", h=H),
                                 w["L1_attn_kernel"][n].rearrange("h m d -> m h d")).then_inc(s["wts"], 16)
                wo_v = w["L1_attn_WO"][0].rearrange("(d q j) m -> j d q m", q=PAIRS, j=2)
                for j in range(2):
                    sp.dma_start(wo[HD * j:HD * (j + 1), :, :], wo_v[j]).then_inc(s["wts"], 16)
                load_ahead(sp, later)

            @block.gpsimd
            def _(pool):
                pool.memset(v[:, :, :, 1, :], 1.0).then_inc(s["ones_v"], 1)
                for n in range(UNITS):
                    pool.wait_ge(s["rowinv"], n + 1)
                    pool.tensor_tensor(pr[:, n % 2, :, :], pr[:, n % 2, :, :], ri[:, n % 2, :, None].to_broadcast([P, 2, S]),
                                       ALU.mult).then_inc(s["p_sb"], 1)

            @block.tensor
            def _(pe):
                ln_tensor(pe, k, s, k.x)
                pe.wait_ge(s["wts"], 80)
                pe.wait_ge(s["ones_v"], 1)
                for c in range(GROUP):
                    pe.wait_ge(s["xn_ready"], c + 1)

                def project(g, what):
                    c, p = g // PAIRS, g % PAIRS
                    if what == "q":
                        if g > 0:
                            pe.wait_ge(s["k_sb"], g)
                        pe.matmul(ps[:, 7, :], wq[:, P * p:P * (p + 1)], k.xn[:, c, :], start=True, stop=True).then_inc(s["q_ps"], 1)
                    else:
                        pe.wait_ge(s["q_sb"], g + 1)
                        pe.matmul(ps[:, 7, :], wk[:, P * p:P * (p + 1)], k.xn[:, c, :], start=True, stop=True).then_inc(s["k_ps"], 1)

                def values_in(c):
                    for n in range(2 * NT):
                        if n < 2:
                            if c > 0:
                                pe.wait_ge(s["y_sb"], c * UPC)
                                pe.wait_ge(s["k_sb"], min(c * PAIRS + 1, GROUP * PAIRS))
                            else:
                                pe.wait_ge(s["k_sb"], 1)
                        else:
                            pe.wait_ge(s["v_dve"] if n % 2 else s["v_act"], c * NT + (n - 2) // 2 + 1)
                        t, half = n // 2, n % 2
                        pe.matmul(ps[:, 6 + half, :], k.xn[:, c, P * t:P * (t + 1)], wv[:, 512 * half:512 * half + 512],
                                  start=True, stop=True).then_inc(s["v_ps"], 1)

                def scores(n):
                    g, j, u = n // 4, n // 2 % 2, n % 2
                    if n % 4 == 0:
                        pe.wait_ge(s["q_sb"], g + 1)
                        pe.wait_ge(s["k_sb"], g + 1)
                    if n >= 2:
                        pe.wait_ge(s["exp_sb"], 2 * (n - 1))
                    for r in range(2):
                        tile = 2 * u + r
                        mm = pe.matmul(ps[:, 2 * (n % 2) + r, :], q[HD * j:HD * (j + 1), g % 2, P * tile:P * (tile + 1)],
                                       kk[HD * j:HD * (j + 1), g % 2, :], start=True, stop=True)
                    mm.then_inc(s["s_ps"], 1)

                def turn(n):
                    pe.wait_ge(s["p_sb"], n + 1)
                    if n >= 1:
                        pe.wait_ge(s["pt_act"], n)
                        pe.wait_ge(s["pt_dve"], n)
                    for t in range(NT):
                        for r in range(2):
                            mm = pe.transpose(ps[:, 4 + t // 2, 2 * P * (t % 2) + P * r:2 * P * (t % 2) + P * (r + 1)],
                                              pr[:, n % 2, r, P * t:P * (t + 1)], k.ident[:, :])
                    mm.then_inc(s["pt_ps"], 1)

                def outputs(n):
                    c, h = n // UPC, n // 2 % H
                    if n % UPC == 0:
                        values_in(c)
                        pe.wait_ge(s["v_act"], (c + 1) * NT)
                        pe.wait_ge(s["v_dve"], (c + 1) * NT)
                    pe.wait_ge(s["pt_act"], n + 1)
                    pe.wait_ge(s["pt_dve"], n + 1)
                    if n >= 2:
                        pe.wait_ge(s["y_sb"], n - 1)
                    for t in range(NT):
                        mm = pe.matmul(ps[:, 6, 2 * P * (n % 2):2 * P * (n % 2 + 1)], v[:, t, h // 2, h % 2:h % 2 + 2, :],
                                       pt[:, n % 2, t, :], start=(t == 0), stop=(t == NT - 1))
                    mm.then_inc(s["y_ps"], 1)

                def project_out(c):
                    pe.wait_ge(s["y_sb"], (c + 1) * UPC)
                    for p in range(PAIRS):
                        mm = pe.matmul(ps[:, 6, :], wo[:, p, :], o[:, p, :], start=(p == 0), stop=(p == PAIRS - 1))
                    mm.then_inc(s["out_ps"], 1)
                    pe.wait_ge(s["x_new"], c + 1)

                project(0, "q")
                project(0, "k")
                scores(0)
                scores(1)
                for n in range(UNITS):
                    if n % 4 == 0 and n // 4 + 1 < GROUP * PAIRS and n % UPC:
                        project(n // 4 + 1, "q")
                    if n % 4 == 1 and n // 4 + 1 < GROUP * PAIRS:
                        if n % UPC == 1:
                            project(n // 4 + 1, "q")
                        project(n // 4 + 1, "k")
                    turn(n)
                    if n + 2 < UNITS:
                        scores(n + 2)
                    outputs(n)
                    if n % UPC == UPC - 1:
                        project_out(n // UPC)

            @block.scalar
            def _(act):
                act.preload_act_table_set(EXPLN)
                ln_scalar(act, k, s)

                def q_out(g):
                    act.wait_ge(s["q_ps"], g + 1)
                    act.activation(q[:, g % 2, :], ps[:, 7, :], ACT.Copy).then_inc(s["q_sb"], 1)

                def exps(n):
                    act.wait_ge(s["negmax"], n + 1)
                    if n >= 2:
                        act.wait_ge(s["pt_ps"], n - 1)
                    for r in range(2):
                        act.activation(pr[:, n % 2, r, :], ps[:, 2 * (n % 2) + r, :], ACT.Exp, bias=nm[:, n % 2, r:r + 1],
                                       scale=SCALE, accum_out=rs[:, n % 2, r:r + 1]).then_inc(s["exp_sb"], 1)

                q_out(0)
                exps(0)
                for n in range(UNITS):
                    if n + 1 < UNITS:
                        exps(n + 1)
                    if n % 4 == 0 and n // 4 + 1 < GROUP * PAIRS and n % UPC:
                        q_out(n // 4 + 1)
                    if n % UPC == 1 and n // 4 + 1 < GROUP * PAIRS:
                        q_out(n // 4 + 1)
                    act.wait_ge(s["pt_ps"], n + 1)
                    if n >= 2:
                        act.wait_ge(s["y_ps"], n - 1)
                    act.activation(flat(pt[:, n % 2, 0:2, :]), ps[:, 4, :], ACT.Copy).then_inc(s["pt_act"], 1)
                    if n % UPC == 0:
                        for t in range(NT):
                            act.wait_ge(s["v_ps"], n // UPC * 2 * NT + 2 * t + 1)
                            act.activation(v[:, t, 0:4, 0:3:2, :], ps[:, 6, :].rearrange("p (a b e) -> p a b e", b=2, e=HD),
                                           ACT.Copy).then_inc(s["v_act"], 1)

            @block.vector
            def _(dve):
                ln_vector(dve, k, s, k.x, k.xn)

                def k_out(g):
                    dve.wait_ge(s["k_ps"], g + 1)
                    dve.tensor_copy(kk[:, g % 2, :], ps[:, 7, :]).then_inc(s["k_sb"], 1)

                def row_max(n):
                    dve.wait_ge(s["s_ps"], n + 1)
                    if n >= 2:
                        dve.wait_ge(s["exp_sb"], 2 * (n - 1))
                    dve.tensor_reduce(mx[:, n % 2, :], ps[:, 2 * (n % 2):2 * (n % 2) + 2, :], AX.X, ALU.max).then_inc(s["rowmax"], 1)
                    dve.wait_ge(s["rowmax"], n + 1)
                    dve.tensor_scalar(nm[:, n % 2, :], mx[:, n % 2, :], -SCALE, None, ALU.mult).then_inc(s["negmax"], 1)

                def row_inv(n):
                    dve.wait_ge(s["exp_sb"], 2 * (n + 1))
                    if n >= 2:
                        dve.wait_ge(s["p_sb"], n - 1)
                    dve.reciprocal(ri[:, n % 2, :], rs[:, n % 2, :]).then_inc(s["rowinv"], 1)

                k_out(0)
                row_max(0)
                row_inv(0)
                row_max(1)
                for n in range(UNITS):
                    if n + 1 < UNITS:
                        row_inv(n + 1)
                    if n % 4 == 1 and n // 4 + 1 < GROUP * PAIRS:
                        k_out(n // 4 + 1)
                    dve.wait_ge(s["pt_ps"], n + 1)
                    if n >= 2:
                        dve.wait_ge(s["y_ps"], n - 1)
                    dve.tensor_copy(flat(pt[:, n % 2, 2:4, :]), ps[:, 5, :]).then_inc(s["pt_dve"], 1)
                    if n + 2 < UNITS:
                        row_max(n + 2)
                    if n % UPC == 0:
                        for t in range(NT):
                            dve.wait_ge(s["v_ps"], n // UPC * 2 * NT + 2 * t + 2)
                            dve.tensor_copy(v[:, t, 4:8, 0:3:2, :], ps[:, 7, :].rearrange("p (a b e) -> p a b e", b=2, e=HD))\
                               .then_inc(s["v_dve"], 1)
                    h, u = n // 2 % H, n % 2
                    r = HD * (h % 2)
                    dve.wait_ge(s["y_ps"], n + 1)
                    dve.tensor_copy(o[r:r + HD, h // 2, 2 * P * u:2 * P * (u + 1)], ps[r:r + HD, 6, 2 * P * u:2 * P * (u + 1)])\
                       .then_inc(s["y_sb"], 1)
                    if n % UPC == UPC - 1:
                        c = n // UPC
                        dve.wait_ge(s["out_ps"], c + 1)
                        dve.tensor_tensor(k.x[:, c, :], k.x[:, c, :], ps[:, 6, :], ALU.add).then_inc(s["x_new"], 1)


def local_weights(nc, ctx, k, w, layer, sem):
    wsb = lambda n, sh: ctx.enter_context(nc.sbuf_tensor(n + str(layer), sh, F32))
    if layer == 0:
        k.rot = wsb("rot", [P, 4, S])
    wl = Bag()
    wl.v = wsb("lw_v", [P, 512])
    wl.qk = wsb("lw_qk", [P, 1024])
    wl.qkr = wsb("lw_qkr", [P, 1024])
    wl.o = wsb("lw_o", [P, 4, P])
    wl.up = wsb("lw_up", [P, 2 * HID])
    wl.down = wsb("lw_down", [P, 3, P])
    wl.scales = wsb("lw_sc", [P, 4])
    wl.b1 = wsb("lw_b1", [P, 6])
    wl.ln = wsb("lw_ln", [P, 3])
    wl.loaded = sem
    moves = [(wl.v[:, :], w["L1_ffn_wqkv"][layer, :, 1024:1536]), (wl.qk[:, :], w["L1_ffn_wqkv"][layer, :, 0:1024]),
             (wl.qkr[:, :], w["L1_qk_rot"][layer]), (wl.o[:, :, :], w["L1_ffn_wo"][layer].rearrange("(t p) d -> p t d", p=P)),
             (wl.up[:, :], w["L1_ffn_w1"][layer]), (wl.scales[:, :], w["L1_scales"][layer]), (wl.ln[:, :], w["L1_ln"][layer])]
    for f, (off, n) in enumerate(HT):
        moves += [(wl.down[0:n, f, :], w["L1_ffn_w2"][layer, off:off + n, :])]
        for half in range(2):
            moves += [(wl.b1[0:n, 3 * half + f:3 * half + f + 1],
                       w["L1_ffn_b1"][layer, HID * half + off:HID * half + off + n][:, None])]
    if layer == 0:
        moves += [(k.rot[:, :, :], w["rot_tables"])]
    wl.moves, wl.dmas = moves, 16 * len(moves)
    return wl


def stage_local(nc, k, w, wl, layer):
    HPAIRS = LH // 2
    BACK = WIN
    KW = P + BACK
    QK_SCALE = 8.0
    TILES = 2 * HPAIRS
    last = layer == 1
    with ExitStack() as mem, Stage(nc, (LN_SEMS if layer == 0 else "ln_mean ln_xc ln_sq ln_var ln_log ln_rstd xn_ready ") +
                                   "window padded parts_zero root_log rpart0 rrest rpart1 masked_rdy folded shifted v_ps v_act v_dve qk_ps sq_sb cos_sb sin_sb raw_sb norm_ps ss_sb "
                                   "root_sb rn_sb bc_ps qk_sb s_ps s_sb rowmax centred exp_sb pt_ps pta_sb ptb_sb "
                                   "o_ps sumlog suminv o_sb out_ps y_new shifted2 hn_pre hn_sb up_ps gelu_sb hid_sb down_ps y_end x_new") as s:
        sb = lambda n, sh: mem.enter_context(nc.sbuf_tensor(n + str(layer), sh, F32))
        hs = sb("c_hs", [P, GROUP, BACK + S])
        v = sb("c_v", [P, NT + 1, HPAIRS, 3, LD])
        qq, kp = sb("c_q", [P, HPAIRS, S]), sb("c_k", [P, HPAIRS, BACK + S])
        raw = sb("c_raw", [P, TILES, S])
        sq, sinp = sb("c_sq", [P, 2, S]), sb("c_sin", [P, 2, S])
        rn = sb("c_rn", [2 * TILES, 2, S])
        rparts = mem.enter_context(nc.sbuf_tensor("c_rparts" + str(layer), [64 + 2 * TILES, S], BF16))
        rmid = mem.enter_context(nc.sbuf_tensor("c_rmid" + str(layer), [2 * TILES, S], BF16))
        tab = sb("c_tab", [P, 4, S])
        mask = sb("c_mask", [P, NT, KW])
        sc, mx = sb("c_s", [P, 3, NT, KW]), sb("c_mx", [P, 3, NT])
        pta, ptb = sb("c_pta", [P, 2, S]), sb("c_ptb", [BACK, 2, S])
        o, si = sb("c_o", [P, HPAIRS, S]), sb("c_si", [P, S])
        hn, ge, hid = sb("c_hn", [P, GROUP, S]), sb("c_ge", [P, 2, S]), sb("c_hid", [P, 3, S])
        ps, y = k.ps, k.y
        with nc.Block() as block:
            @block.gpsimd
            def _(pool):
                pool.memset(hs[:, :, 0:BACK + 1], 0.0).then_inc(s["window"], 1)
                pool.memset(kp[:, :, 0:BACK], 0.0).then_inc(s["padded"], 1)
                pool.memset(rparts[:, :], 0.0).then_inc(s["parts_zero"], 1)
                pool.wait_ge(s["parts_zero"], 1)
                pool.memset(v[:, NT, :, 0:3:2, :], 0.0).then_inc(s["padded"], 1)
                pool.memset(v[:, :, :, 1, :], 1.0).then_inc(s["padded"], 1)
                pool.memset(mask[:, :, :], 0.0).then_inc(s["padded"], 1)
                pool.wait_ge(s["padded"], 4)
                pool.affine_select(out=mask[:, :, :], in_=mask[:, :, :], compare_op=ALU.is_ge, fill=-1e30, base=0,
                                   pattern=[[0, NT], [1, KW]], channel_multiplier=-1).then_inc(s["masked_rdy"], 1)
                pool.wait_ge(s["masked_rdy"], 1)
                pool.affine_select(out=mask[:, :, :], in_=mask[:, :, :], compare_op=ALU.is_ge, fill=-1e30, base=WIN,
                                   pattern=[[0, NT], [-1, KW]], channel_multiplier=1).then_inc(s["masked_rdy"], 1)
                pool.wait_ge(s["masked_rdy"], 2)
                pool.affine_select(out=mask[:, 0, :], in_=mask[:, 0, :], compare_op=ALU.is_ge, fill=-1e30, base=-BACK,
                                   pattern=[[1, KW]], channel_multiplier=0).then_inc(s["masked_rdy"], 1)
                pool.wait_ge(wl.loaded, wl.dmas)
                for n in range(4):
                    pool.tensor_scalar(tab[:, n, :], k.rot[:, n, :], wl.scales[:, n:n + 1], None, ALU.mult).then_inc(s["folded"], 1)

                for c in range(GROUP):
                    for m in range(TILES):
                        i = c * TILES + m
                        pool.wait_ge(s["sin_sb"], i + 1)
                        if m == 0 and c > 0:
                            pool.wait_ge(s["qk_sb"], c * TILES)
                        pool.tensor_tensor(raw[:, m, :], raw[:, m, :], sinp[:, i % 2, :], ALU.add).then_inc(s["raw_sb"], 1)
                    for h in range(LH):
                        i = c * LH + h
                        pool.wait_ge(s["rowmax"], i + 1)
                        pool.tensor_tensor(sc[:, i % 3, :, :], sc[:, i % 3, :, :],
                                           mx[:, i % 3, :, None].to_broadcast([P, NT, KW]), ALU.subtract).then_inc(s["centred"], 1)

            @block.tensor
            def _(pe):
                if layer == 0:
                    ln_tensor(pe, k, s, k.x)
                pe.wait_ge(s["padded"], 4)
                pe.wait_ge(wl.loaded, wl.dmas)
                for c in range(GROUP):
                    pe.wait_ge(s["shifted"], 2 * (c + 1))
                    if c > 0:
                        pe.wait_ge(s["y_new"], c)
                    for t in range(NT + 1):
                        rows = P if t < NT else BACK
                        pe.matmul(ps[0:rows, t, :], hs[:, c, P * t:P * t + rows], wl.v[:, :], start=True, stop=True).then_inc(s["v_ps"], 1)
                    for m in range(TILES):
                        i = c * TILES + m
                        if m == 0:
                            pe.wait_ge(s["v_act"], (c + 1) * 3)
                            pe.wait_ge(s["v_dve"], (c + 1) * 2)
                        if m >= 2:
                            pe.wait_ge(s["sin_sb"], i - 1)
                            pe.wait_ge(s["sq_sb"], i - 1)
                        b = 2 * (m % 2)
                        pe.matmul(ps[:, b, :], wl.qk[:, P * m:P * (m + 1)], hs[:, c, BACK:BACK + S], start=True, stop=True)
                        pe.matmul(ps[:, b + 1, :], wl.qkr[:, P * m:P * (m + 1)], hs[:, c, BACK:BACK + S], start=True,
                                  stop=True).then_inc(s["qk_ps"], 1)
                        if m >= 1:
                            pe.wait_ge(s["sq_sb"], i)
                            pe.matmul(ps[0:2 * TILES, 5, :], k.head_sel[:, m - 1, :], sq[:, (i - 1) % 2, :], start=(m == 1),
                                      stop=False).then_inc(s["norm_ps"], 1)
                    i = (c + 1) * TILES - 1
                    pe.wait_ge(s["sq_sb"], i + 1)
                    pe.matmul(ps[0:2 * TILES, 5, :], k.head_sel[:, TILES - 1, :], sq[:, i % 2, :], start=False,
                              stop=True).then_inc(s["norm_ps"], 1)
                    pe.wait_ge(s["rn_sb"], 2 * (c + 1))
                    for m in range(TILES):
                        i = c * TILES + m
                        if m >= 2:
                            pe.wait_ge(s["qk_sb"], i - 1)
                        pe.matmul(ps[:, 6 + m % 2, :], k.head_sel3[:, m, :], rparts[:, :], start=True, stop=True).then_inc(s["bc_ps"], 1)
                    pe.wait_ge(s["qk_sb"], (c + 1) * TILES)

                    def scores(h):
                        i = c * LH + h
                        m, r = h // 2, LD * (h % 2)
                        if h >= 2:
                            pe.wait_ge(s["s_sb"], i - 1)
                        for t in range(NT):
                            mm = pe.matmul(ps[:, 2 * (i % 2) + t // 2, KW * (t % 2):KW * (t % 2 + 1)],
                                           qq[r:r + LD, m, P * t:P * (t + 1)], kp[r:r + LD, m, P * t:P * t + KW],
                                           start=True, stop=True)
                        mm.then_inc(s["s_ps"], 1)

                    def turn(h):
                        i = c * LH + h
                        pe.wait_ge(s["exp_sb"], i + 1)
                        if h >= 1:
                            pe.wait_ge(s["pta_sb"], i)
                            pe.wait_ge(s["ptb_sb"], i)
                        for t in range(NT):
                            pe.transpose(ps[:, 4, P * t:P * (t + 1)], sc[:, i % 3, t, 0:P], k.ident[:, :])
                            mm = pe.transpose(ps[0:BACK, 5, P * t:P * (t + 1)], sc[:, i % 3, t, P:KW], k.ident[:, :])
                        mm.then_inc(s["pt_ps"], 1)

                    def context(h):
                        i = c * LH + h
                        pe.wait_ge(s["pta_sb"], i + 1)
                        pe.wait_ge(s["ptb_sb"], i + 1)
                        if h >= 2:
                            pe.wait_ge(s["o_sb"], i - 1)
                        for t in range(NT):
                            vv = v[:, t, h // 2, h % 2:h % 2 + 2, :]
                            pe.matmul(ps[:, 6 + i % 2, P * t:P * (t + 1)], vv, pta[:, i % 2, P * t:P * (t + 1)], start=True, stop=False)
                            mm = pe.matmul(ps[:, 6 + i % 2, P * t:P * (t + 1)], v[0:BACK, t + 1, h // 2, h % 2:h % 2 + 2, :],
                                           ptb[:, i % 2, P * t:P * (t + 1)], start=False, stop=True)
                        mm.then_inc(s["o_ps"], 1)

                    scores(0)
                    scores(1)
                    turn(0)
                    for h in range(LH):
                        if h + 2 < LH:
                            scores(h + 2)
                        if h + 1 < LH:
                            turn(h + 1)
                        context(h)
                    pe.wait_ge(s["o_sb"], (c + 1) * LH)
                    for p in range(HPAIRS):
                        mm = pe.matmul(ps[:, 0, :], wl.o[:, p, :], o[:, p, :], start=(p == 0), stop=(p == HPAIRS - 1))
                    mm.then_inc(s["out_ps"], 1)
                base = GROUP if layer == 0 else 0
                for c in range(GROUP):
                    pe.wait_ge(s["shifted2"], 2 * (c + 1))
                    pe.matmul(ps[:, 6 + c, :], k.mean_mat[:, :], hs[:, c, BACK:BACK + S], start=True, stop=True).then_inc(s["ln_mean"], 1)
                for c in range(GROUP):
                    pe.wait_ge(s["ln_sq"], base + c + 1)
                    pe.matmul(ps[:, 6 + c, :], k.mean_mat[:, :], k.sq[:, c, :], start=True, stop=True).then_inc(s["ln_var"], 1)
                for c in range(GROUP):
                    pe.wait_ge(s["hn_sb"], c + 1)
                    for f, (off, n) in enumerate(HT):
                        i = c * 3 + f
                        if c == 0 and f == 0:
                            pe.wait_ge(s["y_new"], GROUP)
                        if i >= 2:
                            pe.wait_ge(s["hid_sb"], i - 1)
                        b = 2 * (i % 2)
                        pe.matmul(ps[0:n, b, :], wl.up[:, off:off + n], hn[:, c, :], start=True, stop=True)
                        pe.matmul(ps[0:n, b + 1, :], wl.up[:, HID + off:HID + off + n], hn[:, c, :], start=True,
                                  stop=True).then_inc(s["up_ps"], 1)
                    for f, (off, n) in enumerate(HT):
                        pe.wait_ge(s["hid_sb"], c * 3 + f + 1)
                        mm = pe.matmul(ps[:, 4 + c, :], wl.down[0:n, f, :], hid[0:n, f, :], start=(f == 0), stop=(f == 2))
                    mm.then_inc(s["down_ps"], 1)

            @block.scalar
            def _(act):
                act.preload_act_table_set(EXPLN)
                if layer == 0:
                    ln_scalar(act, k, s)
                act.wait_ge(wl.loaded, wl.dmas)
                for c in range(GROUP):
                    for n in range(0, NT + 1, 2):
                        rows = P if n < NT else BACK
                        act.wait_ge(s["v_ps"], c * (NT + 1) + n + 1)
                        act.activation(v[0:rows, n, :, 0:3:2, :], ps[0:rows, n, :].rearrange("p (a b e) -> p a b e", b=2, e=LD),
                                       ACT.Copy).then_inc(s["v_act"], 1)
                    for m in range(TILES):
                        i = c * TILES + m
                        act.wait_ge(s["cos_sb"], i + 1)
                        if i >= 2:
                            act.wait_ge(s["norm_ps"], i - 1)
                        act.activation(sq[:, i % 2, :], ps[:, 2 * (m % 2), :], ACT.Square).then_inc(s["sq_sb"], 1)
                    act.wait_ge(s["ss_sb"], c + 1)
                    act.activation(rn[:, 0, :], rn[:, 0, :], ACT.Ln).then_inc(s["root_log"], 1)
                    act.wait_ge(s["root_log"], c + 1)
                    act.activation(rn[:, 1, :], rn[:, 0, :], ACT.Exp, scale=-0.5).then_inc(s["root_sb"], 1)

                    def exponent(h):
                        i = c * LH + h
                        act.wait_ge(s["centred"], i + 1)
                        act.activation(sc[:, i % 3, :, :], sc[:, i % 3, :, :], ACT.Exp, scale=QK_SCALE).then_inc(s["exp_sb"], 1)

                    def copy_turned(h):
                        i = c * LH + h
                        act.wait_ge(s["pt_ps"], i + 1)
                        act.activation(pta[:, i % 2, :], ps[:, 4, :], ACT.Copy).then_inc(s["pta_sb"], 1)

                    exponent(0)
                    exponent(1)
                    copy_turned(0)
                    for h in range(LH):
                        i = c * LH + h
                        if h + 2 < LH:
                            exponent(h + 2)
                        if h + 1 < LH:
                            copy_turned(h + 1)
                        r, t = LD * (h % 2), LD * (1 - h % 2)
                        act.wait_ge(s["o_ps"], i + 1)
                        if i >= 2:
                            act.wait_ge(s["o_sb"], i - 1)
                        act.activation(si[r:r + LD, :], ps[t:t + LD, 6 + i % 2, :], ACT.Ln).then_inc(s["sumlog"], 1)
                        act.wait_ge(s["sumlog"], i + 1)
                        act.activation(si[r:r + LD, :], si[r:r + LD, :], ACT.Exp, scale=-1.0).then_inc(s["suminv"], 1)
                base = GROUP if layer == 0 else 0
                for c in range(GROUP):
                    act.wait_ge(s["ln_xc"], base + c + 1)
                    act.activation(k.sq[:, c, :], k.xc[:, c, :], ACT.Square).then_inc(s["ln_sq"], 1)
                for c in range(GROUP):
                    act.wait_ge(s["ln_var"], base + c + 1)
                    act.activation(k.sq[:, c, :], ps[:, 6 + c, :], ACT.Ln, bias=k.eps[:, 0:1]).then_inc(s["ln_log"], 1)
                    act.wait_ge(s["ln_log"], base + c + 1)
                    act.activation(k.sq[:, c, :], k.sq[:, c, :], ACT.Exp, scale=-0.5).then_inc(s["ln_rstd"], 1)
                for i in range(3 * GROUP):
                    f = i % 3
                    n = HT[f][1]
                    act.wait_ge(s["up_ps"], i + 1)
                    if i >= 2:
                        act.wait_ge(s["hid_sb"], i - 1)
                    act.activation(ge[0:n, i % 2, :], ps[0:n, 2 * (i % 2) + 1, :], ACT.Gelu,
                                   bias=wl.b1[0:n, 3 + f:4 + f]).then_inc(s["gelu_sb"], 1)

            @block.vector
            def _(dve):
                if layer == 0:
                    ln_vector(dve, k, s, k.x, y)
                def shift(c, done):
                    dve.tensor_copy(hs[0:64, c, BACK:BACK + S], y[0:64, c, :]).then_inc(s[done], 1)
                    dve.tensor_copy(hs[64:P, c, BACK + 1:BACK + S], y[64:P, c, 0:S - 1]).then_inc(s[done], 1)

                dve.wait_ge(s["window"], 1)
                for c in range(GROUP):
                    if layer == 0:
                        dve.wait_ge(s["xn_ready"], c + 1)
                    shift(c, "shifted")
                dve.wait_ge(wl.loaded, wl.dmas)
                dve.wait_ge(s["padded"], 4)
                for c in range(GROUP):
                    for n in range(1, NT + 1, 2):
                        dve.wait_ge(s["v_ps"], c * (NT + 1) + n + 1)
                        dve.tensor_copy(v[:, n, :, 0:3:2, :], ps[:, n, :].rearrange("p (a b e) -> p a b e", b=2, e=LD))\
                           .then_inc(s["v_dve"], 1)
                    for m in range(TILES):
                        i = c * TILES + m
                        dve.wait_ge(s["qk_ps"], i + 1)
                        if m == 0:
                            dve.wait_ge(s["folded"], 4)
                        if i >= 2:
                            dve.wait_ge(s["raw_sb"], i - 1)
                        kind = 2 * (m >= HPAIRS)
                        dve.tensor_tensor(raw[:, m, :], ps[:, 2 * (m % 2), :], tab[:, kind, :], ALU.mult).then_inc(s["cos_sb"], 1)
                        dve.tensor_tensor(sinp[:, i % 2, :], ps[:, 2 * (m % 2) + 1, :], tab[:, kind + 1, :], ALU.mult)\
                           .then_inc(s["sin_sb"], 1)
                    dve.wait_ge(s["norm_ps"], (c + 1) * TILES)
                    dve.tensor_scalar(rn[:, 0, :], ps[0:2 * TILES, 5, :], 1e-24, None, ALU.max).then_inc(s["ss_sb"], 1)
                    dve.wait_ge(s["root_sb"], c + 1)
                    if c == 0:
                        dve.wait_ge(s["parts_zero"], 1)
                    dve.tensor_copy(rparts[0:2 * TILES, :], rn[:, 1, :]).then_inc(s["rpart0"], 1)
                    dve.wait_ge(s["rpart0"], c + 1)
                    dve.tensor_tensor(rn[:, 0, :], rn[:, 1, :], rparts[0:2 * TILES, :], ALU.subtract).then_inc(s["rrest"], 1)
                    dve.wait_ge(s["rrest"], c + 1)
                    dve.tensor_copy(rmid[:, :], rn[:, 0, :]).then_inc(s["rpart1"], 1)
                    dve.wait_ge(s["rpart1"], c + 1)
                    dve.tensor_copy(rparts[32:32 + 2 * TILES, :], rmid[:, :]).then_inc(s["rn_sb"], 1)
                    dve.tensor_tensor(rparts[64:64 + 2 * TILES, :], rn[:, 0, :], rmid[:, :], ALU.subtract).then_inc(s["rn_sb"], 1)
                    for m in range(TILES):
                        i = c * TILES + m
                        dve.wait_ge(s["bc_ps"], i + 1)
                        dve.wait_ge(s["raw_sb"], i + 1)
                        dst = qq[:, m, :] if m < HPAIRS else kp[:, m - HPAIRS, BACK:BACK + S]
                        dve.tensor_tensor(dst, raw[:, m, :], ps[:, 6 + m % 2, :], ALU.mult).then_inc(s["qk_sb"], 1)
                    if c == 0:
                        dve.wait_ge(s["masked_rdy"], 3)

                    def mask_max(h):
                        i = c * LH + h
                        dve.wait_ge(s["s_ps"], i + 1)
                        if i >= 3:
                            dve.wait_ge(s["pt_ps"], i - 2)
                        dve.tensor_tensor(sc[:, i % 3, :, :].rearrange("p (a b) k -> p a b k", b=2),
                                          ps[:, 2 * (i % 2):2 * (i % 2) + 2, 0:2 * KW].rearrange("p a (b k) -> p a b k", b=2),
                                          mask[:, :, :].rearrange("p (a b) k -> p a b k", b=2), ALU.add).then_inc(s["s_sb"], 1)
                        dve.wait_ge(s["s_sb"], i + 1)
                        dve.tensor_reduce(mx[:, i % 3, :], sc[:, i % 3, :, :], AX.X, ALU.max).then_inc(s["rowmax"], 1)

                    def copy_turned(h):
                        i = c * LH + h
                        dve.wait_ge(s["pt_ps"], i + 1)
                        dve.tensor_copy(ptb[:, i % 2, :], ps[0:BACK, 5, :]).then_inc(s["ptb_sb"], 1)

                    def normalise(h):
                        i = c * LH + h
                        dve.wait_ge(s["suminv"], i + 1)
                        r = LD * (h % 2)
                        dve.tensor_tensor(o[r:r + LD, h // 2, :], ps[r:r + LD, 6 + i % 2, :], si[r:r + LD, :],
                                          ALU.mult).then_inc(s["o_sb"], 1)

                    mask_max(0)
                    mask_max(1)
                    copy_turned(0)
                    for h in range(LH):
                        if h + 2 < LH:
                            mask_max(h + 2)
                        if h + 1 < LH:
                            copy_turned(h + 1)
                        normalise(h)
                    dve.wait_ge(s["out_ps"], c + 1)
                    dve.tensor_tensor(y[:, c, :], y[:, c, :], ps[:, 0, :], ALU.add).then_inc(s["y_new"], 1)
                    dve.wait_ge(s["y_new"], c + 1)
                    shift(c, "shifted2")
                base = GROUP if layer == 0 else 0
                for c in range(GROUP):
                    dve.wait_ge(s["ln_mean"], base + c + 1)
                    dve.tensor_tensor(k.xc[:, c, :], hs[:, c, BACK:BACK + S], ps[:, 6 + c, :], ALU.subtract).then_inc(s["ln_xc"], 1)
                for c in range(GROUP):
                    dve.wait_ge(s["ln_rstd"], base + c + 1)
                    dve.tensor_tensor(k.xc[:, c, :], k.xc[:, c, :], k.sq[:, c, :], ALU.mult).then_inc(s["hn_pre"], 1)
                    dve.wait_ge(s["hn_pre"], c + 1)
                    dve.tensor_scalar(hn[:, c, :], k.xc[:, c, :], wl.ln[:, 0:1], wl.ln[:, 1:2], ALU.mult, ALU.add).then_inc(s["hn_sb"], 1)
                for c in range(GROUP):
                    for f, (off, n) in enumerate(HT):
                        i = c * 3 + f
                        dve.wait_ge(s["gelu_sb"], i + 1)
                        if f == 0 and c > 0:
                            dve.wait_ge(s["down_ps"], c)
                        dve.scalar_tensor_tensor(hid[0:n, f, :], ps[0:n, 2 * (i % 2), :], wl.b1[0:n, f:f + 1], ge[0:n, i % 2, :],
                                                 ALU.add, ALU.mult).then_inc(s["hid_sb"], 1)
                    dve.wait_ge(s["down_ps"], c + 1)
                    dve.scalar_tensor_tensor(y[:, c, :], ps[:, 4 + c, :], wl.ln[:, 2:3], y[:, c, :], ALU.add, ALU.add)\
                       .then_inc(s["y_end"], 1)
                    if last:
                        dve.wait_ge(s["y_end"], c + 1)
                        dve.tensor_tensor(k.x[:, c, :], k.x[:, c, :], y[:, c, :], ALU.add).then_inc(s["x_new"], 1)


def stage_ln_y(nc, k):
    with Stage(nc, LN_SEMS) as s:
        with nc.Block() as block:
            @block.tensor
            def _(pe):
                ln_tensor(pe, k, s, k.x)

            @block.scalar
            def _(act):
                act.preload_act_table_set(EXPLN)
                ln_scalar(act, k, s)

            @block.vector
            def _(dve):
                ln_vector(dve, k, s, k.x, k.y)


def stage_mamba(nc, k, mw, m, scan):
    NG4 = NS // NGR
    UPC = NG4 * ET
    UNITS = GROUP * UPC
    PADT = TAPS - 1
    CHUNK = (1, 0) if scan else (0,)
    NQ = len(CHUNK)
    ps, y = k.ps, k.y
    AHEAD = 1
    CARRIED = 2 * NGR - 1
    ROW0 = CARRIED if scan else 0
    Q1 = UPC + 1
    ROWS = GROUP * NG4 * NGR
    SKIP = (25, 26)

    LAST_ROWS = (ROWS + CARRIED - len(SKIP), ROWS + CARRIED)

    def rows_at(place):
        if place in SKIP:
            return ()
        return (ROW0 + place - len(SKIP) * (place > SKIP[-1]),)

    PREP, STAGE_B = 7, 6
    with Stage(nc, "rms_sq rms_ps rms_log rms_rstd u_sb x_ps xs_sb tap0 tap_sb z_raw z_sb xc_sb dbc_ps part0 dts_sb rest part1 parts dt_ps "
                   "dt_abs dt_exp dt_log delta_sb dx_sb b_ps b_sb c_ps da_sb bx_sb h_sb hc_sb y_ps y_skip yg_sb out_ps y_new") as s:
        with nc.Block() as block:
            def p_mean(pe, q):
                pe.wait_ge(s["rms_sq"], q + 1)
                if q:
                    pe.wait_ge(s["dt_abs"], q * ET)
                pe.matmul(ps[:, PREP, :], k.mean_mat[:, :], k.sq[:, CHUNK[q], :], start=True, stop=True).then_inc(s["rms_ps"], 1)

            def p_x(pe, q, n):
                if n == 0:
                    pe.wait_ge(s["u_sb"], q + 1)
                elif n < 3:
                    pe.wait_ge(s["xs_sb"], q * ET + n)
                else:
                    pe.wait_ge(s["z_raw"], q * ET + 1)
                pe.matmul(ps[:, PREP, :], mw.win[:, P * n:P * (n + 1)], k.xn[:, CHUNK[q], :], start=True,
                          stop=True).then_inc(s["x_ps"], 1)

            def p_dbc(pe, q):
                pe.wait_ge(s["z_raw"], (q + 1) * ET)
                pe.wait_ge(s["z_sb"], q + 1)
                pe.wait_ge(s["xc_sb"], q + 1)
                for e in range(ET):
                    mm = pe.matmul(ps[0:RANK + 2 * NS, PREP, :], mw.wx[:, e, :], m.xc[:, CHUNK[q], e, :], start=(e == 0), stop=(e == ET - 1))
                mm.then_inc(s["dbc_ps"], 1)

            def p_dt(pe, q, e):
                if e == 0:
                    pe.wait_ge(s["dts_sb"], q + 1)
                    pe.wait_ge(s["rest"], q + 1)
                else:
                    pe.wait_ge(s["dt_abs"], q * ET + e)
                pe.matmul(ps[:, PREP, :], mw.wdt[:, P * e:P * (e + 1)], m.dts[:, :], start=True, stop=True).then_inc(s["dt_ps"], 1)

            def a_square(act, q):
                if q:
                    act.wait_ge(s["y_new"], q)
                act.activation(k.sq[:, CHUNK[q], :], y[:, CHUNK[q], :], ACT.Square).then_inc(s["rms_sq"], 1)

            def a_rstd(act, q):
                c = CHUNK[q]
                act.wait_ge(s["rms_ps"], q + 1)
                act.activation(k.sq[:, c, :], ps[:, PREP, :], ACT.Ln, bias=k.eps[:, 0:1]).then_inc(s["rms_log"], 1)
                act.wait_ge(s["rms_log"], q + 1)
                act.activation(k.sq[:, c, :], k.sq[:, c, :], ACT.Exp, scale=-0.5).then_inc(s["rms_rstd"], 1)

            def a_xs(act, q, e):
                act.wait_ge(s["x_ps"], q * 2 * ET + e + 1)
                act.activation(m.xs[:, e, PADT:PADT + S], ps[:, PREP, :], ACT.Copy).then_inc(s["xs_sb"], 1)

            def a_z(act, q, e):
                act.wait_ge(s["x_ps"], q * 2 * ET + ET + e + 1)
                act.activation(m.zg[:, CHUNK[q], e, :], ps[:, PREP, :], ACT.Copy).then_inc(s["z_raw"], 1)

            def a_silu(act, q):
                c = CHUNK[q]
                act.wait_ge(s["z_raw"], (q + 1) * ET)
                act.activation(m.zg[:, c, :, :], m.zg[:, c, :, :], ACT.Silu).then_inc(s["z_sb"], 1)
                act.wait_ge(s["tap_sb"], (q + 1) * ET * (TAPS - 1))
                act.activation(m.xc[:, c, :, :], m.cv[:, :, :], ACT.Silu).then_inc(s["xc_sb"], 1)
                act.preload_act_table_set(EXPLN)

            def a_dbc(act, q):
                act.wait_ge(s["dbc_ps"], q + 1)
                act.activation(m.parts[0:2 * NS, CHUNK[q], :], ps[RANK:RANK + 2 * NS, PREP, :], ACT.Copy).then_inc(s["part0"], 1)
                act.activation(m.dts[:, :], ps[0:RANK, PREP, :], ACT.Copy).then_inc(s["dts_sb"], 1)

            def a_dt(act, q, e):
                act.wait_ge(s["dt_ps"], q * ET + e + 1)
                act.activation(m.rl[:, e, :], ps[:, PREP, :], ACT.Relu, bias=mw.cols[:, 2, e:e + 1])
                act.activation(m.dl[:, CHUNK[q], e, :], ps[:, PREP, :], ACT.Abs, bias=mw.cols[:, 2, e:e + 1]).then_inc(s["dt_abs"], 1)

            def a_soft(act, q):
                c = CHUNK[q]
                for e in range(ET):
                    act.wait_ge(s["dt_abs"], q * ET + e + 1)
                    act.activation(m.dl[:, c, e, :], m.dl[:, c, e, :], ACT.Exp, scale=-1.0).then_inc(s["dt_exp"], 1)
                for e in range(ET):
                    act.wait_ge(s["dt_exp"], q * ET + e + 1)
                    act.activation(m.dl[:, c, e, :], m.dl[:, c, e, :], ACT.Ln, bias=1.0).then_inc(s["dt_log"], 1)

            def v_u(dve, q):
                c = CHUNK[q]
                dve.wait_ge(s["rms_rstd"], q + 1)
                dve.scalar_tensor_tensor(k.xn[:, c, :], y[:, c, :], mw.vec[:, 0:1], k.sq[:, c, :], ALU.mult, ALU.mult).then_inc(s["u_sb"], 1)

            def v_taps(dve, q, e):
                i = q * ET + e
                dve.wait_ge(s["xs_sb"], i + 1)
                dve.tensor_scalar(m.cv[:, e, :], m.xs[:, e, PADT:PADT + S], mw.taps[:, e, PADT:PADT + 1], mw.cols[:, 0, e:e + 1],
                                  ALU.mult, ALU.add).then_inc(s["tap0"], 1)
                dve.wait_ge(s["tap0"], i + 1)
                for j in range(TAPS - 1):
                    if j:
                        dve.wait_ge(s["tap_sb"], i * (TAPS - 1) + j)
                    dve.scalar_tensor_tensor(m.cv[:, e, :], m.xs[:, e, j:j + S], mw.taps[:, e, j:j + 1], m.cv[:, e, :],
                                             ALU.mult, ALU.add).then_inc(s["tap_sb"], 1)

            def v_parts(dve, q):
                c = CHUNK[q]
                dve.wait_ge(s["part0"], q + 1)
                dve.wait_ge(s["dts_sb"], q + 1)
                dve.tensor_tensor(m.rest[:, :], ps[RANK:RANK + 2 * NS, PREP, :], m.parts[0:2 * NS, c, :], ALU.subtract).then_inc(s["rest"], 1)
                dve.wait_ge(s["rest"], q + 1)
                dve.tensor_copy(m.mid[:, :], m.rest[:, :]).then_inc(s["part1"], 1)
                dve.wait_ge(s["part1"], q + 1)
                dve.tensor_copy(m.parts[2 * NS:4 * NS, c, :], m.mid[:, :]).then_inc(s["parts"], 1)
                dve.tensor_tensor(m.parts[4 * NS:6 * NS, c, :], m.rest[:, :], m.mid[:, :], ALU.subtract).then_inc(s["parts"], 1)

            def v_delta(dve, q, e):
                c, i = CHUNK[q], q * ET + e
                dve.wait_ge(s["dt_log"], i + 1)
                dve.tensor_tensor(m.dl[:, c, e, :], m.dl[:, c, e, :], m.rl[:, e, :], ALU.add).then_inc(s["delta_sb"], 1)

            def g_dx(pool, q):
                for e in range(ET):
                    pool.wait_ge(s["delta_sb"], q * ET + e + 1)
                    pool.tensor_tensor(m.dx[:, CHUNK[q], e, :], m.dl[:, CHUNK[q], e, :], m.xc[:, CHUNK[q], e, :],
                                       ALU.mult).then_inc(s["dx_sb"], 1)

            @block.gpsimd
            def _(pool):
                def state_input(u):
                    g, e = u // ET, u % ET
                    if (g + 1) * NGR > ROW0:
                        pool.wait_ge(s["b_sb"], (g + 1) * NGR - ROW0)
                    if u > 2:
                        pool.wait_ge(s["h_sb"], u - 2)
                    if u in (0, UPC, UNITS):
                        pool.wait_ge(s["dx_sb"], ET * max(1, u // UPC))
                    pool.tensor_tensor(m.bx[:, u % 2, :, :], m.bb[:, g % 2, :, :],
                                       m.dx[:, u // UPC % 2, e, None, :].to_broadcast([P, NGR, S]), ALU.mult).then_inc(s["bx_sb"], 1)

                if not scan:
                    g_dx(pool, 0)
                    for u in range(AHEAD):
                        state_input(u)
                    return
                for u in range(AHEAD, UNITS + AHEAD):
                    state_input(u)
                    if u == UPC - 1:
                        g_dx(pool, 0)
                    if u == UNITS - 1:
                        g_dx(pool, 1)

            @block.tensor
            def _(pe):
                def spread(bank, g, row):
                    return pe.matmul(ps[:, bank, :], k.sel3[:, row, None].to_broadcast([6 * NS, P]), m.parts[:, g // NG4 % 2, :],
                                     start=True, stop=True)

                def spread_b(r):
                    if r in (0, ROWS // 2, ROWS):
                        pe.wait_ge(s["parts"], 2 * max(1, r // (ROWS // 2)))
                    if r > ROW0:
                        pe.wait_ge(s["b_sb"], r - ROW0)
                    spread(STAGE_B, r // NGR, r % (NG4 * NGR)).then_inc(s["b_ps"], 1)

                def spread_c(g):
                    if g > 0:
                        pe.wait_ge(s["hc_sb"], g * ET)
                    for n in range(NGR):
                        mm = spread(n, g, NS + NGR * (g % NG4) + n)
                    mm.then_inc(s["c_ps"], 1)

                if not scan:
                    p_mean(pe, 0)
                    for n in range(2 * ET):
                        p_x(pe, 0, n)
                    p_dbc(pe, 0)
                    for e in range(ET):
                        p_dt(pe, 0, e)
                    for r in range(CARRIED):
                        spread_b(r)
                    spread_c(0)
                    return

                def out_product(c):
                    pe.wait_ge(s["yg_sb"], (c + 1) * ET)
                    pe.wait_ge(s["dt_abs"], (c + 1) * ET)
                    for e in range(ET):
                        mm = pe.matmul(ps[:, PREP, :], mw.wout[:, e, :], m.yg[:, e, :], start=(e == 0), stop=(e == ET - 1))
                    mm.then_inc(s["out_ps"], 1)

                def reduce(u, half):
                    g, e = u // ET % NG4, u % ET
                    if half == 0:
                        pe.wait_ge(s["hc_sb"], u + 1)
                    for n in range(NGR // 2 * half, NGR // 2 * (half + 1)):
                        mm = pe.matmul(ps[:, 4 + e, :], k.ident[:, :], m.hh[:, u % 2, n, :], start=(g == 0 and n == 0),
                                       stop=(g == NG4 - 1 and n == NGR - 1))
                    if half == 1:
                        mm.then_inc(s["y_ps"], 1)

                for u in range(UNITS):
                    g, q, r = u // ET, u // Q1, u % Q1
                    if u % 2 and u + 1 < UNITS:
                        spread_c(g + 1)
                    for row in rows_at(2 * u):
                        spread_b(row)
                    if u == UPC:
                        out_product(0)
                    if r == 0:
                        p_mean(pe, q)
                    if r == 1:
                        p_x(pe, q, 0)
                    if r == 2:
                        p_x(pe, q, 2)
                    if r == 5:
                        p_dt(pe, q, 1)
                    reduce(u, 0)
                    if r in (3, 4, 6):
                        reduce(u, 1)
                    for row in rows_at(2 * u + 1):
                        spread_b(row)
                    if r == 1:
                        p_x(pe, q, 1)
                    if r == 2:
                        p_x(pe, q, 3)
                    if r == 3:
                        p_dbc(pe, q)
                    if r == 4:
                        p_dt(pe, q, 0)
                    if r not in (3, 4, 6):
                        reduce(u, 1)
                spread_c(GROUP * NG4)
                for row in range(*LAST_ROWS):
                    spread_b(row)
                out_product(1)

            @block.scalar
            def _(act):
                def copy_b(r):
                    g, n = r // NGR, r % NGR
                    act.wait_ge(s["b_ps"], r - ROW0 + 1)
                    if n == 0 and g >= 2:
                        act.wait_ge(s["bx_sb"], (g - 1) * ET - AHEAD)
                    act.activation(m.bb[:, g % 2, n, :], ps[:, STAGE_B, :], ACT.Copy).then_inc(s["b_sb"], 1)

                def decay(u):
                    g, e = u // ET % NG4, u % ET
                    if u in (0, UPC, UNITS):
                        act.wait_ge(s["delta_sb"], ET * max(1, u // UPC))
                    if u > 2:
                        act.wait_ge(s["h_sb"], u - 2)
                    for n in range(NGR):
                        ins = act.activation(m.da[:, u % 2, n, 1:S], m.dl[:, u // UPC % 2, e, 1:S], ACT.Exp,
                                             scale=mw.a[:, e, NGR * g + n:NGR * g + n + 1])
                    ins.then_inc(s["da_sb"], 1)

                if not scan:
                    act.preload_act_table_set(EXPLN)
                    a_square(act, 0)
                    a_rstd(act, 0)
                    for e in range(ET):
                        a_xs(act, 0, e)
                    for e in range(ET):
                        a_z(act, 0, e)
                    a_silu(act, 0)
                    a_dbc(act, 0)
                    for e in range(ET):
                        a_dt(act, 0, e)
                    a_soft(act, 0)
                    for r in range(CARRIED):
                        copy_b(r)
                    for u in range(AHEAD):
                        decay(u)
                    return

                SOON = (0, 4, 6, 7, 8)
                decay(1)
                for u in range(UNITS):
                    q, r = u // Q1, u % Q1
                    if r == 0:
                        a_square(act, q)
                    for row in rows_at(2 * u - 1) if u else ():
                        copy_b(row)
                    for row in rows_at(2 * u) if r in SOON else ():
                        copy_b(row)
                    if r == 0:
                        a_rstd(act, q)
                    if r == 1:
                        a_xs(act, q, 0)
                    if r == 2:
                        a_xs(act, q, 1)
                    if r == 4:
                        a_dbc(act, q)
                    if r == 5:
                        a_dt(act, q, 0)
                    if u + 2 < UNITS:
                        decay(u + 2)
                    elif u + 2 > UNITS:
                        decay(UNITS)
                    for row in rows_at(2 * u) if r not in SOON else ():
                        copy_b(row)
                    if r == 2:
                        a_z(act, q, 0)
                    if r == 3:
                        a_z(act, q, 1)
                        a_silu(act, q)
                    if r == 5:
                        a_dt(act, q, 1)
                        a_soft(act, q)
                for row in rows_at(2 * UNITS - 1):
                    copy_b(row)
                for row in range(*LAST_ROWS):
                    copy_b(row)

            @block.vector
            def _(dve):
                def run_states(u):
                    if u >= AHEAD or not scan:
                        n = max(1, u + 1 - AHEAD)
                        dve.wait_ge(s["da_sb"], n)
                        dve.wait_ge(s["bx_sb"], n)
                    if u >= 2:
                        dve.wait_ge(s["y_ps"], u - 1)
                    dve.tensor_tensor_scan(flat(m.hh[:, u % 2, :, :]), flat(m.da[:, u % 2, :, :]), flat(m.bx[:, u % 2, :, :]), 0.0,
                                           ALU.mult, ALU.add).then_inc(s["h_sb"], 1)

                if not scan:
                    v_u(dve, 0)
                    for e in range(ET):
                        v_taps(dve, 0, e)
                    v_parts(dve, 0)
                    for e in range(ET):
                        v_delta(dve, 0, e)
                    run_states(0)
                    return

                def gate(c):
                    for e in range(ET):
                        i = c * ET + e
                        dve.wait_ge(s["y_ps"], (c + 1) * UPC)
                        dve.scalar_tensor_tensor(m.yg[:, e, :], m.xc[:, c, e, :], mw.cols[:, 1, e:e + 1], ps[:, 4 + e, :],
                                                 ALU.mult, ALU.add).then_inc(s["y_skip"], 1)
                        dve.wait_ge(s["y_skip"], i + 1)
                        dve.tensor_tensor(m.yg[:, e, :], m.yg[:, e, :], m.zg[:, c, e, :], ALU.mult).then_inc(s["yg_sb"], 1)

                def finish(c):
                    dve.wait_ge(s["out_ps"], c + 1)
                    dve.scalar_tensor_tensor(y[:, c, :], y[:, c, :], 2.0, ps[:, PREP, :], ALU.mult, ALU.add).then_inc(s["y_new"], 1)

                for u in range(UNITS):
                    g, q, r = u // ET, u // Q1, u % Q1
                    if u > 0:
                        dve.wait_ge(s["h_sb"], u)
                    if g > 0:
                        dve.wait_ge(s["c_ps"], g)
                    dve.tensor_tensor(m.hh[:, u % 2, :, :], m.hh[:, u % 2, :, :], ps[:, 0:NGR, :], ALU.mult).then_inc(s["hc_sb"], 1)
                    if u == UPC:
                        gate(0)
                    if r == 2:
                        v_taps(dve, q, 1)
                    if u + 1 < UNITS:
                        run_states(u + 1)
                    if r == 0:
                        v_u(dve, q)
                    if r == 1:
                        v_taps(dve, q, 0)
                    if r == 4:
                        v_parts(dve, q)
                    if r == 5:
                        for e in range(ET):
                            v_delta(dve, q, e)
                    if u == UPC:
                        finish(0)
                gate(1)
                run_states(UNITS)
                finish(1)


def mamba_tiles(nc, ctx):
    m = Bag()
    sb = lambda n, sh, dt=F32: ctx.enter_context(nc.sbuf_tensor(n, sh, dt))
    m.xs = sb("m_xs", [P, ET, TAPS - 1 + S])
    m.cv, m.rl, m.yg = [sb(n, [P, ET, S]) for n in ("m_cv", "m_rl", "m_yg")]
    m.xc, m.zg, m.dl, m.dx = [sb(n, [P, GROUP, ET, S]) for n in ("m_xc", "m_zg", "m_dl", "m_dx")]
    m.dts, m.rest, m.mid = sb("m_dts", [RANK, S]), sb("m_rest", [2 * NS, S]), sb("m_mid", [2 * NS, S], BF16)
    m.parts = sb("m_parts", [6 * NS, GROUP, S], BF16)
    m.bb, m.da, m.bx, m.hh = [sb(n, [P, 2, NGR, S]) for n in ("m_bb", "m_da", "m_bx", "m_h")]
    with Stage(nc, "zero_col") as s:
        with nc.Block() as block:
            @block.gpsimd
            def _(pool):
                pool.memset(m.xs[:, :, 0:TAPS - 1], 0.0).then_inc(s["zero_col"], 1)
                pool.memset(m.da[:, :, :, 0:1], 0.0).then_inc(s["zero_col"], 1)
                pool.wait_ge(s["zero_col"], 2)
    return m


def stage_lowrank(nc, k, w, mw, later):
    with ExitStack() as mem, Stage(nc, LN_SEMS + "wts affine x_mid m1_ps m1_sb m2_ps m2_sb lo_ps lo_sb out_ps x_new") as s:
        sb = lambda n, sh: mem.enter_context(nc.sbuf_tensor(n, sh, F32))
        wt, b = sb("r_w", [P, P]), sb("r_b", [P, 1])
        ld, lu = sb("r_ld", [100, 4]), sb("r_lu", [4, 50])
        da, ua = sb("r_da", [100, P]), sb("r_ua", [50, P])
        m1, m2, lo = sb("r_m1", [4, P]), sb("r_m2", [50, P]), sb("r_lo", [P, P])
        ps = k.ps
        with nc.Block() as block:
            @block.sync
            def _(sp):
                for dst, src in ((wt, w["L2_ffn_W"]), (b, w["L2_ffn_b"]), (ld, w["L2_ffn_lora_down"]), (lu, w["L2_ffn_lora_up"]),
                                 (da, w["L2_ffn_down_aux"]), (ua, w["L2_ffn_up_aux"])):
                    sp.dma_start(dst[:, :], src).then_inc(s["wts"], 16)
                load_ahead(sp, later)

            @block.tensor
            def _(pe):
                ln_tensor(pe, k, s, k.y)
                pe.wait_ge(s["wts"], 96)
                pe.matmul(ps[0:4, 0, 0:P], ld[:, :], da[:, :], start=True, stop=True).then_inc(s["m1_ps"], 1)
                pe.wait_ge(s["m1_sb"], 1)
                pe.matmul(ps[0:50, 1, 0:P], lu[:, :], m1[:, :], start=True, stop=True).then_inc(s["m2_ps"], 1)
                pe.wait_ge(s["m2_sb"], 1)
                pe.matmul(ps[:, 2, 0:P], m2[:, :], ua[:, :], start=True, stop=True).then_inc(s["lo_ps"], 1)
                for c in range(GROUP):
                    pe.wait_ge(s["x_mid"], c + 1)
                    pe.matmul(ps[:, 6 + c, :], k.mean_mat[:, :], k.x[:, c, :], start=True, stop=True).then_inc(s["ln_mean"], 1)
                for c in range(GROUP):
                    pe.wait_ge(s["ln_sq"], GROUP + c + 1)
                    pe.matmul(ps[:, 6 + c, :], k.mean_mat[:, :], k.sq[:, c, :], start=True, stop=True).then_inc(s["ln_var"], 1)
                pe.wait_ge(s["lo_sb"], 1)
                for c in range(GROUP):
                    pe.wait_ge(s["xn_ready"], GROUP + c + 1)
                    pe.matmul(ps[:, 3 + c, :], wt[:, :], k.xn[:, c, :], start=True, stop=False)
                    pe.matmul(ps[:, 3 + c, :], lo[:, :], k.xn[:, c, :], start=False, stop=True).then_inc(s["out_ps"], 1)

            @block.scalar
            def _(act):
                act.preload_act_table_set(EXPLN)
                ln_scalar(act, k, s)
                act.wait_ge(s["m1_ps"], 1)
                act.activation(m1[:, :], ps[0:4, 0, 0:P], ACT.Copy).then_inc(s["m1_sb"], 1)
                act.wait_ge(s["m2_ps"], 1)
                act.activation(m2[:, :], ps[0:50, 1, 0:P], ACT.Copy).then_inc(s["m2_sb"], 1)
                act.wait_ge(s["lo_ps"], 1)
                act.activation(lo[:, :], ps[:, 2, 0:P], ACT.Copy).then_inc(s["lo_sb"], 1)
                for c in range(GROUP):
                    act.wait_ge(s["ln_xc"], GROUP + c + 1)
                    act.activation(k.sq[:, c, :], k.xc[:, c, :], ACT.Square).then_inc(s["ln_sq"], 1)
                for c in range(GROUP):
                    act.wait_ge(s["ln_var"], GROUP + c + 1)
                    act.activation(k.sq[:, c, :], ps[:, 6 + c, :], ACT.Ln, bias=k.eps[:, 0:1]).then_inc(s["ln_log"], 1)
                    act.wait_ge(s["ln_log"], GROUP + c + 1)
                    act.activation(k.sq[:, c, :], k.sq[:, c, :], ACT.Exp, scale=-0.5).then_inc(s["ln_rstd"], 1)

            @block.vector
            def _(dve):
                ln_vector(dve, k, s, k.y, k.y)
                for c in range(GROUP):
                    dve.wait_ge(s["xn_ready"], c + 1)
                    dve.tensor_scalar(k.y[:, c, :], k.y[:, c, :], mw.vec[:, 1:2], mw.vec[:, 2:3], ALU.mult, ALU.add).then_inc(s["affine"], 1)
                    dve.wait_ge(s["affine"], c + 1)
                    dve.tensor_tensor(k.x[:, c, :], k.x[:, c, :], k.y[:, c, :], ALU.add).then_inc(s["x_mid"], 1)
                for c in range(GROUP):
                    dve.wait_ge(s["ln_mean"], GROUP + c + 1)
                    dve.tensor_tensor(k.xc[:, c, :], k.x[:, c, :], ps[:, 6 + c, :], ALU.subtract).then_inc(s["ln_xc"], 1)
                for c in range(GROUP):
                    dve.wait_ge(s["ln_rstd"], GROUP + c + 1)
                    dve.tensor_tensor(k.xn[:, c, :], k.xc[:, c, :], k.sq[:, c, :], ALU.mult).then_inc(s["xn_ready"], 1)
                dve.wait_ge(s["wts"], 96)
                for c in range(GROUP):
                    dve.wait_ge(s["out_ps"], c + 1)
                    dve.scalar_tensor_tensor(k.x[:, c, :], ps[:, 3 + c, :], b[:, 0:1], k.x[:, c, :], ALU.add, ALU.add).then_inc(s["x_new"], 1)


def stage_delta(nc, k, w):
    H, D = 16, 8
    with ExitStack() as mem, Stage(nc, LN_SEMS + "wts block0 block_rdy fold_ps fold_sb proj_ps beta_sb vs_sb qs_sb kv_sb g_sb o_sb out_ps r_sb "
                                   "affine x_new") as s:
        sb = lambda n, sh: mem.enter_context(nc.sbuf_tensor(n, sh, F32))
        wk, wo, wqt, wvt = [sb(n, [P, P]) for n in ("d_wk", "d_wo", "d_wqt", "d_wvt")]
        wb, cols = sb("d_wb", [P, H]), sb("d_cols", [P, 4])
        blk = sb("d_blk", [P, H, D])
        wqs, wvs = sb("d_wqs", [P, P]), sb("d_wvs", [P, P])
        wbr = sb("d_wbr", [P, H, D])
        beta, vs, qs, kv, g, o, r = [sb(n, [P, GROUP, S]) for n in ("d_beta", "d_vs", "d_qs", "d_kv", "d_g", "d_o", "d_r")]
        ps = k.ps
        with nc.Block() as block:
            @block.sync
            def _(sp):
                for dst, src in ((wk, w["L3_attn_Wk"]), (wo, w["L3_attn_Wo"]), (wqt, w["L3_attn_Wq"]), (wvt, w["L3_attn_Wv"]),
                                 (wb, w["L3_attn_Wbeta"]), (cols, w["L3_cols"])):
                    sp.dma_start(dst[:, :], src).then_inc(s["wts"], 16)

            @block.gpsimd
            def _(pool):
                pool.memset(blk[:, :, :], 1.0).then_inc(s["block0"], 1)
                pool.wait_ge(s["block0"], 1)
                pool.affine_select(out=blk[:, :, :], in_=blk[:, :, :], compare_op=ALU.is_ge, fill=0.0, base=0,
                                   pattern=[[-D, H], [0, D]], channel_multiplier=1).then_inc(s["block0"], 1)
                pool.wait_ge(s["block0"], 2)
                pool.affine_select(out=blk[:, :, :], in_=blk[:, :, :], compare_op=ALU.is_ge, fill=0.0, base=D - 1,
                                   pattern=[[D, H], [0, D]], channel_multiplier=-1).then_inc(s["block0"], 1)
                pool.wait_ge(s["wts"], 96)
                pool.tensor_copy(wbr[:, :, :], wb[:, :, None].to_broadcast([P, H, D])).then_inc(s["block_rdy"], 1)

            @block.tensor
            def _(pe):
                ln_tensor(pe, k, s, k.x)
                pe.wait_ge(s["wts"], 96)
                pe.wait_ge(s["block0"], 3)
                pe.wait_ge(s["block_rdy"], 1)
                pe.matmul(ps[:, 4, 0:P], wvt[:, :], flat(blk[:, :, :]), start=True, stop=True).then_inc(s["fold_ps"], 1)
                pe.matmul(ps[:, 5, 0:P], wqt[:, :], flat(blk[:, :, :]), start=True, stop=True).then_inc(s["fold_ps"], 1)
                pe.wait_ge(s["fold_sb"], 2)
                for c in range(GROUP):
                    pe.wait_ge(s["xn_ready"], c + 1)
                    if c > 0:
                        pe.wait_ge(s["kv_sb"], c)
                        pe.wait_ge(s["beta_sb"], c)
                        pe.wait_ge(s["qs_sb"], c)
                    for n, wt in enumerate((flat(wbr[:, :, :]), wvs[:, :], wqs[:, :], wk[:, :])):
                        pe.matmul(ps[:, n, :], wt, k.xn[:, c, :], start=True, stop=True).then_inc(s["proj_ps"], 1)
                for c in range(GROUP):
                    pe.wait_ge(s["o_sb"], c + 1)
                    pe.matmul(ps[:, 4 + c, :], wo[:, :], o[:, c, :], start=True, stop=True).then_inc(s["out_ps"], 1)
                for c in range(GROUP):
                    pe.wait_ge(s["r_sb"], c + 1)
                    pe.matmul(ps[:, 6 + c, :], k.mean_mat[:, :], r[:, c, :], start=True, stop=True).then_inc(s["ln_mean"], 1)
                for c in range(GROUP):
                    pe.wait_ge(s["ln_sq"], GROUP + c + 1)
                    pe.matmul(ps[:, 6 + c, :], k.mean_mat[:, :], k.sq[:, c, :], start=True, stop=True).then_inc(s["ln_var"], 1)

            @block.scalar
            def _(act):
                act.preload_act_table_set(EXPLN)
                ln_scalar(act, k, s)
                for n, dst in enumerate((wvs, wqs)):
                    act.wait_ge(s["fold_ps"], n + 1)
                    act.activation(dst[:, :], ps[:, 4 + n, 0:P], ACT.Copy).then_inc(s["fold_sb"], 1)
                act.wait_ge(s["wts"], 96)
                for c in range(GROUP):
                    act.wait_ge(s["proj_ps"], 4 * c + 1)
                    act.activation(beta[:, c, :], ps[:, 0, :], ACT.Sigmoid, bias=cols[:, 0:1]).then_inc(s["beta_sb"], 1)
                    act.wait_ge(s["proj_ps"], 4 * c + 2)
                    act.activation(vs[:, c, :], ps[:, 1, :], ACT.Copy).then_inc(s["vs_sb"], 1)
                    act.wait_ge(s["proj_ps"], 4 * c + 3)
                    act.activation(qs[:, c, :], ps[:, 2, :], ACT.Copy).then_inc(s["qs_sb"], 1)
                for c in range(GROUP):
                    act.wait_ge(s["ln_xc"], GROUP + c + 1)
                    act.activation(k.sq[:, c, :], k.xc[:, c, :], ACT.Square).then_inc(s["ln_sq"], 1)
                for c in range(GROUP):
                    act.wait_ge(s["ln_var"], GROUP + c + 1)
                    act.activation(k.sq[:, c, :], ps[:, 6 + c, :], ACT.Ln, bias=k.eps[:, 0:1]).then_inc(s["ln_log"], 1)
                    act.wait_ge(s["ln_log"], GROUP + c + 1)
                    act.activation(k.sq[:, c, :], k.sq[:, c, :], ACT.Exp, scale=-0.5).then_inc(s["ln_rstd"], 1)

            @block.vector
            def _(dve):
                ln_vector(dve, k, s, k.x, k.xn)
                for c in range(GROUP):
                    dve.wait_ge(s["vs_sb"], c + 1)
                    dve.wait_ge(s["proj_ps"], 4 * c + 4)
                    dve.tensor_tensor(kv[:, c, :], vs[:, c, :], ps[:, 3, :], ALU.mult).then_inc(s["kv_sb"], 1)
                    dve.wait_ge(s["kv_sb"], c + 1)
                    dve.wait_ge(s["beta_sb"], c + 1)
                    dve.tensor_tensor_scan(g[:, c, :], beta[:, c, :], kv[:, c, :], 0.0, ALU.mult, ALU.add).then_inc(s["g_sb"], 1)
                    dve.wait_ge(s["g_sb"], c + 1)
                    dve.wait_ge(s["qs_sb"], c + 1)
                    dve.tensor_tensor(o[:, c, :], g[:, c, :], qs[:, c, :], ALU.mult).then_inc(s["o_sb"], 1)
                for c in range(GROUP):
                    dve.wait_ge(s["out_ps"], c + 1)
                    dve.scalar_tensor_tensor(r[:, c, :], ps[:, 4 + c, :], cols[:, 1:2], k.xn[:, c, :], ALU.add, ALU.add).then_inc(s["r_sb"], 1)
                for c in range(GROUP):
                    dve.wait_ge(s["ln_mean"], GROUP + c + 1)
                    dve.tensor_tensor(k.xc[:, c, :], r[:, c, :], ps[:, 6 + c, :], ALU.subtract).then_inc(s["ln_xc"], 1)
                for c in range(GROUP):
                    dve.wait_ge(s["ln_rstd"], GROUP + c + 1)
                    dve.tensor_tensor(r[:, c, :], k.xc[:, c, :], k.sq[:, c, :], ALU.mult).then_inc(s["affine"], 1)
                    dve.wait_ge(s["affine"], 2 * c + 1)
                    dve.tensor_scalar(r[:, c, :], r[:, c, :], cols[:, 2:3], cols[:, 3:4], ALU.mult, ALU.add).then_inc(s["affine"], 1)
                    dve.wait_ge(s["affine"], 2 * c + 2)
                    dve.tensor_tensor(k.x[:, c, :], k.x[:, c, :], r[:, c, :], ALU.add).then_inc(s["x_new"], 1)


def stage_store(nc, k, g, out_dram):
    with Stage(nc, "turned tok_sb stored") as s:
        with nc.Block() as block:
            @block.tensor
            def _(pe):
                for c in range(GROUP):
                    for t in range(NT):
                        mm = pe.transpose(k.ps[:, c, P * t:P * (t + 1)], k.x[:, c, P * t:P * (t + 1)], k.ident[:, :])
                    mm.then_inc(s["turned"], 1)

            @block.vector
            def _(dve):
                for c in range(GROUP):
                    dve.wait_ge(s["turned"], c + 1)
                    dve.tensor_copy(flat(k.tok[:, c, :, :]), k.ps[:, c, :]).then_inc(s["tok_sb"], 1)

            @block.sync
            def _(sp):
                sp.wait_ge(s["tok_sb"], GROUP)
                sp.dma_start(out_dram[bass.ds(g * GROUP, GROUP), :, :].rearrange("b (t p) d -> p b t d", p=P),
                             k.tok[:, :, :, :]).then_inc(s["stored"], 16)
                sp.wait_ge(s["stored"], 16)


def build(nc, d):
    w = d
    with ExitStack() as ctx:
        sb = lambda n, sh: ctx.enter_context(nc.sbuf_tensor(n, sh, F32))
        k = Bag()
        k.ps = ctx.enter_context(nc.psum_tensor("ps", [P, 8, S], F32))
        k.ident, k.mean_mat = sb("ident", [P, P]), sb("mean_mat", [P, P])
        k.eps, k.eps_z = sb("eps", [P, 1]), sb("eps_z", [P, 1])
        k.sel3 = ctx.enter_context(nc.sbuf_tensor("sel3", [6 * NS, 2 * NS], BF16))
        k.head_sel3 = ctx.enter_context(nc.sbuf_tensor("head_sel3", [64 + 16, 8, P], BF16))
        k.lower = sb("lower", [P, EXPERTS, EXPERTS])
        k.head_sel, k.head_sel_t = sb("head_sel", [P, 8, 16]), sb("head_sel_t", [16, 8, P])
        k.x, k.y, k.xn, k.xc, k.sq = [sb(n, [P, GROUP, S]) for n in ("x", "y", "xn", "xc", "sq")]
        k.tok = k.sq[:, :, :].rearrange("p b (t d) -> p b t d", d=P)
        mw = Bag()
        mw.win = sb("mw_in", [P, 2 * ED])
        mw.taps = sb("mw_taps", [P, ET, TAPS])
        mw.cols = sb("mw_cols", [P, 3, ET])
        mw.wx = sb("mw_x", [P, ET, RANK + 2 * NS])
        mw.wdt = sb("mw_dt", [RANK, ED])
        mw.a = sb("mw_a", [P, ET, NS])
        mw.wout = sb("mw_out", [P, ET, P])
        mw.vec = sb("mw_vec", [P, 3])

        with Stage(nc, "fills sel3_zero sel wts a_exp") as s:
            with nc.Block() as block:
                @block.sync
                def _(sp):
                    for dst, src in ((mw.win[:, :], w["L2_attn_W_in"]), (mw.taps[:, :, :], w["L2_attn_conv_w"].rearrange("(e p) t -> p e t", p=P)),
                                     (mw.cols[:, :, :], w["L2_cols"]), (mw.wx[:, :, :], w["L2_attn_W_x"].rearrange("(e p) n -> p e n", p=P)),
                                     (mw.wdt[:, :], w["L2_attn_W_dt"]), (mw.a[:, :, :], w["L2_attn_A_log"].rearrange("(e p) n -> p e n", p=P)),
                                     (mw.wout[:, :, :], w["L2_attn_W_out"].rearrange("(e p) n -> p e n", p=P)), (mw.vec[:, :], w["L2_vec"]),
                                     (k.head_sel[:, :, :], w["head_sel"]), (k.head_sel_t[:, :, :], w["head_sel_t"])):
                        sp.dma_start(dst, src).then_inc(s["wts"], 16)
                    sp.wait_ge(s["wts"], 160)

                @block.gpsimd
                def _(pool):
                    pool.memset(k.ident[:, :], 0.0).then_inc(s["fills"], 1)
                    pool.memset(k.mean_mat[:, :], 1.0 / P).then_inc(s["fills"], 1)
                    pool.memset(k.eps[:, :], EPS).then_inc(s["fills"], 1)
                    pool.memset(k.eps_z[:, :], 2e-12).then_inc(s["fills"], 1)
                    pool.memset(k.lower[:, :, :], 1.0).then_inc(s["fills"], 1)
                    pool.memset(k.sel3[:, :], 0.0).then_inc(s["fills"], 1)
                    pool.memset(k.head_sel3[:, :, :], 0.0).then_inc(s["sel3_zero"], 1)
                    pool.wait_ge(s["fills"], 6)
                    pool.wait_ge(s["sel3_zero"], 1)
                    for part in range(3):
                        pool.affine_select(out=k.sel3[:, :], in_=k.sel3[:, :], compare_op=ALU.not_equal, fill=1.0,
                                           base=-2 * NS * part, pattern=[[-1, 2 * NS]], channel_multiplier=1).then_inc(s["sel"], 1)
                        pool.wait_ge(s["sel"], part + 1)
                    pool.affine_select(out=k.ident[:, :], in_=k.ident[:, :], compare_op=ALU.not_equal, fill=1.0, base=0,
                                       pattern=[[-1, P]], channel_multiplier=1).then_inc(s["sel"], 1)
                    pool.affine_select(out=k.lower[:, :, :], in_=k.lower[:, :, :], compare_op=ALU.is_gt, fill=0.0, base=0,
                                       pattern=[[1, EXPERTS], [-1, EXPERTS]], channel_multiplier=0).then_inc(s["sel"], 1)
                    pool.wait_ge(s["sel"], 5)

                @block.scalar
                def _(act):
                    act.wait_ge(s["wts"], 160)
                    act.activation(mw.a[:, :, :], mw.a[:, :, :], ACT.Exp).then_inc(s["a_exp"], 1)

                @block.vector
                def _(dve):
                    dve.wait_ge(s["a_exp"], 1)
                    dve.tensor_scalar(mw.a[:, :, :], mw.a[:, :, :], -1.0, None, ALU.mult).then_inc(s["a_exp"], 1)
                    dve.wait_ge(s["sel3_zero"], 1)
                    dve.wait_ge(s["wts"], 160)
                    for row in (0, 32, 64):
                        dve.tensor_copy(k.head_sel3[row:row + 16, :, :], k.head_sel_t[:, :, :]).then_inc(s["a_exp"], 1)
                    dve.wait_ge(s["a_exp"], 5)

        with nc.Fori(0, BATCH // GROUP) as g:
            stage_load(nc, k, g, w["x"])
            with ExitStack() as emem, Stage(nc, "w_moe") as ws:
                mo = moe_weights(nc, emem, "e", ws["w_moe"], w["L0_ffn_Wg"], None, w["L0_ffn_W1"], w["L0_ffn_W2"], w["L0_ffn_W3"], 2)
                stage_taylor(nc, k, w, [mo])
                stage_moe(nc, k, "e", mo, 2)
            with ExitStack() as lmem, Stage(nc, "w_local_0 w_local_1") as ws:
                local = [local_weights(nc, lmem, k, w, layer, ws["w_local_%d" % layer]) for layer in range(2)]
                stage_softmax(nc, k, w, local)
                for layer in range(2):
                    stage_local(nc, k, w, local[layer], layer)
            stage_ln_y(nc, k)
            with ExitStack() as mmem:
                m = mamba_tiles(nc, mmem)
                stage_mamba(nc, k, mw, m, scan=False)
                with nc.Fori(0, DEPTH):
                    stage_mamba(nc, k, mw, m, scan=True)
            with ExitStack() as fmem, Stage(nc, "w_moe") as ws:
                mo = moe_weights(nc, fmem, "f", ws["w_moe"], w["L3_ffn_gate_w"], w["L3_ffn_gate_b"], w["L3_wa"], w["L3_wb"], w["L3_ffn_w2"], 4,
                                 w["L3_ba"], w["L3_bb"], w["L3_ffn_b2"])
                stage_lowrank(nc, k, w, mw, [mo])
                stage_delta(nc, k, w)
                stage_moe(nc, k, "f", mo, 4)
            stage_store(nc, k, g, w["out"])


def rotary_tables():
    f = np.float32
    half = np.arange(0, LD, 2, dtype=f)
    inv = (f(1.0) / np.power(f(10000.0), half / f(LD))).astype(f)
    t = np.arange(S, dtype=f)
    freqs = (t[:, None] * inv[None, :]).astype(f)
    freqs = np.concatenate([freqs, freqs], -1)
    base = ((half + f(0.4 * LD)) / f(1.4 * LD)).astype(f)
    power = ((t - f(S // 2)) / f(WIN // 2)).astype(f)
    scale = np.power(base[None, :], power[:, None]).astype(f)
    scale = np.concatenate([scale, scale], -1)
    cos, sin = np.cos(freqs), np.sin(freqs)
    sign = np.where(np.arange(LD) < LD // 2, f(-1), f(1))[None, :]
    tabs = [cos * scale, sin * scale * sign, cos / scale, sin / scale * sign]
    return np.ascontiguousarray(np.stack([np.tile(a.T, (2, 1)) for a in tabs], 1).astype(f))


def head_selectors():
    sel = np.zeros((P, 8, 16), np.float32)
    for m in range(8):
        for j in range(2):
            sel[LD * j:LD * (j + 1), m, 2 * m + j] = 1
    return sel, np.ascontiguousarray(sel.transpose(2, 1, 0))


def lay_out(i):
    a = {n: np.ascontiguousarray(v) for n, v in i.items()}
    T = lambda v, *ax: np.ascontiguousarray(v.transpose(*ax))
    o = {"x": a["L0_attn_hidden_states"]}
    for n in ("L0_attn_Wq", "L0_attn_Wk", "L0_attn_Wv", "L0_attn_Wo", "L1_attn_kernel", "L1_attn_WO", "L1_ffn_wqkv", "L1_ffn_wo",
              "L1_ffn_w1", "L1_ffn_b1", "L1_ffn_w2", "L2_attn_W_in", "L2_attn_conv_w", "L2_attn_W_x", "L2_attn_W_dt",
              "L2_attn_A_log", "L2_attn_W_out", "L2_ffn_down_aux", "L3_attn_Wk", "L3_attn_Wo", "L3_attn_Wbeta", "L3_ffn_gate_w",
              "L3_ffn_gate_b", "L3_ffn_w2", "L3_ffn_b2"):
        o[n] = a[n]
    for n in ("L0_ffn_Wg", "L2_ffn_W", "L2_ffn_lora_down", "L2_ffn_lora_up", "L2_ffn_up_aux", "L3_attn_Wq", "L3_attn_Wv"):
        o[n] = T(a[n], 1, 0)
    for n in ("L0_ffn_W1", "L0_ffn_W2", "L0_ffn_W3"):
        o[n] = T(a[n], 0, 2, 1)
    qk = a["L1_ffn_wqkv"][:, :, 0:1024].reshape(2, P, 16, 2, 32)
    o["L1_qk_rot"] = np.ascontiguousarray(qk[:, :, :, ::-1, :]).reshape(2, P, 1024)
    two = lambda v: np.tile(v, (1, 2))
    swap = lambda v: np.concatenate([v[:, 32:], v[:, :32]], 1)
    qs, ks = a["L1_ffn_q_scale"], a["L1_ffn_k_scale"]
    o["L1_scales"] = np.ascontiguousarray(np.stack([two(qs), two(swap(qs)), two(ks), two(swap(ks))], -1))
    o["L1_ln"] = np.ascontiguousarray(np.stack([a["L1_ffn_ln_g"], a["L1_ffn_ln_b"], a["L1_ffn_b2"]], -1))
    o["rot_tables"] = rotary_tables()
    o["head_sel"], o["head_sel_t"] = head_selectors()
    ecol = lambda n: a[n].reshape(ET, P).T
    o["L2_cols"] = np.ascontiguousarray(np.stack([ecol("L2_attn_conv_b"), ecol("L2_attn_Dp"), ecol("L2_attn_b_dt")], 1))
    o["L2_vec"] = np.ascontiguousarray(np.stack([a["L2_attn_rms_w"], a["L2_attn_ln_w"], a["L2_attn_ln_b"]], -1))
    o["L2_ffn_b"] = a["L2_ffn_b"][:, None]
    o["L3_cols"] = np.ascontiguousarray(np.stack([np.repeat(a["L3_attn_b_beta"], 8), a["L3_attn_b_o"], a["L3_attn_ln_g"],
                                                  a["L3_attn_ln_b"]], -1))
    w1, b1 = a["L3_ffn_w1"], a["L3_ffn_b1"].reshape(EXPERTS, 2, MOE_F // P, P)
    o["L3_wa"], o["L3_wb"] = np.ascontiguousarray(w1[:, :, MOE_F:]), np.ascontiguousarray(w1[:, :, :MOE_F])
    o["L3_ba"], o["L3_bb"] = T(b1[:, 1], 2, 0, 1), T(b1[:, 0], 2, 0, 1)
    return o


def kernel(**inputs):
    import numpy as _np
    import concourse.bacc as _bacc
    from concourse import mybir as _mybir
    from concourse.bass_utils import run_bass_kernel_spmd as _run

    nc = _bacc.Bacc("TRN2", target_bir_lowering=False, num_devices=1)
    arrays, d = {}, {}
    for name, a in lay_out({n: _np.asarray(v) for n, v in inputs.items()}).items():
        a = _np.ascontiguousarray(a)
        arrays[f"in_{name}"] = a
        d[name] = nc.dram_tensor(f"in_{name}", a.shape, _mybir.dt.from_np(a.dtype), kind="ExternalInput").ap()
    d["out"] = nc.dram_tensor("out_0", (BATCH, S, P), F32, kind="ExternalOutput").ap()
    build(nc, d)
    r = _run(nc, [arrays], core_ids=[0])
    return r.results[0]["out_0"]
```
